# Optimizing a Trainium2 kernel written in Bass

```python
import numpy as np
import jax
import jax.numpy as jnp

def _softmax(x, axis=-1):
    return jax.nn.softmax(x, axis=axis)

def _gelu(x):
    return jax.nn.gelu(x, approximate=True)

def _silu(x):
    return jax.nn.silu(x)

def _sigmoid(x):
    return jax.nn.sigmoid(x)

def _layernorm(x, axis=-1, eps=1e-05):
    m = jnp.mean(x, axis=axis, keepdims=True)
    v = jnp.var(x, axis=axis, keepdims=True)
    return (x - m) / jnp.sqrt(v + eps)

def _scatter_add(tgt, idx, src, axis=0):
    return tgt.at[idx].add(src)

def _segment_sum(src, seg, n):
    return jax.ops.segment_sum(src, seg, n)
kernel_name = 'mk_hybrid_d1_jaxref_r4_baa669'

def setup_inputs(seed: int=0):
    np.random.seed(seed)
    _w = jnp.asarray

    def _L0_attn_a_setup():
        import jax, jax.numpy as jnp
        import numpy as np
        import math
        D_MODEL = 256
        NUM_HEADS = 16
        HEAD_DIM = D_MODEL // NUM_HEADS
        B, S = (2, 512)

        def _causal_attn(q, k, v):
            scale = 1.0 / math.sqrt(q.shape[-1])
            scores = jnp.einsum('bthd,bshd->bhts', q, k) * scale
            t = q.shape[1]
            mask = jnp.tril(jnp.ones((t, t), dtype=bool))
            scores = jnp.where(mask, scores, -jnp.inf)
            attn = jax.nn.softmax(scores, axis=-1)
            return jnp.einsum('bhts,bshd->bthd', attn, v)
        key = jax.random.key(seed)
        ks = jax.random.split(key, 7)
        sc = 0.02
        return {'x': jax.random.normal(ks[0], (B, S, D_MODEL), dtype=jnp.float32), 'Wqkv_w': jax.random.normal(ks[1], (3 * D_MODEL, D_MODEL), dtype=jnp.float32) * sc, 'Wqkv_b': jnp.zeros((3 * D_MODEL,), dtype=jnp.float32), 'conv_w': jax.random.normal(ks[2], (D_MODEL, D_MODEL, 3), dtype=jnp.float32) * sc, 'conv_b': jnp.zeros((D_MODEL,), dtype=jnp.float32), 'out_w': jax.random.normal(ks[3], (D_MODEL, D_MODEL), dtype=jnp.float32) * sc, 'out_b': jnp.zeros((D_MODEL,), dtype=jnp.float32)}
    _L0_attn_a_in = _L0_attn_a_setup()

    def _L0_attn_b_setup():
        import jax, jax.numpy as jnp
        import numpy as np
        B, S, D = (4, 512, 256)
        GAMMA = 1.0
        key = jax.random.key(seed)
        ks = jax.random.split(key, 9)
        scale = 1.0 / np.sqrt(D)
        return {'x': jax.random.normal(ks[0], (B, S, D), dtype=jnp.float32), 'Wq': jax.random.normal(ks[1], (D, D), dtype=jnp.float32) * scale, 'bq': jax.random.normal(ks[2], (D,), dtype=jnp.float32) * 0.01, 'Wk': jax.random.normal(ks[3], (D, D), dtype=jnp.float32) * scale, 'bk': jax.random.normal(ks[4], (D,), dtype=jnp.float32) * 0.01, 'Wv': jax.random.normal(ks[5], (D, D), dtype=jnp.float32) * scale, 'bv': jax.random.normal(ks[6], (D,), dtype=jnp.float32) * 0.01, 'Wo': jax.random.normal(ks[7], (D, D), dtype=jnp.float32) * scale, 'bo': jax.random.normal(ks[8], (D,), dtype=jnp.float32) * 0.01}
    _L0_attn_b_in = _L0_attn_b_setup()

    def _L0_ffn_setup():
        import jax, jax.numpy as jnp
        import numpy as np
        TOP_K = 2
        key = jax.random.key(seed)
        k1, k2, k3 = jax.random.split(key, 3)
        B, S, D, E = (8, 512, 256, 8)
        x = jax.random.normal(k1, (B, S, D), dtype=jnp.float32)
        gate_w = jax.random.normal(k2, (E, D), dtype=jnp.float32) * (1.0 / np.sqrt(D))
        gate_b = jnp.zeros((E,), dtype=jnp.float32)
        expert_w = jax.random.normal(k3, (E, D, D), dtype=jnp.float32) * (1.0 / np.sqrt(D))
        expert_b = jnp.zeros((E, D), dtype=jnp.float32)
        return {'x': x, 'gate_w': gate_w, 'gate_b': gate_b, 'expert_w': expert_w, 'expert_b': expert_b}
    _L0_ffn_in = _L0_ffn_setup()
    _d = {'L0_attn_a_x': _L0_attn_a_in['x'], 'L0_attn_a_Wqkv_w': _L0_attn_a_in['Wqkv_w'], 'L0_attn_a_Wqkv_b': _L0_attn_a_in['Wqkv_b'], 'L0_attn_a_conv_w': _L0_attn_a_in['conv_w'], 'L0_attn_a_conv_b': _L0_attn_a_in['conv_b'], 'L0_attn_a_out_w': _L0_attn_a_in['out_w'], 'L0_attn_a_out_b': _L0_attn_a_in['out_b'], 'L0_attn_b_Wq': _L0_attn_b_in['Wq'], 'L0_attn_b_bq': _L0_attn_b_in['bq'], 'L0_attn_b_Wk': _L0_attn_b_in['Wk'], 'L0_attn_b_bk': _L0_attn_b_in['bk'], 'L0_attn_b_Wv': _L0_attn_b_in['Wv'], 'L0_attn_b_bv': _L0_attn_b_in['bv'], 'L0_attn_b_Wo': _L0_attn_b_in['Wo'], 'L0_attn_b_bo': _L0_attn_b_in['bo'], 'L0_ffn_gate_w': _L0_ffn_in['gate_w'], 'L0_ffn_gate_b': _L0_ffn_in['gate_b'], 'L0_ffn_expert_w': _L0_ffn_in['expert_w'], 'L0_ffn_expert_b': _L0_ffn_in['expert_b']}
    _x0 = _d['L0_attn_a_x']
    _d['L0_attn_a_x'] = jax.random.normal(jax.random.fold_in(jax.random.key(seed), 1), (8, 512, 256), dtype=_x0.dtype)
    del _x0
    return _d

def reference(L0_attn_a_x, L0_attn_a_Wqkv_w, L0_attn_a_Wqkv_b, L0_attn_a_conv_w, L0_attn_a_conv_b, L0_attn_a_out_w, L0_attn_a_out_b, L0_attn_b_Wq, L0_attn_b_bq, L0_attn_b_Wk, L0_attn_b_bk, L0_attn_b_Wv, L0_attn_b_bv, L0_attn_b_Wo, L0_attn_b_bo, L0_ffn_gate_w, L0_ffn_gate_b, L0_ffn_expert_w, L0_ffn_expert_b):

    def _L0_attn_a_ref(x, Wqkv_w, Wqkv_b, conv_w, conv_b, out_w, out_b):
        import jax, jax.numpy as jnp
        import numpy as np
        import math
        D_MODEL = 256
        NUM_HEADS = 16
        HEAD_DIM = D_MODEL // NUM_HEADS
        B, S = (2, 512)

        def _causal_attn(q, k, v):
            scale = 1.0 / math.sqrt(q.shape[-1])
            scores = jnp.einsum('bthd,bshd->bhts', q, k) * scale
            t = q.shape[1]
            mask = jnp.tril(jnp.ones((t, t), dtype=bool))
            scores = jnp.where(mask, scores, -jnp.inf)
            attn = jax.nn.softmax(scores, axis=-1)
            return jnp.einsum('bhts,bshd->bthd', attn, v)
        b, s, d = x.shape
        qkv = x @ Wqkv_w.T + Wqkv_b
        qkv = qkv.reshape(b, s, 3, NUM_HEADS, HEAD_DIM)
        q, k, v = (qkv[:, :, 0], qkv[:, :, 1], qkv[:, :, 2])
        ctx = _causal_attn(q, k, v)
        ctx_c = ctx.reshape(b, s, d).transpose(0, 2, 1)
        conv_out = jax.lax.conv_general_dilated(ctx_c, conv_w, window_strides=(1,), padding=[(1, 1)], dimension_numbers=('NCH', 'OIH', 'NCH')) + conv_b[None, :, None]
        q2 = conv_out.transpose(0, 2, 1).reshape(b, s, NUM_HEADS, HEAD_DIM)
        ctx2 = _causal_attn(q2, k, v)
        out = ctx2.reshape(b, s, d) @ out_w.T + out_b
        return out

    def _L0_attn_b_ref(x, Wq, bq, Wk, bk, Wv, bv, Wo, bo):
        import jax, jax.numpy as jnp
        import numpy as np
        B, S, D = (4, 512, 256)
        GAMMA = 1.0
        q = x @ Wq + bq
        k = x @ Wk + bk
        v = x @ Wv + bv
        q_sq = jnp.sum(q * q, axis=-1)
        k_sq = jnp.sum(k * k, axis=-1)
        qk = jnp.einsum('bqd,bkd->bqk', q, k)
        dist_sq = q_sq[:, :, None] + k_sq[:, None, :] - 2.0 * qk
        scores = jnp.exp(-GAMMA * dist_sq)
        attn = jax.nn.softmax(scores, axis=-1)
        out = jnp.einsum('bqk,bkd->bqd', attn, v)
        return out @ Wo + bo

    def _L0_ffn_ref(x, gate_w, gate_b, expert_w, expert_b):
        import jax, jax.numpy as jnp
        import numpy as np
        TOP_K = 2
        gate = jnp.einsum('bsd,ed->bse', x, gate_w) + gate_b
        _, idx = jax.lax.top_k(gate, TOP_K)
        E = gate_w.shape[0]
        flat_idx = idx.reshape(-1)
        counts = jnp.zeros((E,), dtype=x.dtype).at[flat_idx].add(1.0)
        expert_out = jax.nn.relu(jnp.einsum('bsd,ehd->bseh', x, expert_w) + expert_b)
        total = flat_idx.size
        out = jnp.einsum('bseh,e->bsh', expert_out, counts) / total
        return out
    x = L0_attn_a_x
    x = x + _L0_attn_a_ref(_layernorm(x, axis=-1), L0_attn_a_Wqkv_w, L0_attn_a_Wqkv_b, L0_attn_a_conv_w, L0_attn_a_conv_b, L0_attn_a_out_w, L0_attn_a_out_b)
    x = x + _L0_ffn_ref(_layernorm(x, axis=-1), L0_ffn_gate_w, L0_ffn_gate_b, L0_ffn_expert_w, L0_ffn_expert_b)
    x = x + _L0_attn_b_ref(_layernorm(x, axis=-1), L0_attn_b_Wq, L0_attn_b_bq, L0_attn_b_Wk, L0_attn_b_bk, L0_attn_b_Wv, L0_attn_b_bv, L0_attn_b_Wo, L0_attn_b_bo)
    x = x + _L0_ffn_ref(_layernorm(x, axis=-1), L0_ffn_gate_w, L0_ffn_gate_b, L0_ffn_expert_w, L0_ffn_expert_b)
    return x

_drawn_inputs = setup_inputs


def setup_inputs(seed=0):
    import zlib

    import numpy as np

    out = dict(_drawn_inputs(seed))
    spreads = {'L0_attn_a_Wqkv_b': (0.0, 0.1),
     'L0_attn_a_conv_b': (0.0, 0.8),
     'L0_attn_a_out_b': (0.0, 0.1),
     'L0_ffn_gate_b': (0.0, 0.1),
     'L0_ffn_expert_b': (0.0, 0.1)}
    factors = {'L0_attn_a_Wqkv_w': 5.165,
     'L0_attn_a_conv_w': 8.0,
     'L0_attn_b_bv': 6.757,
     'L0_attn_b_bo': 7.515}
    for name, (base, spread) in spreads.items():
        noise = np.random.default_rng([zlib.crc32(name.encode()), seed]).standard_normal(out[name].shape)
        drawn = base * np.exp(spread * noise) if base else spread * noise
        out[name] = jnp.asarray(drawn.astype(out[name].dtype))
    for name, factor in factors.items():
        out[name] = (out[name] * factor).astype(out[name].dtype)
    return out
```

```python
from contextlib import ExitStack

import concourse.bass as bass
from concourse import mybir

ALU = mybir.AluOpType
ACT = mybir.ActivationFunctionType
AX = mybir.AxisListType
F32 = mybir.dt.float32
F32R = mybir.dt.float32r
BF16 = mybir.dt.bfloat16

P = 128
B, S, D = 8, 512, 256
KT = D // P
TT = S // P
H, HD = 16, 16
GH = 4
NG = H // GH
GROUPS = B * NG
GR = GH * HD
NE, TOP_K = 8, 2
EPS = 1e-5
SCALE = HD ** -0.5
NEG = -1e30
SPLITS = 3
ROWS = 6 * HD
RUNS = ((0, (0, 3), (0, 3)), (3, (0, 2), (1, 3)), (5, (0, 1), (2, 3)))
PASSES = ((0, 0), (0, 1), (1, 0))


def each_batch(eng, step, head=1):
    for b in range(head):
        step(b, b % 2, b // 2, b == 0, False)
    with eng.Fori(0, (B - 2 * head) // 2) as t:
        for j in range(head, head + 2):
            step(2 * t + j, j % 2, t + j // 2, False, False)
    for b in range(B - head, B):
        step(b, b % 2, b // 2, False, b == B - 1)


def is_first(b):
    return isinstance(b, int) and b == 0


def wait_apart(eng, sem, value):
    eng.wait_ge(sem, value)
    eng.nop(nofuse=True)


class Shared:

    def __init__(self, nc, ctx):
        self.nc, self.used = nc, []
        self.x = ctx.enter_context(nc.sbuf_tensor("x_res", [P, B * TT, D], F32))
        self.ident = ctx.enter_context(nc.sbuf_tensor("ident", [P, P], F32))
        self.ident_bf = ctx.enter_context(nc.sbuf_tensor("ident_bf", [P, P], BF16))
        self.causal_neg = ctx.enter_context(nc.sbuf_tensor("causal_neg", [P, P], BF16))
        self.causal_neg_t = ctx.enter_context(nc.sbuf_tensor("causal_neg_t", [P, P], BF16))
        self.minus_half = ctx.enter_context(nc.sbuf_tensor("minus_half", [P, TT], F32))
        self.psum = [ctx.enter_context(nc.psum_tensor(f"bank{i}", [P, 512], F32)) for i in range(8)]
        self.experts = ctx.enter_context(nc.sbuf_tensor("experts", [P, KT, NE, D], F32))
        self.s_experts = ctx.enter_context(nc.semaphore("experts_in"))
        self.q_parts = nc.dram_tensor("q_parts", [GROUPS, SPLITS, GR, S], BF16, kind="Internal").ap()
        self.k_parts = nc.dram_tensor("k_parts", [GROUPS, SPLITS, GR, S], BF16, kind="Internal").ap()
        self.q2_parts = nc.dram_tensor("q2_parts", [GROUPS, SPLITS, GR, S], BF16, kind="Internal").ap()
        self.v_ones = nc.dram_tensor("v_ones", [GROUPS, P, TT, GH * 32], F32, kind="Internal").ap()

    def semaphore(self, name):
        self.used.append(self.nc.alloc_semaphore(name))
        return self.used[-1]

    def recycle_semaphores(self):
        self.nc.clear_and_free_semaphores(self.used)
        self.nc.all_engine_barrier()
        self.used = []

    def after_attention(self, ctx):
        sb = lambda n, s, d=F32: ctx.enter_context(self.nc.sbuf_tensor(f"{n}_sb", s, d))
        self.xt = sb("xt", [P, 2, KT, B * S], F32R)
        self.gate_w = [sb(f"gate_w{i}", [P, KT, P], F32R) for i in range(2)]
        self.gate_b = sb("gate_b", [NE, 1])
        self.gates = sb("gates", [P, B * TT, NE])

    def xt_part(self, i):
        return lambda b, p, k: self.xt[:, i, k, bass.ds(S * b, S)]


class Turned:

    def __init__(self, nc, ctx, sh, name, banks, hi, lo, pieces, tokens=None):
        self.sb = lambda n, s, d=F32: ctx.enter_context(nc.sbuf_tensor(f"{name}_{n}", s, d))
        self.sem = lambda n: sh.semaphore(f"{name}_{n}")
        self.sh, self.banks, self.hi, self.lo, self.pieces = sh, banks, hi, lo, pieces
        self.tokens = self.sb("tokens", [P, TT, D]) if tokens is None else tokens
        self.s_tokens, self.s_turned = self.sem("tokens"), self.sem("turned")
        self.s_hi, self.s_lo = self.sem("hi"), self.sem("lo")

    def turn(self, pe, b):
        pe.wait_ge(self.s_tokens, self.pieces * (b + 1))
        if not is_first(b):
            pe.wait_ge(self.s_lo, KT * b)
        for k in range(KT):
            for j in range(TT):
                mm = pe.transpose(self.banks[k][:, j * P:(j + 1) * P], self.tokens[:, j, k * P:(k + 1) * P],
                                  self.sh.ident[:, :])
            mm.then_inc(self.s_turned, 1)

    def take_hi(self, act, b, p):
        for k in range(KT):
            act.wait_ge(self.s_turned, KT * b + k + 1)
            act.copy(self.hi(b, p, k), self.banks[k][:, :]).then_inc(self.s_hi, 1)

    def take_lo(self, dve, b, p):
        for k in range(KT):
            dve.wait_ge(self.s_hi, KT * b + k + 1)
            dve.tensor_tensor(self.lo(b, p, k), self.banks[k][:, :], self.hi(b, p, k).bitcast(F32),
                              ALU.subtract).then_inc(self.s_lo, 1)


class LayerNorm(Turned):

    def __init__(self, nc, ctx, sh, name, banks, hi, lo, tokens=None):
        super().__init__(nc, ctx, sh, name, banks, hi, lo, TT, tokens)
        self.stats, self.mv = self.sb("stats", [P, TT, 6]), self.sb("mv", [P, TT, 2])
        self.rstd, self.var_eps = self.sb("rstd", [P, TT]), self.sb("var_eps", [P, TT])
        self.s_stats, self.s_mean = self.sem("stats"), self.sem("mean")
        self.s_var, self.s_rstd = self.sem("var"), self.sem("rstd")

    def moments(self, dve, b, written=None):
        if written is not None:
            wait_apart(dve, *written)
        for j in range(TT):
            dve.bn_stats(self.stats[:, j, :], self.sh.x[:, TT * b + j, :]).then_inc(self.s_stats, 1)
        for j in range(TT):
            wait_apart(dve, self.s_stats, TT * b + j + 1)
            dve.bn_aggr(self.mv[:, j, :], self.stats[:, j, :]).then_inc(self.s_mean, 1)

    def deviation(self, pool, b):
        if not is_first(b):
            pool.wait_ge(self.s_tokens, TT * b)
        wait_apart(pool, self.s_mean, TT * b + TT)
        pool.tensor_scalar(self.var_eps[:, :], self.mv[:, :, 1], EPS, None, ALU.add).then_inc(self.s_var, 1)
        pool.wait_ge(self.s_var, b + 1)
        pool.tensor_tensor(self.rstd[:, :], self.var_eps[:, :], self.sh.minus_half[:, :], ALU.pow).then_inc(self.s_rstd, 1)

    def normalise(self, dve, b):
        dve.wait_ge(self.s_rstd, b + 1)
        if not is_first(b):
            dve.wait_ge(self.s_turned, KT * b)
        for j in range(TT):
            dve.tensor_scalar(self.tokens[:, j, :], self.sh.x[:, TT * b + j, :], self.mv[:, j, 0:1],
                              self.rstd[:, j:j + 1], ALU.subtract, ALU.mult).then_inc(self.s_tokens, 1)


class SplitOut:

    def __init__(self, nc, ctx, sh, name, banks, bias, dest, units):
        sb = lambda n, s, d=F32: ctx.enter_context(nc.sbuf_tensor(f"{name}_{n}", s, d))
        sem = lambda n: sh.semaphore(f"{name}_{n}")
        self.banks, self.bias, self.dest, self.units = banks, bias, dest, units
        self.t, self.rest = [sb(f"t{i}", [P, S]) for i in range(2)], [sb(f"rest{i}", [P, S]) for i in range(2)]
        self.parts = [sb(f"parts{i}", [P, SPLITS, S], BF16) for i in range(units)]
        self.s_made, self.s_t, self.s_p0, self.s_rest = sem("made"), sem("t"), sem("p0"), sem("rest")
        self.s_p1, self.s_p2 = sem("p1"), sem("p2")
        self.s_stored = [sem(f"stored{i}") for i in range(units)]

    def slot(self, u, part):
        return SPLITS - 1 - part if self.dest[u][2] else part

    def bias_and_first(self, act, b, u):
        n = self.units * b + u
        act.wait_ge(self.s_made, n + 1)
        if not (is_first(b) and u < 2):
            act.wait_ge(self.s_rest, n - 1)
        act.activation(self.t[u % 2][:, :], self.banks[u][:, :], ACT.Identity,
                       bias=self.bias[:, u:u + 1]).then_inc(self.s_t, 1)
        act.wait_ge(self.s_t, n + 1)
        if not is_first(b):
            act.wait_ge(self.s_stored[u], 32 * b)
        act.copy(self.parts[u][:, self.slot(u, 0), :], self.t[u % 2][:, :]).then_inc(self.s_p0, 1)

    def second(self, dve, b, u):
        n = self.units * b + u
        dve.wait_ge(self.s_p0, n + 1)
        if not (is_first(b) and u < 2):
            dve.wait_ge(self.s_p2, n - 1)
        dve.tensor_tensor(self.rest[u % 2][:, :], self.t[u % 2][:, :], self.parts[u][:, self.slot(u, 0), :],
                          ALU.subtract).then_inc(self.s_rest, 1)
        dve.wait_ge(self.s_rest, n + 1)
        dve.tensor_copy(self.parts[u][:, self.slot(u, 1), :], self.rest[u % 2][:, :]).then_inc(self.s_p1, 1)

    def third(self, pool, b, u):
        n = self.units * b + u
        pool.wait_ge(self.s_p1, n + 1)
        pool.tensor_tensor(self.parts[u][:, self.slot(u, 2), :], self.rest[u % 2][:, :], self.parts[u][:, self.slot(u, 1), :],
                           ALU.subtract).then_inc(self.s_p2, 1)

    def store(self, sp, b, u):
        dest, m, _ = self.dest[u]
        sp.wait_ge(self.s_p2, self.units * b + u + 1)
        for g in range(P // GR):
            sp.dma_start(dest[NG * b + P // GR * m + g].rearrange("s p t -> p s t"),
                         self.parts[u][GR * g:GR * (g + 1), :, :]).then_inc(self.s_stored[u], 16)

    def all_stored(self, sp):
        for s in self.s_stored:
            sp.wait_ge(s, 32 * B)


def split_weights(act, dve, raw, hi, lo, s_raw, need, s_hi, s_lo, at):
    if act is not None:
        act.wait_ge(s_raw, need)
        act.copy(hi, raw).then_inc(s_hi, 1)
    if dve is not None:
        dve.wait_ge(s_hi, at)
        dve.tensor_tensor(lo, raw, hi.bitcast(F32), ALU.subtract).then_inc(s_lo, 1)


def project_qkv(nc, sh, x, w, b_qk, b_v, experts):
    with ExitStack() as ctx:
        sb = lambda n, s, d=F32: ctx.enter_context(nc.sbuf_tensor(f"qkv_{n}", s, d))
        sem = lambda n: sh.semaphore(f"qkv_{n}")
        raw = sb("raw", [P, KT, 3 * D])
        wp = [sb(f"w{i}", [P, KT, 3 * D], F32R) for i in range(2)]
        bias_qk, bias_v = sb("bias_qk", [P, 2 * KT]), sb("bias_v", [P, D])
        xt = [[[sb(f"xt{p}{i}{k}", [P, S], F32R) for k in range(KT)] for i in range(2)] for p in range(2)]
        v = [sb(f"v{p}", [P, TT, H, 32]) for p in range(2)]
        s_w, s_bias, s_const, s_whi, s_wlo = sem("w"), sem("bias"), sem("const"), sem("whi"), sem("wlo")
        s_x = [sem(f"x{i}") for i in range(3)]
        s_v, s_vout = sem("v"), sem("vout")
        s_vst = [sem(f"vst{p}") for p in range(2)]
        ln = LayerNorm(nc, ctx, sh, "qkv_ln", sh.psum[0:2], lambda b, p, k: xt[p][0][k][:, :],
                       lambda b, p, k: xt[p][1][k][:, :])
        out = SplitOut(nc, ctx, sh, "qkv_out", sh.psum[2:6], bias_qk,
                       [(sh.q_parts, 0, False), (sh.q_parts, 1, False), (sh.k_parts, 0, True), (sh.k_parts, 1, True)], 2 * KT)
        vbank = sh.psum[6:8]
        CHUNKS = 3
        W = 3 * D // CHUNKS

        with nc.Block() as block:
            @block.sync
            def _(sp):
                for p in range(2):
                    sp.sem_inc(s_vst[p], 16 * NG)
                xs = x.rearrange("b (j p) d -> p (b j) d", p=P)
                sp.dma_start(sh.x[:, 0:TT, :], xs[:, 0:TT, :]).then_inc(s_x[0], 16)
                sp.dma_start(raw[:, :, :], w.rearrange("(k p) n -> p k n", p=P)).then_inc(s_w, 16)
                sp.dma_start(bias_qk[:, :], b_qk).then_inc(s_bias, 16)
                sp.dma_start(bias_v[:, :], b_v.unsqueeze(0).broadcast_to([P, D])).then_inc(s_bias, 16)
                sp.dma_start(sh.x[:, TT:2 * TT, :], xs[:, TT:2 * TT, :]).then_inc(s_x[1], 16)
                sp.dma_start(sh.x[:, 2 * TT:B * TT, :], xs[:, 2 * TT:B * TT, :]).then_inc(s_x[2], 16)
                sp.dma_start(sh.experts[:, :, :, :], experts.rearrange("(k p) e n -> p k e n", p=P)).then_inc(sh.s_experts, 16)

                def step(b, p, half, first, last):
                    for u in range(2 * KT):
                        out.store(sp, b, u)
                    sp.wait_ge(s_vout, 2 * b + 2)
                    for g in range(NG):
                        sp.dma_start(sh.v_ones[NG * b + g], v[p][:, :, GH * g:GH * (g + 1), :]
                                     .rearrange("p k h c -> p k (h c)")).then_inc(s_vst[p], 16)
                each_batch(sp, step)
                out.all_stored(sp)
                for p in range(2):
                    sp.wait_ge(s_vst[p], 16 * NG * (B // 2 + 1))

            @block.gpsimd
            def _(pool):
                pool.memset(sh.ident[:, :], 0.0).then_inc(s_const, 1)
                pool.memset(sh.ident_bf[:, :], 0.0).then_inc(s_const, 1)
                pool.memset(sh.causal_neg[:, :], 0.0).then_inc(s_const, 1)
                pool.memset(sh.causal_neg_t[:, :], 0.0).then_inc(s_const, 1)
                pool.memset(sh.minus_half[:, :], -0.5).then_inc(s_const, 1)
                for m in range(2):
                    pool.memset(v[m][:, :, :, HD:32], 1.0).then_inc(s_const, 1)
                pool.wait_ge(s_const, 7)
                for m in (sh.ident, sh.ident_bf):
                    pool.affine_select(out=m[:, :], in_=m[:, :], compare_op=ALU.not_equal, fill=1.0, base=0,
                                       pattern=[[-1, P]], channel_multiplier=1).then_inc(s_const, 1)
                pool.affine_select(out=sh.causal_neg[:, :], in_=sh.causal_neg[:, :], compare_op=ALU.is_ge,
                                   fill=NEG, base=0, pattern=[[-1, P]], channel_multiplier=1).then_inc(s_const, 1)
                pool.affine_select(out=sh.causal_neg_t[:, :], in_=sh.causal_neg_t[:, :], compare_op=ALU.is_ge,
                                   fill=NEG, base=0, pattern=[[1, P]], channel_multiplier=-1).then_inc(s_const, 1)

                ln.deviation(pool, 0)

                def step(b, p, half, first, last):
                    if not last:
                        ln.deviation(pool, b + 1)
                    for u in range(2 * KT):
                        out.third(pool, b, u)
                each_batch(pool, step)

            @block.scalar
            def _(act):
                for c in range(CHUNKS):
                    split_weights(act, None, raw[:, :, c * W:(c + 1) * W], wp[0][:, :, c * W:(c + 1) * W], None,
                                  s_w, 16, s_whi, None, 0)
                ln.take_hi(act, 0, 0)
                act.wait_ge(s_bias, 32)

                def step(b, p, half, first, last):
                    for u in range(2 * KT):
                        out.bias_and_first(act, b, u)
                        if u == 1 and not last:
                            if not first:
                                act.wait_ge(s_v, 2 * b)
                            ln.take_hi(act, b + 1, 1 - p)
                each_batch(act, step)

            @block.vector
            def _(dve):
                dve.wait_ge(s_x[0], 16)
                ln.moments(dve, 0)
                ln.normalise(dve, 0)
                for c in range(CHUNKS):
                    cut = slice(c * W, (c + 1) * W)
                    split_weights(None, dve, raw[:, :, cut], wp[0][:, :, cut], wp[1][:, :, cut],
                                  s_w, 16, s_whi, s_wlo, c + 1)
                ln.take_lo(dve, 0, 0)
                dve.wait_ge(s_bias, 32)
                dve.wait_ge(s_const, 11)

                def step(b, p, half, first, last):
                    if not last:
                        dve.wait_ge(s_x[1] if first else s_x[2], 16)
                        ln.moments(dve, b + 1)
                        ln.normalise(dve, b + 1)
                    for u in range(2 * KT):
                        out.second(dve, b, u)
                        if u == 1 and not last:
                            ln.take_lo(dve, b + 1, 1 - p)
                    dve.wait_ge(s_vst[p], 16 * NG * (half + 1))
                    for i in range(2):
                        dve.wait_ge(s_v, 2 * b + i + 1)
                        for j in range(2):
                            ins = dve.tensor_tensor(
                                v[p][:, 2 * i + j, :, 0:HD],
                                vbank[i][:, j * D:(j + 1) * D].rearrange("p (h d) -> p h d", d=HD),
                                bias_v[:, :].rearrange("p (h d) -> p h d", d=HD), ALU.add)
                        ins.then_inc(s_vout, 1)
                each_batch(dve, step)

            @block.tensor
            def _(pe):
                pe.wait_ge(s_const, 11)
                ln.turn(pe, 0)

                def step(b, p, half, first, last):
                    pe.wait_ge(ln.s_lo, KT * b + KT)
                    for u in range(2 * KT):
                        if first:
                            pe.wait_ge(s_wlo, 2 if u >= KT else 1)
                        else:
                            pe.wait_ge(out.s_t, 2 * KT * b + u - 3)
                        for i, (wi, xi) in enumerate(PASSES):
                            for k in range(KT):
                                mm = pe.matmul(out.banks[u][:, :], wp[wi][:, k, u * P:(u + 1) * P],
                                               xt[p][xi][k][:, :], start=(i == 0 and k == 0),
                                               stop=(i == 2 and k == KT - 1))
                        mm.then_inc(out.s_made, 1)
                        if u == 1 and not last:
                            ln.turn(pe, b + 1)
                    for j in range(TT):
                        if first:
                            pe.wait_ge(s_wlo, 3)
                        elif j % 2 == 0:
                            pe.wait_ge(s_vout, 2 * b - 1 + j // 2)
                        for i, (wi, xi) in enumerate(PASSES):
                            for k in range(KT):
                                mm = pe.matmul(vbank[j // 2][:, (j % 2) * D:(j % 2 + 1) * D],
                                               xt[p][xi][k][:, j * P:(j + 1) * P], wp[wi][:, k, 2 * D:3 * D],
                                               start=(i == 0 and k == 0), stop=(i == 2 and k == KT - 1))
                        if j % 2:
                            mm.then_inc(s_v, 1)
                each_batch(pe, step)


MAX_UNITS = [[(0, 3, 0, 512)], [(1, 3, 0, 512)],
             [(0, 2, 0, 384), (0, 0, 384, 128)], [(1, 2, 0, 384), (1, 0, 384, 128)],
             [(0, 1, 0, 256), (1, 1, 256, 256)]]
EXP_UNITS = [[(0, 0, 0, 512)], [(1, 0, 0, 512)],
             [(0, 1, 0, 384), (0, 3, 384, 128)], [(1, 1, 0, 384), (1, 3, 384, 128)],
             [(0, 2, 0, 256), (1, 2, 256, 256)]]
PAIRS = GH // 2
UNITS = PAIRS * len(MAX_UNITS)
AHEAD = 3
MAX_DIAGONAL = [slice(3, 4), slice(3, 4), slice(2, 4), slice(2, 4), slice(1, 4, 2)]
EXP_DIAGONAL = [slice(0, 1), slice(0, 1), slice(0, 4, 3), slice(0, 4, 3), slice(0, 4, 2)]


def probs_at(head, kt):
    for u, segments in enumerate(EXP_UNITS):
        for h, t, c, _ in segments:
            if (h, t) == (head % 2, kt):
                return head // 2 * len(EXP_UNITS) + u, c


def attention(nc, sh, name, q_parts, k_parts, v_ones, context):
    with ExitStack() as ctx:
        sb = lambda n, s, d=F32: ctx.enter_context(nc.sbuf_tensor(f"{name}_{n}", s, d))
        sem = lambda n: sh.semaphore(f"{name}_{n}")
        three = range(AHEAD)
        k = [sb(f"k{i}", [ROWS + 2, GH, S], BF16) for i in three]
        q = [sb(f"q{i}", [ROWS + 2, GH, S], BF16) for i in three]
        v = [sb(f"v{i}", [P, TT, GH * 32]) for i in three]
        probs = [sb(f"probs{i}", [P, UNITS, S]) for i in three]
        block_max = sb("block_max", [P, UNITS, TT])
        row_max = sb("row_max", [P, GH, TT])
        shift = sb("shift", [P, 2, GH * TT], BF16)
        shift_rows = [sb(f"shift_rows{i}", [2 * GH * TT, P], BF16) for i in three]
        raw = [sb(f"raw{i}", [P, S]) for i in three]
        recip = sb("recip", [P, TT * GH])
        max_bank, exp_bank, pv_bank = sh.psum[0:3], sh.psum[3:6], sh.psum[6]
        turned_bank = sh.psum[7]

        s_ones = sem("ones")
        s_loaded = [sem(f"loaded{i}") for i in three]
        s_v = [sem(f"v{i}") for i in three]
        s_max_made, s_max_read = sem("max_made"), sem("max_read")
        s_row_max, s_shift_hi, s_shift = sem("row_max"), sem("hi"), sem("shift")
        s_shift_turned, s_shift_rows = sem("shift_turned"), sem("shift_rows")
        s_shifted = [sem(f"shifted{i}") for i in three]
        s_exp_made, s_exp_read = sem("exp_made"), sem("exp_read")
        s_pv, s_raw = sem("pv"), sem("raw")
        s_ctx_turned, s_recip, s_ctx = sem("ctx_turned"), sem("recip"), sem("ctx")
        LOADS = 2 * len(RUNS)

        def each_group(eng, step, tail=1):
            step(0, 0, 0, True, False)
            with eng.Fori(0, (GROUPS - 1 - tail) // AHEAD) as t:
                step(AHEAD * t + 1, 1, t, False, False)
                step(AHEAD * t + 2, 2, t, False, False)
                step(AHEAD * t + 3, 0, t + 1, False, False)
            for i in range(GROUPS - tail, GROUPS):
                step(i, i % AHEAD, i // AHEAD, False, i == GROUPS - 1)

        with nc.Block() as block:
            @block.sync
            def _(sp):
                def load(dst, parts, which, i, r):
                    for row, *slots in RUNS:
                        a, z = slots[which]
                        sp.dma_start(dst[r][HD * row:HD * (row + z - a), :, :].rearrange("r h t -> r (h t)"),
                                     parts[i, a:z].rearrange("s (r h) t -> (s r) (h t)", h=GH)
                                     ).then_inc(s_loaded[r], 16)

                def load_v(i, r):
                    sp.dma_start(v[r][:, :, :], v_ones[i]).then_inc(s_v[r], 16)

                for i in three:
                    load(k, k_parts, 1, i, i)
                    load(q, q_parts, 0, i, i)
                    load_v(i, i)

                def step(i, r, turn, first, last):
                    more = not first and not (isinstance(i, int) and i + 2 >= GROUPS)
                    nr = (r + 2) % AHEAD
                    if more:
                        sp.wait_ge(s_exp_made, UNITS * i)
                        load(k, k_parts, 1, i + 2, nr)
                    sp.wait_ge(s_shift_rows, i + 1)
                    sp.dma_start(q[r][ROWS:ROWS + 2, :, :].rearrange("s h (c t) -> s (h c) t", t=P),
                                 shift_rows[r][:, :]).then_inc(s_shifted[r], 16)
                    if more:
                        load(q, q_parts, 0, i + 2, nr)
                        sp.wait_ge(s_pv, i)
                        load_v(i + 2, nr)
                each_group(sp, step, tail=4)

            @block.gpsimd
            def _(pool):
                for i in three:
                    pool.memset(k[i][ROWS:ROWS + 2, :, :], 1.0).then_inc(s_ones, 1)

            @block.scalar
            def _(act):
                act.sem_inc(s_raw, 1)

                def take_pv(i, r):
                    act.wait_ge(s_pv, i + 1)
                    act.copy(raw[r][:, :], pv_bank[:, :]).then_inc(s_raw, 1)

                def exponentials(i, r):
                    for u in range(UNITS):
                        act.wait_ge(s_exp_made, UNITS * i + u + 1)
                        act.activation(probs[r][:, u, :], exp_bank[(r + u) % 3][:, :], ACT.Exp,
                                       scale=SCALE).then_inc(s_exp_read, 1)

                def step(i, r, turn, first, last):
                    if not first:
                        take_pv(i - 1, (r + 2) % AHEAD)
                    exponentials(i, r)
                each_group(act, step)
                take_pv(GROUPS - 1, (GROUPS - 1) % AHEAD)

            @block.vector
            def _(dve):
                def maxima(i, r, units):
                    for u in units:
                        dve.wait_ge(s_max_made, UNITS * i + u + 1)
                        dve.tensor_reduce(block_max[:, u, :],
                                          max_bank[(r + u) % 3][:, :].rearrange("p (c t) -> p c t", t=P),
                                          AX.X, ALU.max).then_inc(s_max_read, 1)

                def shifts(i):
                    bm = block_max[:, :, :].rearrange("p (g u) c -> p g u c", g=PAIRS)
                    rm = row_max[:, :, :].rearrange("p (g h) t -> p g h t", g=PAIRS)
                    dve.wait_ge(s_max_read, UNITS * (i + 1))
                    dve.tensor_reduce(rm[:, :, :, 3], bm[:, :, 0:2, :], AX.X, ALU.max, negate=True).then_inc(s_row_max, 1)
                    dve.tensor_reduce(rm[:, :, :, 2], bm[:, :, 2:4, 0:3], AX.X, ALU.max, negate=True).then_inc(s_row_max, 1)
                    dve.tensor_scalar(rm[:, :, :, 0], bm[:, :, 2:4, 3], -1.0, None, ALU.mult).then_inc(s_row_max, 1)
                    for g in range(PAIRS):
                        dve.tensor_reduce(rm[:, g, :, 1], bm[:, g, 4, :].rearrange("p (h c) -> p h c", c=2),
                                          AX.X, ALU.max, negate=True).then_inc(s_row_max, 1)
                    dve.wait_ge(s_row_max, (3 + PAIRS) * (i + 1))
                    flat = row_max[:, :, :].rearrange("p h t -> p (h t)")
                    if not is_first(i):
                        dve.wait_ge(s_shift_turned, i)
                    dve.tensor_copy(shift[:, 0, :], flat).then_inc(s_shift_hi, 1)
                    dve.wait_ge(s_shift_hi, i + 1)
                    dve.tensor_tensor(shift[:, 1, :], flat, shift[:, 0, :], ALU.subtract).then_inc(s_shift, 1)

                def shift_to_rows(i, r):
                    dve.wait_ge(s_shift_turned, i + 1)
                    dve.tensor_copy(shift_rows[r][:, :], turned_bank[0:2 * GH * TT, 0:P // 2].bitcast(BF16)).then_inc(s_shift_rows, 1)

                def normalise(i):
                    dve.wait_ge(s_ctx_turned, i + 1)
                    heads = turned_bank[:, :].rearrange("p (n c) -> p n c", c=32)
                    dve.reciprocal(recip[:, :], heads[:, :, HD]).then_inc(s_recip, 1)
                    dve.wait_ge(s_recip, i + 1)
                    dve.tensor_tensor(context[:, i, :, :].rearrange("p t (h d) -> p (t h) d", d=HD),
                                      heads[:, :, 0:HD], recip[:, :].unsqueeze(2).broadcast_to([P, TT * GH, HD]),
                                      ALU.mult).then_inc(s_ctx, 1)

                dve.sem_inc(s_ctx, 1)
                maxima(0, 0, range(UNITS))
                shifts(0)

                def step(i, r, turn, first, last):
                    if not last:
                        maxima(i + 1, (r + 1) % AHEAD, range(2))
                    shift_to_rows(i, r)
                    if not last:
                        maxima(i + 1, (r + 1) % AHEAD, range(2, 5))
                    if not last:
                        maxima(i + 1, (r + 1) % AHEAD, range(5, 7))
                    if not first:
                        normalise(i - 1)
                    if not last:
                        maxima(i + 1, (r + 1) % AHEAD, range(7, UNITS))
                        shifts(i + 1)
                each_group(dve, step)
                normalise(GROUPS - 1)

            @block.tensor
            def _(pe):
                def mask(bank, blocks, causal):
                    out = bank[:, :].rearrange("p (c t) -> p c t", t=P)[:, blocks, :]
                    return pe.matmul(out, sh.ident_bf[:, :], causal[:, :].unsqueeze(1).broadcast_to([P, out.shape[1], P]),
                                     start=False, stop=True, skip_group_check=True)

                def max_units(i, r, units, first=False):
                    for u in units:
                        n = UNITS * i + u
                        if not (first and u < 3):
                            pe.wait_ge(s_max_read, n - 2)
                        pair, segments = u // len(MAX_UNITS), MAX_UNITS[u % len(MAX_UNITS)]
                        for h, qt, c, w in segments:
                            h += 2 * pair
                            bank = max_bank[(r + u) % 3]
                            pe.matmul(bank[:, c:c + w], q[r][0:ROWS, h, qt * P:(qt + 1) * P], k[r][0:ROWS, h, 0:w],
                                      start=(c == 0), stop=False, skip_group_check=True)
                        mask(bank, MAX_DIAGONAL[u % len(MAX_UNITS)], sh.causal_neg).then_inc(s_max_made, 1)

                def exp_units(i, r, units, first=False):
                    for u in units:
                        n = UNITS * i + u
                        if not (first and u < 3):
                            pe.wait_ge(s_exp_read, n - 2)
                        pair, segments = u // len(EXP_UNITS), EXP_UNITS[u % len(EXP_UNITS)]
                        for h, kt, c, w in segments:
                            h += 2 * pair
                            bank = exp_bank[(r + u) % 3]
                            pe.matmul(bank[:, c:c + w], k[r][:, h, kt * P:(kt + 1) * P], q[r][:, h, kt * P:S],
                                      start=(c == 0), stop=False, skip_group_check=True)
                        mask(bank, EXP_DIAGONAL[u % len(EXP_UNITS)], sh.causal_neg_t).then_inc(s_exp_made, 1)

                def turn_shift(i, first):
                    pe.wait_ge(s_shift, i + 1)
                    if not first:
                        pe.wait_ge(s_shift_rows, i)
                        pe.wait_ge(s_ctx, i)
                    pe.transpose(turned_bank[0:2 * GH * TT, 0:P // 2].bitcast(BF16), shift[:, :, :].rearrange("p s c -> p (s c)"),
                                 sh.ident_bf[:, :]).then_inc(s_shift_turned, 1)

                def weigh(i, r, turn):
                    pe.wait_ge(s_v[r], 16 * (turn + 1))
                    pe.wait_ge(s_exp_read, UNITS * (i + 1))
                    pe.wait_ge(s_raw, i + 1)
                    for kt in range(TT):
                        for h in range(GH):
                            u, c = probs_at(h, kt)
                            mm = pe.matmul(pv_bank[32 * h:32 * (h + 1), kt * P:S], v[r][:, kt, 32 * h:32 * (h + 1)],
                                           probs[r][:, u, c:c + S - kt * P], start=(kt == 0), stop=(kt == TT - 1))
                    mm.then_inc(s_pv, 1)

                def turn_ctx(i, r):
                    pe.wait_ge(s_raw, i + 2)
                    for t in range(TT):
                        mm = pe.transpose(turned_bank[:, t * P:(t + 1) * P], raw[r][:, t * P:(t + 1) * P],
                                          sh.ident[:, :])
                    mm.then_inc(s_ctx_turned, 1)

                pe.wait_ge(s_loaded[0], 16 * LOADS)
                pe.wait_ge(s_ones, AHEAD)
                max_units(0, 0, range(UNITS), first=True)

                def step(i, r, turn, first, last):
                    nr = (r + 1) % AHEAD
                    if not last:
                        pe.wait_ge(s_loaded[nr], 16 * LOADS * ((turn + 1 if nr == 0 else turn) + 1))
                        max_units(i + 1, nr, range(2))
                    turn_shift(i, first)
                    if not first:
                        pr = (r + 2) % AHEAD
                        weigh(i - 1, pr, turn - 1 if r == 0 else turn)
                    if not last:
                        max_units(i + 1, nr, range(2, 5))
                    if not first:
                        pe.wait_ge(s_shift_rows, i + 1)
                        turn_ctx(i - 1, pr)
                    pe.wait_ge(s_shifted[r], 16 * (turn + 1))
                    exp_units(i, r, range(2), first)
                    for n in range(5):
                        if not last:
                            max_units(i + 1, nr, [5 + n])
                        if n < 4:
                            exp_units(i, r, range(2 + 2 * n, 4 + 2 * n), first)
                each_group(pe, step)
                weigh(GROUPS - 1, (GROUPS - 1) % AHEAD, (GROUPS - 1) // AHEAD)
                pe.wait_ge(s_ctx, GROUPS)
                turn_ctx(GROUPS - 1, (GROUPS - 1) % AHEAD)


def stage_context(act, turned, context, b):
    if not is_first(b):
        act.wait_ge(turned.s_turned, KT * b)
    act.copy(turned.tokens[:, :, :].rearrange("p t (g c) -> p g t c", c=GR),
             context[:, bass.ds(NG * b, NG), :, :]).then_inc(turned.s_tokens, 1)


def convolve(nc, sh, context, w, bias):
    TAPS = 3
    with ExitStack() as ctx:
        sb = lambda n, s, d=F32: ctx.enter_context(nc.sbuf_tensor(f"conv_{n}", s, d))
        sem = lambda n: sh.semaphore(f"conv_{n}")
        raw = sb("raw", [P, KT, TAPS * D])
        wp = [sb(f"w{i}", [P, KT, TAPS * D], F32R) for i in range(2)]
        bias_sb = sb("bias", [P, KT])
        c = [[[sb(f"c{p}{i}{k}", [P, S + 2], F32R) for k in range(KT)] for i in range(2)] for p in range(2)]
        s_w, s_bias, s_zero, s_whi, s_wlo = sem("w"), sem("bias"), sem("zero"), sem("whi"), sem("wlo")
        turned = Turned(nc, ctx, sh, "conv_in", sh.psum[0:2], lambda b, p, k: c[p][0][k][:, 1:S + 1],
                        lambda b, p, k: c[p][1][k][:, 1:S + 1], 1)
        out = SplitOut(nc, ctx, sh, "conv_out", sh.psum[2:4], bias_sb,
                       [(sh.q2_parts, 0, False), (sh.q2_parts, 1, False)], KT)

        with nc.Block() as block:
            @block.sync
            def _(sp):
                sp.dma_start(raw[:, :, :], w.rearrange("(k p) n -> p k n", p=P)).then_inc(s_w, 16)
                sp.dma_start(bias_sb[:, :], bias).then_inc(s_bias, 16)

                def step(b, p, half, first, last):
                    for u in range(KT):
                        out.store(sp, b, u)
                each_batch(sp, step)
                out.all_stored(sp)

            @block.gpsimd
            def _(pool):
                for p in range(2):
                    for i in range(2):
                        for k in range(KT):
                            pool.memset(c[p][i][k][:, 0:S + 2:S + 1].bitcast(F32), 0.0).then_inc(s_zero, 1)

                def step(b, p, half, first, last):
                    for u in range(KT):
                        out.third(pool, b, u)
                each_batch(pool, step)

            @block.scalar
            def _(act):
                stage_context(act, turned, context, 0)
                for t in range(TAPS):
                    split_weights(act, None, raw[:, :, t * D:(t + 1) * D], wp[0][:, :, t * D:(t + 1) * D], None,
                                  s_w, 16, s_whi, None, 0)
                turned.take_hi(act, 0, 0)
                act.wait_ge(s_bias, 16)

                def step(b, p, half, first, last):
                    if not last:
                        stage_context(act, turned, context, b + 1)
                    out.bias_and_first(act, b, 0)
                    if not last:
                        turned.take_hi(act, b + 1, 1 - p)
                    out.bias_and_first(act, b, 1)
                each_batch(act, step)

            @block.vector
            def _(dve):
                for t in range(TAPS):
                    cut = slice(t * D, (t + 1) * D)
                    split_weights(None, dve, raw[:, :, cut], wp[0][:, :, cut], wp[1][:, :, cut],
                                  s_w, 16, s_whi, s_wlo, t + 1)
                turned.take_lo(dve, 0, 0)

                def step(b, p, half, first, last):
                    out.second(dve, b, 0)
                    if not last:
                        turned.take_lo(dve, b + 1, 1 - p)
                    out.second(dve, b, 1)
                each_batch(dve, step)

            @block.tensor
            def _(pe):
                turned.turn(pe, 0)
                pe.wait_ge(s_zero, 4 * KT)

                def step(b, p, half, first, last):
                    pe.wait_ge(turned.s_lo, KT * b + KT)
                    for u in range(KT):
                        if not first:
                            pe.wait_ge(out.s_t, KT * b + u - 1)
                        for t in range(TAPS):
                            if first and u == 0:
                                pe.wait_ge(s_wlo, t + 1)
                            for i, (wi, xi) in enumerate(PASSES):
                                for k in range(KT):
                                    at = t * D + u * P
                                    mm = pe.matmul(out.banks[u][:, :], wp[wi][:, k, at:at + P],
                                                   c[p][xi][k][:, t:t + S], start=(t == 0 and i == 0 and k == 0),
                                                   stop=(t == TAPS - 1 and i == 2 and k == KT - 1))
                        mm.then_inc(out.s_made, 1)
                        if u == 0 and not last:
                            turned.turn(pe, b + 1)
                each_batch(pe, step)


class Gate:

    def __init__(self, nc, ctx, sh, name, banks):
        sb = lambda n, s, d=F32: ctx.enter_context(nc.sbuf_tensor(f"{name}_{n}", s, d))
        sem = lambda n: sh.semaphore(f"{name}_{n}")
        self.sh, self.banks, self.rows = sh, banks, sb("rows", [NE, S])
        self.s_made, self.s_rows, self.s_turned, self.s_kept = sem("made"), sem("rows"), sem("turned"), sem("kept")

    def multiply(self, pe, b):
        if not is_first(b):
            pe.wait_ge(self.s_rows, b)
        for i, (wi, xi) in enumerate(PASSES):
            for k in range(KT):
                mm = pe.matmul(self.banks[0][:, :], self.sh.gate_w[wi][:, k, :],
                               self.sh.xt[:, xi, k, bass.ds(S * b, S)], start=(i == 0 and k == 0),
                               stop=(i == 2 and k == KT - 1))
        mm.then_inc(self.s_made, 1)

    def take_rows(self, act, b):
        act.wait_ge(self.s_made, b + 1)
        if not is_first(b):
            act.wait_ge(self.s_turned, b)
        act.activation(self.rows[:, :], self.banks[0][0:NE, :], ACT.Identity,
                       bias=self.sh.gate_b[:, :]).then_inc(self.s_rows, 1)

    def turn(self, pe, b):
        if not is_first(b):
            pe.wait_ge(self.s_kept, b)
        wait_apart(pe, self.s_rows, b + 1)
        for j in range(TT):
            mm = pe.transpose(self.banks[1][:, NE * j:NE * (j + 1)], self.rows[:, j * P:(j + 1) * P],
                              self.sh.ident[0:NE, 0:NE])
        mm.then_inc(self.s_turned, 1)

    def keep(self, dve, b):
        dve.wait_ge(self.s_turned, b + 1)
        dve.tensor_copy(self.sh.gates[:, bass.ds(TT * b, TT), :],
                        self.banks[1][:, 0:TT * NE].rearrange("p (t e) -> p t e", e=NE)).then_inc(self.s_kept, 1)


def project_out(nc, sh, context, w, bias, gate_w, gate_b):
    with ExitStack() as ctx:
        sb = lambda n, s, d=F32: ctx.enter_context(nc.sbuf_tensor(f"proj_{n}", s, d))
        sem = lambda n: sh.semaphore(f"proj_{n}")
        raw, gate_raw = sb("raw", [P, KT, D]), sb("gate_raw", [P, KT, P])
        wp = [sb(f"w{i}", [P, KT, D], F32R) for i in range(2)]
        bias_row = sb("bias", [P, D])
        c = [[[sb(f"c{p}{i}{k}", [P, S], F32R) for k in range(KT)] for i in range(2)] for p in range(2)]
        s_w, s_const, s_whi, s_wlo, s_pad = sem("w"), sem("const"), sem("whi"), sem("wlo"), sem("pad")
        s_gw = sem("gw")
        s_biased, s_made, s_added = sem("biased"), sem("made"), sem("added")
        turned = Turned(nc, ctx, sh, "proj_in", sh.psum[0:2], lambda b, p, k: c[p][0][k][:, :],
                        lambda b, p, k: c[p][1][k][:, :], 1)
        bank = sh.psum[2:4]
        ln = LayerNorm(nc, ctx, sh, "proj_ln", sh.psum[4:6], sh.xt_part(0), sh.xt_part(1))
        gate = Gate(nc, ctx, sh, "proj_gate", sh.psum[6:8])

        with nc.Block() as block:
            @block.sync
            def _(sp):
                sp.dma_start(raw[:, :, :], w.rearrange("(k p) n -> p k n", p=P)).then_inc(s_w, 16)
                sp.dma_start(bias_row[:, :], bias.unsqueeze(0).broadcast_to([P, D])).then_inc(s_const, 16)
                sp.dma_start(sh.gate_b[:, :], gate_b).then_inc(s_const, 16)
                sp.wait_ge(s_pad, 1)
                sp.dma_start(gate_raw[:, :, 0:NE], gate_w.rearrange("(k p) n -> p k n", p=P)).then_inc(s_gw, 16)
                sp.wait_ge(s_gw, 16)

            @block.gpsimd
            def _(pool):
                pool.memset(gate_raw[:, :, :], 0.0).then_inc(s_pad, 1)
                pool.wait_ge(s_const, 32)

                def step(b, p, half, first, last):
                    if not first:
                        ln.deviation(pool, b - 1)
                    row = bias_row[:, :].unsqueeze(1).broadcast_to([P, TT, D])
                    tokens = sh.x[:, bass.ds(TT * b, TT), :]
                    pool.tensor_tensor(tokens, tokens, row, ALU.add).then_inc(s_biased, 1)
                each_batch(pool, step, head=2)
                ln.deviation(pool, B - 1)

            @block.scalar
            def _(act):
                stage_context(act, turned, context, 0)
                split_weights(act, None, raw[:, :, :], wp[0][:, :, :], None, s_w, 16, s_whi, None, 0)
                split_weights(act, None, gate_raw[:, :, :], sh.gate_w[0][:, :, :], None, s_gw, 16, s_whi, None, 0)
                turned.take_hi(act, 0, 0)
                act.wait_ge(s_const, 32)

                def step(b, p, half, first, last):
                    if not last:
                        stage_context(act, turned, context, b + 1)
                        if not first:
                            act.wait_ge(s_made, 2 * b)
                        turned.take_hi(act, b + 1, 1 - p)
                    if not first:
                        ln.take_hi(act, b - 1, 0)
                        gate.take_rows(act, b - 1)
                each_batch(act, step, head=2)
                ln.take_hi(act, B - 1, 0)
                gate.take_rows(act, B - 1)

            @block.vector
            def _(dve):
                split_weights(None, dve, raw[:, :, :], wp[0][:, :, :], wp[1][:, :, :], s_w, 16, s_whi, s_wlo, 1)
                split_weights(None, dve, gate_raw[:, :, :], sh.gate_w[0][:, :, :], sh.gate_w[1][:, :, :],
                              s_gw, 16, s_whi, s_wlo, 2)
                turned.take_lo(dve, 0, 0)

                def step(b, p, half, first, last):
                    if not first:
                        ln.normalise(dve, b - 1)
                    if not last:
                        turned.take_lo(dve, b + 1, 1 - p)
                    dve.wait_ge(s_biased, b + 1)
                    for i in range(2):
                        dve.wait_ge(s_made, 2 * b + i + 1)
                        tokens = sh.x[:, bass.ds(TT * b + 2 * i, 2), :]
                        dve.tensor_tensor(tokens, bank[i][:, :].rearrange("p (t d) -> p t d", d=D), tokens,
                                          ALU.add).then_inc(s_added, 1)
                    if not first:
                        ln.take_lo(dve, b - 1, 0)
                    ln.moments(dve, b, (s_added, 2 * b + 2))
                    if not first:
                        gate.keep(dve, b - 1)
                each_batch(dve, step, head=2)
                ln.normalise(dve, B - 1)
                ln.take_lo(dve, B - 1, 0)
                gate.keep(dve, B - 1)

            @block.tensor
            def _(pe):
                turned.turn(pe, 0)
                pe.wait_ge(s_wlo, 2)

                def step(b, p, half, first, last):
                    pe.wait_ge(turned.s_lo, KT * b + KT)
                    for j in range(TT):
                        if not first and j % 2 == 0:
                            pe.wait_ge(s_added, 2 * b - 1 + j // 2)
                        for i, (wi, xi) in enumerate(PASSES):
                            for k in range(KT):
                                mm = pe.matmul(bank[j // 2][:, (j % 2) * D:(j % 2 + 1) * D],
                                               c[p][xi][k][:, j * P:(j + 1) * P], wp[wi][:, k, :],
                                               start=(i == 0 and k == 0), stop=(i == 2 and k == KT - 1))
                        if j % 2:
                            mm.then_inc(s_made, 1)
                    if not last:
                        turned.turn(pe, b + 1)
                    if not first:
                        ln.turn(pe, b - 1)
                        pe.wait_ge(ln.s_lo, KT * b)
                        gate.multiply(pe, b - 1)
                        gate.turn(pe, b - 1)
                each_batch(pe, step, head=2)
                ln.turn(pe, B - 1)
                pe.wait_ge(ln.s_lo, KT * B)
                gate.multiply(pe, B - 1)
                gate.turn(pe, B - 1)


def mix_experts(nc, sh, name, expert_b, out):
    TOTAL = B * S * TOP_K
    with ExitStack() as ctx:
        sb = lambda n, s, d=F32: ctx.enter_context(nc.sbuf_tensor(f"{name}_{n}", s, d))
        sem = lambda n: sh.semaphore(f"{name}_{n}")
        beats = sb("beats", [P, B * TT, NE, NE])
        rank, chosen = sb("rank", [P, B * TT, NE]), sb("chosen", [P, B * TT, NE])
        won, ones = sb("won", [P, NE]), sb("ones", [P, P])
        share = sb("share", [P, NE])
        bias_raw, floor, bias = sb("bias_raw", [P, KT, NE]), sb("floor", [P, KT, NE]), sb("bias_e", [P, KT, NE])
        bias_sum = sb("bias_sum", [P, KT])
        scaled = [sb(f"scaled{i}", [P, KT, D]) for i in range(2)]
        wp = [sb(f"w{i}", [P, KT, NE, D], F32R) for i in range(2)]
        acc = [[sb(f"acc{p}{m}", [P, S]) for m in range(KT)] for p in range(2)]
        s_bias, s_ones, s_beats, s_rank = sem("bias"), sem("ones"), sem("beats"), sem("rank")
        s_chosen, s_won, s_count = sem("chosen"), sem("won"), sem("count")
        s_share, s_floor, s_scaled, s_whi, s_wlo = sem("share"), sem("floor"), sem("scaled"), sem("whi"), sem("wlo")
        s_made, s_acc, s_back, s_added, s_stored = sem("made"), sem("acc"), sem("back"), sem("added"), sem("stored")
        unit_bank, back_bank = sh.psum[0:4], sh.psum[4:6]
        UN = NE * KT
        ln = None if out is not None else LayerNorm(nc, ctx, sh, f"{name}_ln", sh.psum[6:8], sh.xt_part(0), sh.xt_part(1))

        with nc.Block() as block:
            @block.sync
            def _(sp):
                sp.dma_start(bias_raw[:, :, :], expert_b).then_inc(s_bias, 16)
                sp.wait_ge(s_bias, 16)
                if out is not None:
                    def store(b):
                        sp.wait_ge(s_added, KT * (b + 1))
                        sp.dma_start(out[b].rearrange("(j p) d -> p j d", p=P),
                                     sh.x[:, bass.ds(TT * b, TT), :]).then_inc(s_stored, 16)

                    def step(b, p, half, first, last):
                        if not first:
                            store(b - 1)
                    each_batch(sp, step)
                    store(B - 1)
                    sp.wait_ge(s_stored, 16 * B)

            @block.gpsimd
            def _(pool):
                pool.memset(ones[:, :], 1.0).then_inc(s_ones, 1)
                pool.memset(beats[:, :, :, :], 0.0).then_inc(s_ones, 1)
                if ln is not None:
                    def step(b, p, half, first, last):
                        if not first:
                            ln.deviation(pool, b - 1)
                    each_batch(pool, step, head=2)
                    ln.deviation(pool, B - 1)

            @block.scalar
            def _(act):
                for e in range(NE):
                    act.wait_ge(s_scaled, e + 1)
                    act.copy(wp[0][:, :, e, :], scaled[e % 2][:, :, :]).then_inc(s_whi, 1)
                if ln is not None:
                    def step(b, p, half, first, last):
                        if not first:
                            ln.take_hi(act, b - 1, 0)
                    each_batch(act, step, head=2)
                    ln.take_hi(act, B - 1, 0)

            @block.vector
            def _(dve):
                dve.wait_ge(s_ones, 2)
                g = sh.gates
                for e in range(NE):
                    for lo, hi, op in ((0, e, ALU.is_ge), (e + 1, NE, ALU.is_gt)):
                        if lo < hi:
                            ins = dve.tensor_tensor(beats[:, :, e, lo:hi], g[:, :, lo:hi],
                                                    g[:, :, e:e + 1].broadcast_to([P, B * TT, hi - lo]), op)
                            ins.then_inc(s_beats, 1)
                dve.wait_ge(s_beats, 2 * NE - 2)
                dve.tensor_reduce(rank[:, :, :], beats[:, :, :, :], AX.X, ALU.add).then_inc(s_rank, 1)
                dve.wait_ge(s_rank, 1)
                dve.tensor_scalar(chosen[:, :, :], rank[:, :, :], TOP_K - 0.5, None, ALU.is_lt).then_inc(s_chosen, 1)
                dve.wait_ge(s_chosen, 1)
                dve.tensor_reduce(won[:, :], chosen[:, :, :].rearrange("p t e -> p e t"), AX.X, ALU.add).then_inc(s_won, 1)
                dve.wait_ge(s_count, 1)
                dve.tensor_scalar(share[:, :], unit_bank[0][:, 0:NE], 1.0 / TOTAL, None, ALU.mult).then_inc(s_share, 1)
                dve.wait_ge(s_share, 1)

                def scale_expert(e):
                    if e >= 2:
                        dve.wait_ge(s_wlo, e - 1)
                    dve.tensor_scalar(scaled[e % 2][:, :, :], sh.experts[:, :, e, :], share[:, e:e + 1], None,
                                      ALU.mult).then_inc(s_scaled, 1)

                def scaled_low(e):
                    dve.wait_ge(s_whi, e + 1)
                    dve.tensor_tensor(wp[1][:, :, e, :], scaled[e % 2][:, :, :], wp[0][:, :, e, :].bitcast(F32),
                                      ALU.subtract).then_inc(s_wlo, 1)

                dve.wait_ge(sh.s_experts, 16)
                scale_expert(0)
                dve.wait_ge(s_bias, 16)
                dve.tensor_tensor(bias[:, :, :], bias_raw[:, :, :],
                                  share[:, :].unsqueeze(1).broadcast_to([P, KT, NE]), ALU.mult).then_inc(s_floor, 1)
                dve.wait_ge(s_floor, 1)
                dve.tensor_scalar(floor[:, :, :], bias[:, :, :], -1.0, None, ALU.mult).then_inc(s_floor, 1)
                dve.tensor_reduce(bias_sum[:, :], bias[:, :, :], AX.X, ALU.add).then_inc(s_floor, 1)
                for e in range(1, NE):
                    scale_expert(e)
                    scaled_low(e - 1)
                scaled_low(NE - 1)
                dve.wait_ge(s_floor, 3)

                def add_expert(b, p, e):
                    for m in range(KT):
                        n = UN * b + KT * e + m
                        z = unit_bank[(KT * e + m) % 4]
                        dve.wait_ge(s_made, n + 1)
                        if e == 0:
                            dve.tensor_scalar(acc[p][m][:, :], z[:, :], floor[:, m, e:e + 1], bias_sum[:, m:m + 1],
                                              ALU.max, ALU.add).then_inc(s_acc, 1)
                        else:
                            dve.wait_ge(s_acc, n - 1)
                            dve.scalar_tensor_tensor(out=acc[p][m][:, :], in0=z[:, :], scalar=floor[:, m, e:e + 1],
                                                     in1=acc[p][m][:, :], op0=ALU.max, op1=ALU.add).then_inc(s_acc, 1)

                def add_residual(b):
                    for m in range(KT):
                        dve.wait_ge(s_back, KT * b + m + 1)
                        tokens = sh.x[:, bass.ds(TT * b, TT), m * P:(m + 1) * P]
                        dve.tensor_tensor(tokens, back_bank[m][:, :].rearrange("p (t d) -> p t d", d=P), tokens,
                                          ALU.add).then_inc(s_added, 1)

                def step(b, p, half, first, last):
                    for e in range(NE):
                        add_expert(b, p, e)
                        if not first:
                            if e == 1:
                                add_residual(b - 1)
                            if ln is not None and e == 2:
                                ln.moments(dve, b - 1, (s_added, KT * b))
                            if ln is not None and e == 4:
                                ln.normalise(dve, b - 1)
                            if ln is not None and e == 7:
                                ln.take_lo(dve, b - 1, 0)
                each_batch(dve, step, head=2)
                add_residual(B - 1)
                if ln is not None:
                    ln.moments(dve, B - 1, (s_added, KT * B))
                    ln.normalise(dve, B - 1)
                    ln.take_lo(dve, B - 1, 0)

            @block.tensor
            def _(pe):
                pe.wait_ge(s_ones, 1)
                pe.wait_ge(s_won, 1)
                pe.matmul(unit_bank[0][:, 0:NE], ones[:, :], won[:, :], start=True, stop=True).then_inc(s_count, 1)
                pe.wait_ge(s_share, 1)

                def turn_back(b, p):
                    for m in range(KT):
                        pe.wait_ge(s_acc, UN * b + UN - 1 + m)
                        if not is_first(b):
                            pe.wait_ge(s_added, KT * b - 1 + m)
                        for j in range(TT):
                            mm = pe.transpose(back_bank[m][:, j * P:(j + 1) * P], acc[p][m][:, j * P:(j + 1) * P],
                                              sh.ident[:, :])
                        mm.then_inc(s_back, 1)

                def step(b, p, half, first, last):
                    for e in range(NE):
                        if first:
                            pe.wait_ge(s_wlo, e + 1)
                        for m in range(KT):
                            u = KT * e + m
                            if not (first and u < 4):
                                pe.wait_ge(s_acc, UN * b + u - 3)
                            for i, (wi, xi) in enumerate(PASSES):
                                for k in range(KT):
                                    mm = pe.matmul(unit_bank[u % 4][:, :], wp[wi][:, k, e, m * P:(m + 1) * P],
                                                   sh.xt[:, xi, k, bass.ds(S * b, S)], start=(i == 0 and k == 0),
                                                   stop=(i == 2 and k == KT - 1))
                            mm.then_inc(s_made, 1)
                        if not first:
                            if e == 0:
                                turn_back(b - 1, 1 - p)
                            if ln is not None and e == 6:
                                ln.turn(pe, b - 1)
                each_batch(pe, step, head=2)
                turn_back(B - 1, (B - 1) % 2)
                if ln is not None:
                    ln.turn(pe, B - 1)


def distance_attention(nc, sh, w, bias, bias_o, spare):
    VC = D + 2
    UN = 10
    with ExitStack() as ctx:
        sb = lambda n, s, d=F32: ctx.enter_context(nc.sbuf_tensor(f"dist_{n}", s, d))
        sem = lambda n: sh.semaphore(f"dist_{n}")
        raw = spare[:, 0:KT * 4 * D].rearrange("p (k n) -> p k n", k=KT)
        free = [0]

        def take(columns):
            free[0] += columns
            return spare[:, free[0] - columns:free[0]]

        vw = [take(TT * VC).rearrange("p (t n) -> p t n", t=TT) for _ in range(2)]
        probs = take(TT * S).rearrange("p (t s) -> p t s", t=TT)
        squares = take(2 * KT * S)
        square = [squares[:, S * u:S * (u + 1)] for u in range(2 * KT)]
        q_norm, k_norm_row = take(S), take(S)
        bias_row = take(D)
        wp = [sb(f"w{i}", [P, KT, 4 * D], F32R) for i in range(2)]
        bias_sb, ones = sb("bias", [P, 3 * KT]), sb("ones", [P, P])
        qk = [[[sb(f"qk{p}{i}{u}", [P, S], F32R) for u in range(2 * KT)] for i in range(2)] for p in range(2)]
        fv = [[sb(f"v{i}{u}", [P, S], F32R) for u in range(KT)] for i in range(2)]
        k_norm = [sb(f"k_norm{p}", [P, TT]) for p in range(2)]
        recip = sb("recip", [P, TT])
        unit_bank, score_bank, out_bank = sh.psum[0:2], sh.psum[2:4], sh.psum[4:6]
        s_w, s_const, s_ones, s_whi, s_wlo = sem("w"), sem("const"), sem("ones"), sem("whi"), sem("wlo")
        s_made, s_hi, s_square, s_lo = sem("made"), sem("hi"), sem("square"), sem("lo")
        s_q_norm, s_k_row, s_k_turned, s_k_norm = sem("q_norm"), sem("k_row"), sem("k_turned"), sem("k_norm")
        s_vw, s_score, s_exponent, s_kernel, s_probs = sem("vw"), sem("score"), sem("exponent"), sem("kernel"), sem("probs")
        s_out, s_recip, s_biased, s_added = sem("out"), sem("recip"), sem("biased"), sem("added")
        ln = LayerNorm(nc, ctx, sh, "dist_ln", sh.psum[6:8], sh.xt_part(0), sh.xt_part(1),
                       squares[:, 0:TT * D].rearrange("p (t d) -> p t d", t=TT))
        gate = Gate(nc, ctx, sh, "dist_gate", score_bank)

        with nc.Block() as block:
            @block.sync
            def _(sp):
                sp.dma_start(raw, w.rearrange("(k p) n -> p k n", p=P)).then_inc(s_w, 16)
                sp.dma_start(bias_sb[:, :], bias).then_inc(s_const, 16)
                sp.dma_start(bias_row[:, :], bias_o.unsqueeze(0).broadcast_to([P, D])).then_inc(s_const, 16)

            @block.gpsimd
            def _(pool):
                pool.memset(ones[:, :], 1.0).then_inc(s_ones, 1)
                pool.wait_ge(s_wlo, 4)
                for p in range(2):
                    pool.memset(vw[p][:, :, D:VC], 1.0).then_inc(s_ones, 1)
                pool.wait_ge(s_const, 32)

                def step(b, p, half, first, last):
                    if not first:
                        ln.deviation(pool, b - 1)
                    row = bias_row[:, :].unsqueeze(1).broadcast_to([P, TT, D])
                    tokens = sh.x[:, bass.ds(TT * b, TT), :]
                    pool.tensor_tensor(tokens, tokens, row, ALU.add).then_inc(s_biased, 1)
                each_batch(pool, step, head=2)
                ln.deviation(pool, B - 1)

            @block.scalar
            def _(act):
                for c in range(4):
                    split_weights(act, None, raw[:, :, c * D:(c + 1) * D], wp[0][:, :, c * D:(c + 1) * D], None,
                                  s_w, 16, s_whi, None, 0)
                act.wait_ge(s_const, 32)

                def project(b, p):
                    for u in range(3 * KT):
                        act.wait_ge(s_made, UN * b + u + 1)
                        hi = (qk[p][0][u] if u < 2 * KT else fv[0][u - 2 * KT])[:, :]
                        act.activation(hi, unit_bank[u % 2][:, :], ACT.Identity,
                                       bias=bias_sb[:, u:u + 1]).then_inc(s_hi, 1)
                        if u < 2 * KT:
                            act.activation(square[u][:, :], unit_bank[u % 2][:, :], ACT.Square,
                                           bias=bias_sb[:, u:u + 1]).then_inc(s_square, 1)

                project(0, 0)

                def step(b, p, half, first, last):
                    act.wait_ge(s_k_norm, b + 1)
                    for t in range(TT):
                        act.wait_ge(s_exponent, TT * b + t + 1)
                        act.activation(probs[:, t, :], probs[:, t, :], ACT.Exp,
                                       bias=k_norm[p][:, t:t + 1]).then_inc(s_kernel, 1)
                        act.wait_ge(s_kernel, TT * b + t + 1)
                        act.activation(probs[:, t, :], probs[:, t, :], ACT.Exp).then_inc(s_probs, 1)
                    if not first:
                        ln.take_hi(act, b - 1, 0)
                    if not last:
                        project(b + 1, 1 - p)
                    if not first:
                        gate.take_rows(act, b - 1)
                each_batch(act, step, head=2)
                ln.take_hi(act, B - 1, 0)
                gate.take_rows(act, B - 1)

            @block.vector
            def _(dve):
                for c in range(4):
                    cut = slice(c * D, (c + 1) * D)
                    split_weights(None, dve, raw[:, :, cut], wp[0][:, :, cut], wp[1][:, :, cut],
                                  s_w, 16, s_whi, s_wlo, c + 1)
                dve.wait_ge(s_const, 32)

                def project(b, p):
                    for u in range(3 * KT):
                        dve.wait_ge(s_hi, 3 * KT * b + u + 1)
                        if u < 2 * KT:
                            dve.wait_ge(s_square, 2 * KT * b + u + 1)
                        hi, lo = ((qk[p][0][u], qk[p][1][u]) if u < 2 * KT else
                                  (fv[0][u - 2 * KT], fv[1][u - 2 * KT]))
                        dve.scalar_tensor_tensor(out=lo[:, :], in0=unit_bank[u % 2][:, :], scalar=bias_sb[:, u:u + 1],
                                                 in1=hi[:, :].bitcast(F32), op0=ALU.add,
                                                 op1=ALU.subtract).then_inc(s_lo, 1)
                    dve.wait_ge(s_made, UN * b + 7)
                    dve.tensor_copy(q_norm[:, :], unit_bank[0][:, :]).then_inc(s_q_norm, 1)
                    dve.wait_ge(s_made, UN * b + 8)
                    dve.tensor_copy(k_norm_row[:, :], unit_bank[1][:, :]).then_inc(s_k_row, 1)
                    dve.wait_ge(s_k_turned, b + 1)
                    dve.tensor_scalar(k_norm[p][:, :], out_bank[1][:, 0:2 * TT:2], -1.0, None,
                                      ALU.mult).then_inc(s_k_norm, 1)
                    for i in range(2):
                        dve.wait_ge(s_made, UN * b + 9 + i)
                        dve.tensor_copy(vw[p][:, 2 * i:2 * i + 2, 0:D],
                                        unit_bank[i][:, :].rearrange("p (t d) -> p t d", d=D)).then_inc(s_vw, 1)

                project(0, 0)

                def step(b, p, half, first, last):
                    if not first:
                        ln.normalise(dve, b - 1)
                    dve.wait_ge(s_q_norm, b + 1)
                    for t in range(TT):
                        dve.wait_ge(s_score, TT * b + t + 1)
                        dve.scalar_tensor_tensor(out=probs[:, t, :], in0=score_bank[t % 2][:, :], scalar=2.0,
                                                 in1=q_norm[:, :], op0=ALU.mult,
                                                 op1=ALU.subtract).then_inc(s_exponent, 1)
                    if not first:
                        ln.take_lo(dve, b - 1, 0)
                    if not last:
                        project(b + 1, 1 - p)
                    dve.wait_ge(s_biased, b + 1)
                    for j in range(TT):
                        dve.wait_ge(s_out, TT * b + j + 1)
                        dve.reciprocal(recip[:, j:j + 1], out_bank[j % 2][:, D:D + 1]).then_inc(s_recip, 1)
                        dve.wait_ge(s_recip, TT * b + j + 1)
                        dve.scalar_tensor_tensor(out=sh.x[:, TT * b + j, :], in0=out_bank[j % 2][:, 0:D],
                                                 scalar=recip[:, j:j + 1], in1=sh.x[:, TT * b + j, :],
                                                 op0=ALU.mult, op1=ALU.add).then_inc(s_added, 1)
                    ln.moments(dve, b, (s_added, TT * b + TT))
                    if not first:
                        gate.keep(dve, b - 1)
                each_batch(dve, step, head=2)
                ln.normalise(dve, B - 1)
                ln.take_lo(dve, B - 1, 0)
                gate.keep(dve, B - 1)

            @block.tensor
            def _(pe):
                def three_pass(out, weight, moving):
                    for i, (wi, xi) in enumerate(PASSES):
                        for k in range(KT):
                            mm = pe.matmul(out, weight(wi, k), moving(xi, k), start=(i == 0 and k == 0),
                                           stop=(i == 2 and k == KT - 1))
                    return mm

                def project(b, p):
                    for u in range(3 * KT):
                        if u < 2:
                            if not is_first(b):
                                pe.wait_ge(s_vw, 2 * b - 1 + u)
                        else:
                            pe.wait_ge(s_lo, 3 * KT * b + u - 1)
                            pe.wait_ge(s_square, 2 * KT * b + u - 1)
                        three_pass(unit_bank[u % 2][:, :], lambda i, k: wp[i][:, k, u * P:(u + 1) * P],
                                   lambda i, k: sh.xt[:, i, k, bass.ds(S * b, S)]).then_inc(s_made, 1)
                    for n in range(2):
                        pe.wait_ge(s_lo, 3 * KT * b + 2 * KT + n + 1)
                        for k in range(KT):
                            mm = pe.matmul(unit_bank[n][:, :], ones[:, :], square[KT * n + k][:, :],
                                           start=(k == 0), stop=(k == KT - 1))
                        mm.then_inc(s_made, 1)
                    for j in range(TT):
                        if j == 0:
                            pe.wait_ge(s_q_norm, b + 1)
                        if j == 2:
                            pe.wait_ge(s_k_row, b + 1)
                        mm = three_pass(unit_bank[j // 2][:, (j % 2) * D:(j % 2 + 1) * D],
                                        lambda i, k: fv[i][k][:, j * P:(j + 1) * P],
                                        lambda i, k: wp[i][:, k, 3 * D:4 * D])
                        if j % 2:
                            mm.then_inc(s_made, 1)
                        if j == 1:
                            pe.wait_ge(s_k_row, b + 1)
                            if not is_first(b):
                                wait_apart(pe, s_added, TT * b - TT)
                            for t in range(TT):
                                mm = pe.transpose(out_bank[1][:, 2 * t:2 * t + 2],
                                                  k_norm_row[0:2, t * P:(t + 1) * P], sh.ident[0:2, 0:2])
                            mm.then_inc(s_k_turned, 1)

                pe.wait_ge(s_wlo, 4)
                pe.wait_ge(s_ones, 3)
                project(0, 0)

                def step(b, p, half, first, last):
                    pe.wait_ge(s_lo, 3 * KT * b + 2 * KT)
                    if not first and not (isinstance(b, int) and b == 1):
                        pe.wait_ge(gate.s_rows, b - 1)
                        pe.wait_ge(gate.s_kept, b - 1)
                    for t in range(TT):
                        if not (first and t < 2):
                            pe.wait_ge(s_exponent, TT * b + t - 1)
                        three_pass(score_bank[t % 2][:, :], lambda i, k: qk[p][i][KT + k][:, t * P:(t + 1) * P],
                                   lambda i, k: qk[p][i][k][:, :]).then_inc(s_score, 1)
                    if not first:
                        ln.turn(pe, b - 1)
                    if not last:
                        project(b + 1, 1 - p)
                    if not first:
                        pe.wait_ge(ln.s_lo, KT * b)
                        pe.wait_ge(s_exponent, TT * b + TT)
                        gate.multiply(pe, b - 1)
                    pe.wait_ge(s_probs, TT * b + TT)
                    pe.wait_ge(s_vw, 2 * b + 2)
                    pe.wait_ge(s_k_norm, (b + 1 if last else b + 2))
                    for j in range(TT):
                        if not (first and j < 2):
                            pe.wait_ge(s_added, TT * b + j - 1)
                        for t in range(TT):
                            mm = pe.matmul(out_bank[j % 2][:, 0:VC], probs[:, t, j * P:(j + 1) * P], vw[p][:, t, :],
                                           start=(t == 0), stop=(t == TT - 1))
                        mm.then_inc(s_out, 1)
                    if not first:
                        gate.turn(pe, b - 1)
                each_batch(pe, step, head=2)
                ln.turn(pe, B - 1)
                pe.wait_ge(ln.s_lo, KT * B)
                gate.multiply(pe, B - 1)
                gate.turn(pe, B - 1)


def hybrid_layer(nc, x, w_qkv, b_qk, b_v, conv_w, conv_b, out_w, out_b, dist_w, dist_b, dist_bo, gate_w, gate_b,
                 expert_w, expert_b, out):
    with ExitStack() as ctx:
        sh = Shared(nc, ctx)
        context = ctx.enter_context(nc.sbuf_tensor("context", [P, GROUPS, TT, GR], F32))
        project_qkv(nc, sh, x, w_qkv, b_qk, b_v, expert_w)
        attention(nc, sh, "attn1", sh.q_parts, sh.k_parts, sh.v_ones, context)
        convolve(nc, sh, context, conv_w, conv_b)
        attention(nc, sh, "attn2", sh.q2_parts, sh.k_parts, sh.v_ones, context)
        sh.after_attention(ctx)
        project_out(nc, sh, context, out_w, out_b, gate_w, gate_b)
        mix_experts(nc, sh, "ffn1", expert_b, None)
        sh.recycle_semaphores()
        distance_attention(nc, sh, dist_w, dist_b, dist_bo,
                           context[:, :, :, :].rearrange("p g t c -> p (g t c)"))
        mix_experts(nc, sh, "ffn2", expert_b, out)


def laid_out(i):
    import numpy as np

    def channels(a):
        return np.ascontiguousarray(a.reshape(NG, GH, HD, -1).transpose(0, 2, 1, 3)).reshape(a.shape)

    def by_partition(a):
        return np.ascontiguousarray(a.reshape(-1, P).T)

    w, b = i["L0_attn_a_Wqkv_w"], i["L0_attn_a_Wqkv_b"]
    return {
        "x": i["L0_attn_a_x"],
        "w_qkv": np.ascontiguousarray(np.concatenate([channels(w[:D]), channels(w[D:2 * D]), w[2 * D:]]).T),
        "b_qk": by_partition(np.concatenate([channels(b[:D]), channels(b[D:2 * D])])),
        "b_v": b[2 * D:],
        "conv_w": np.ascontiguousarray(channels(i["L0_attn_a_conv_w"]).transpose(1, 2, 0)).reshape(D, 3 * D),
        "conv_b": by_partition(channels(i["L0_attn_a_conv_b"])),
        "out_w": i["L0_attn_a_out_w"].T,
        "out_b": i["L0_attn_a_out_b"],
        "dist_w": np.concatenate([i["L0_attn_b_W" + n] for n in "qkvo"], axis=1),
        "dist_b": by_partition(np.concatenate([i["L0_attn_b_b" + n] for n in "qkv"])),
        "dist_bo": i["L0_attn_b_bo"],
        "gate_w": i["L0_ffn_gate_w"].T,
        "gate_b": i["L0_ffn_gate_b"].reshape(NE, 1),
        "expert_w": i["L0_ffn_expert_w"].transpose(2, 0, 1),
        "expert_b": np.ascontiguousarray(i["L0_ffn_expert_b"].reshape(NE, KT, P).transpose(2, 1, 0)),
    }


def kernel(**inputs):
    import numpy as np
    import concourse.bacc as bacc
    from concourse.bass_utils import run_bass_kernel_spmd

    nc = bacc.Bacc("TRN2", target_bir_lowering=False, num_devices=1)
    arrays, args = {}, []
    for name, a in laid_out({n: np.asarray(a) for n, a in inputs.items()}).items():
        arrays[name] = np.ascontiguousarray(a)
        args.append(nc.dram_tensor(name, a.shape, F32, kind="ExternalInput").ap())
    out = nc.dram_tensor("out", (B, S, D), F32, kind="ExternalOutput").ap()
    hybrid_layer(nc, *args, out)
    return run_bass_kernel_spmd(nc, [arrays], core_ids=[0]).results[0]["out"]
```

```python
from contextlib import ExitStack

import concourse.bass as bass
from concourse import mybir

ALU = mybir.AluOpType
ACT = mybir.ActivationFunctionType
AX = mybir.AxisListType
F32 = mybir.dt.float32
F32R = mybir.dt.float32r
BF16 = mybir.dt.bfloat16

P = 128
B, S, D = 8, 512, 256
KT = D // P
TT = S // P
H, HD = 16, 16
GH = 4
NG = H // GH
GROUPS = B * NG
GR = GH * HD
NE, TOP_K = 8, 2
EPS = 1e-5
SCALE = HD ** -0.5
NEG = -1e30
SPLITS = 3
ROWS = 6 * HD
RUNS = ((0, (0, 3), (0, 3)), (3, (0, 2), (1, 3)), (5, (0, 1), (2, 3)))
PASSES = ((0, 0), (0, 1), (1, 0))


def each_batch(eng, step, head=1):
    for b in range(head):
        step(b, b % 2, b // 2, b == 0, False)
    with eng.Fori(0, (B - 2 * head) // 2) as t:
        for j in range(head, head + 2):
            step(2 * t + j, j % 2, t + j // 2, False, False)
    for b in range(B - head, B):
        step(b, b % 2, b // 2, False, b == B - 1)


def is_first(b):
    return isinstance(b, int) and b == 0


def is_early(b):
    return isinstance(b, int) and b < 2


def is_late(b):
    return isinstance(b, int) and b >= B - 2


def wait_apart(eng, sem, value):
    eng.wait_ge(sem, value)
    eng.nop(nofuse=True)


class Shared:

    def __init__(self, nc, ctx):
        self.nc, self.used = nc, []
        self.x = ctx.enter_context(nc.sbuf_tensor("x_res", [P, B * TT, D], F32))
        self.ident = ctx.enter_context(nc.sbuf_tensor("ident", [P, P], F32))
        self.ident_bf = ctx.enter_context(nc.sbuf_tensor("ident_bf", [P, P], BF16))
        self.causal_neg = ctx.enter_context(nc.sbuf_tensor("causal_neg", [P, P], BF16))
        self.causal_neg_t = ctx.enter_context(nc.sbuf_tensor("causal_neg_t", [P, P], BF16))
        self.minus_half = ctx.enter_context(nc.sbuf_tensor("minus_half", [P, TT], F32))
        self.psum = [ctx.enter_context(nc.psum_tensor(f"bank{i}", [P, 512], F32)) for i in range(8)]
        self.experts = ctx.enter_context(nc.sbuf_tensor("experts", [P, KT, NE, D], F32))
        self.s_experts = ctx.enter_context(nc.semaphore("experts_in"))
        self.q_parts, self.k_parts, self.q2_parts = [
            nc.dram_tensor(n, [B * KT, SPLITS, P, S], BF16, kind="Internal").ap() for n in ("q_parts", "k_parts", "q2_parts")]
        self.v_ones = nc.dram_tensor("v_ones", [B, P, TT, H * 32], F32, kind="Internal").ap()

    def semaphore(self, name):
        self.used.append(self.nc.alloc_semaphore(name))
        return self.used[-1]

    def recycle_semaphores(self):
        self.nc.clear_and_free_semaphores(self.used)
        self.nc.all_engine_barrier()
        self.used = []

    def after_attention(self, ctx):
        sb = lambda n, s, d=F32: ctx.enter_context(self.nc.sbuf_tensor(f"{n}_sb", s, d))
        self.xt = sb("xt", [P, 2, KT, B * S], F32R)
        self.gate_w = [sb(f"gate_w{i}", [P, KT, P], F32R) for i in range(2)]
        self.gate_b = sb("gate_b", [NE, 1])
        self.gates = sb("gates", [P, B * TT, NE])

    def xt_part(self, i):
        return lambda b, p, k: self.xt[:, i, k, bass.ds(S * b, S)]


class Turned:

    def __init__(self, nc, ctx, sh, name, banks, hi, lo, pieces, tokens=None):
        self.sb = lambda n, s, d=F32: ctx.enter_context(nc.sbuf_tensor(f"{name}_{n}", s, d))
        self.sem = lambda n: sh.semaphore(f"{name}_{n}")
        self.sh, self.banks, self.hi, self.lo, self.pieces = sh, banks, hi, lo, pieces
        self.tokens = self.sb("tokens", [P, TT, D]) if tokens is None else tokens
        self.s_tokens, self.s_turned = self.sem("tokens"), self.sem("turned")
        self.s_hi, self.s_lo = self.sem("hi"), self.sem("lo")

    def turn(self, pe, b):
        pe.wait_ge(self.s_tokens, self.pieces * (b + 1))
        if not is_first(b):
            pe.wait_ge(self.s_lo, KT * b)
        for k in range(KT):
            for j in range(TT):
                mm = pe.transpose(self.banks[k][:, j * P:(j + 1) * P], self.tokens[:, j, k * P:(k + 1) * P],
                                  self.sh.ident[:, :])
            mm.then_inc(self.s_turned, 1)

    def take_hi(self, act, b, p):
        for k in range(KT):
            act.wait_ge(self.s_turned, KT * b + k + 1)
            act.copy(self.hi(b, p, k), self.banks[k][:, :]).then_inc(self.s_hi, 1)

    def take_lo(self, dve, b, p):
        for k in range(KT):
            dve.wait_ge(self.s_hi, KT * b + k + 1)
            dve.tensor_tensor(self.lo(b, p, k), self.banks[k][:, :], self.hi(b, p, k).bitcast(F32),
                              ALU.subtract).then_inc(self.s_lo, 1)


class LayerNorm(Turned):

    def __init__(self, nc, ctx, sh, name, banks, hi, lo, tokens=None):
        super().__init__(nc, ctx, sh, name, banks, hi, lo, TT, tokens)
        self.stats, self.mv = self.sb("stats", [P, TT, 6]), self.sb("mv", [P, TT, 2])
        self.rstd, self.var_eps = self.sb("rstd", [P, TT]), self.sb("var_eps", [P, TT])
        self.s_stats, self.s_mean = self.sem("stats"), self.sem("mean")
        self.s_var, self.s_rstd = self.sem("var"), self.sem("rstd")

    def moments(self, dve, b, written=None):
        if written is not None:
            wait_apart(dve, *written)
        for j in range(TT):
            dve.bn_stats(self.stats[:, j, :], self.sh.x[:, TT * b + j, :]).then_inc(self.s_stats, 1)
        for j in range(TT):
            wait_apart(dve, self.s_stats, TT * b + j + 1)
            dve.bn_aggr(self.mv[:, j, :], self.stats[:, j, :]).then_inc(self.s_mean, 1)

    def deviation(self, pool, b):
        if not is_first(b):
            pool.wait_ge(self.s_tokens, TT * b)
        wait_apart(pool, self.s_mean, TT * b + TT)
        pool.tensor_scalar(self.var_eps[:, :], self.mv[:, :, 1], EPS, None, ALU.add).then_inc(self.s_var, 1)
        pool.wait_ge(self.s_var, b + 1)
        pool.tensor_tensor(self.rstd[:, :], self.var_eps[:, :], self.sh.minus_half[:, :], ALU.pow).then_inc(self.s_rstd, 1)

    def normalise(self, dve, b):
        dve.wait_ge(self.s_rstd, b + 1)
        if not is_first(b):
            dve.wait_ge(self.s_turned, KT * b)
        for j in range(TT):
            dve.tensor_scalar(self.tokens[:, j, :], self.sh.x[:, TT * b + j, :], self.mv[:, j, 0:1],
                              self.rstd[:, j:j + 1], ALU.subtract, ALU.mult).then_inc(self.s_tokens, 1)


class SplitOut:

    def __init__(self, nc, ctx, sh, name, banks, bias, dest, units):
        sb = lambda n, s, d=F32: ctx.enter_context(nc.sbuf_tensor(f"{name}_{n}", s, d))
        sem = lambda n: sh.semaphore(f"{name}_{n}")
        self.banks, self.bias, self.dest, self.units = banks, bias, dest, units
        self.t, self.rest = [sb(f"t{i}", [P, S]) for i in range(2)], [sb(f"rest{i}", [P, S]) for i in range(2)]
        self.parts = [sb(f"parts{i}", [P, SPLITS, S], BF16) for i in range(units)]
        self.s_made, self.s_t, self.s_p0, self.s_rest = sem("made"), sem("t"), sem("p0"), sem("rest")
        self.s_p1, self.s_p2 = sem("p1"), sem("p2")
        self.s_stored = [sem(f"stored{i}") for i in range(units)]

    def slot(self, u, part):
        return SPLITS - 1 - part if self.dest[u][2] else part

    def bias_and_first(self, act, b, u):
        n = self.units * b + u
        act.wait_ge(self.s_made, n + 1)
        if not (is_first(b) and u < 2):
            act.wait_ge(self.s_rest, n - 1)
        act.activation(self.t[u % 2][:, :], self.banks[u][:, :], ACT.Identity,
                       bias=self.bias[:, u:u + 1]).then_inc(self.s_t, 1)
        act.wait_ge(self.s_t, n + 1)
        if not is_first(b):
            act.wait_ge(self.s_stored[u], 16 * b)
        act.copy(self.parts[u][:, self.slot(u, 0), :], self.t[u % 2][:, :]).then_inc(self.s_p0, 1)

    def second(self, dve, b, u):
        n = self.units * b + u
        dve.wait_ge(self.s_p0, n + 1)
        if not (is_first(b) and u < 2):
            dve.wait_ge(self.s_p2, n - 1)
        dve.tensor_tensor(self.rest[u % 2][:, :], self.t[u % 2][:, :], self.parts[u][:, self.slot(u, 0), :],
                          ALU.subtract).then_inc(self.s_rest, 1)
        dve.wait_ge(self.s_rest, n + 1)
        dve.tensor_copy(self.parts[u][:, self.slot(u, 1), :], self.rest[u % 2][:, :]).then_inc(self.s_p1, 1)

    def third(self, pool, b, u):
        n = self.units * b + u
        pool.wait_ge(self.s_p1, n + 1)
        pool.tensor_tensor(self.parts[u][:, self.slot(u, 2), :], self.rest[u % 2][:, :], self.parts[u][:, self.slot(u, 1), :],
                           ALU.subtract).then_inc(self.s_p2, 1)

    def store(self, sp, b, u):
        dest, m, _ = self.dest[u]
        sp.wait_ge(self.s_p2, self.units * b + u + 1)
        sp.dma_start(dest[KT * b + m].rearrange("s p t -> p s t"), self.parts[u][:, :, :]).then_inc(self.s_stored[u], 16)

    def stores(self):
        return [(s, 16 * B) for s in self.s_stored]


def split_weights(act, dve, raw, hi, lo, s_raw, need, s_hi, s_lo, at):
    if act is not None:
        act.wait_ge(s_raw, need)
        act.copy(hi, raw).then_inc(s_hi, 1)
    if dve is not None:
        dve.wait_ge(s_hi, at)
        dve.tensor_tensor(lo, raw, hi.bitcast(F32), ALU.subtract).then_inc(s_lo, 1)


def project_qkv(nc, sh, x, w, b_qk, b_v, experts, heads):
    with ExitStack() as ctx:
        sb = lambda n, s, d=F32: ctx.enter_context(nc.sbuf_tensor(f"qkv_{n}", s, d))
        sem = lambda n: sh.semaphore(f"qkv_{n}")
        raw = sb("raw", [P, KT, 3 * D])
        wp = [sb(f"w{i}", [P, KT, 3 * D], F32R) for i in range(2)]
        bias_qk, bias_v = sb("bias_qk", [P, 2 * KT]), sb("bias_v", [P, D])
        xt = [[[sb(f"xt{p}{i}{k}", [P, S], F32R) for k in range(KT)] for i in range(2)] for p in range(2)]
        v = [sb(f"v{p}", [P, TT, H, 32]) for p in range(2)]
        s_w, s_bias, s_const, s_whi, s_wlo = sem("w"), sem("bias"), sem("const"), sem("whi"), sem("wlo")
        s_x = [sem(f"x{i}") for i in range(3)]
        s_v, s_vout, s_ones = sem("v"), sem("vout"), sem("ones")
        s_vst = [sem(f"vst{p}") for p in range(2)]
        ln = LayerNorm(nc, ctx, sh, "qkv_ln", sh.psum[0:2], lambda b, p, k: xt[p][0][k][:, :],
                       lambda b, p, k: xt[p][1][k][:, :])
        out = SplitOut(nc, ctx, sh, "qkv_out", sh.psum[2:6], bias_qk,
                       [(sh.q_parts, 0, False), (sh.q_parts, 1, False), (sh.k_parts, 0, True), (sh.k_parts, 1, True)], 2 * KT)
        vbank = sh.psum[6:8]
        CHUNKS = 3
        W = 3 * D // CHUNKS

        with nc.Block() as block:
            @block.sync
            def _(sp):
                for p in range(2):
                    sp.sem_inc(s_vst[p], 16)
                xs = x.rearrange("b (j p) d -> p (b j) d", p=P)
                sp.dma_start(sh.x[:, 0:TT, :], xs[:, 0:TT, :]).then_inc(s_x[0], 16)
                sp.dma_start(raw[:, :, :], w.rearrange("(k p) n -> p k n", p=P)).then_inc(s_w, 16)
                sp.dma_start(bias_qk[:, :], b_qk).then_inc(s_bias, 16)
                sp.dma_start(bias_v[:, :], b_v.unsqueeze(0).broadcast_to([P, D])).then_inc(s_bias, 16)
                sp.dma_start(sh.x[:, TT:2 * TT, :], xs[:, TT:2 * TT, :]).then_inc(s_x[1], 16)
                sp.dma_start(sh.x[:, 2 * TT:B * TT, :], xs[:, 2 * TT:B * TT, :]).then_inc(s_x[2], 16)
                sp.dma_start(sh.experts[:, :, :, :], experts.rearrange("(k p) e n -> p k e n", p=P)).then_inc(sh.s_experts, 16)

                def step(b, p, half, first, last):
                    for u in range(2 * KT):
                        out.store(sp, b, u)
                    sp.wait_ge(s_vout, 2 * b + 2)
                    sp.dma_start(sh.v_ones[b], v[p][:, :, :, :].rearrange("p k h c -> p k (h c)")).then_inc(s_vst[p], 16)
                    heads.load_early(sp, b, out)
                each_batch(sp, step, head=2)
                heads.stores = out.stores() + [(s, 16 * (B // 2 + 1)) for s in s_vst]

            @block.gpsimd
            def _(pool):
                pool.memset(sh.ident[:, :], 0.0).then_inc(s_const, 1)
                pool.memset(sh.ident_bf[:, :], 0.0).then_inc(s_const, 1)
                pool.memset(sh.causal_neg[:, :], 0.0).then_inc(s_const, 1)
                pool.memset(sh.causal_neg_t[:, :], 0.0).then_inc(s_const, 1)
                pool.memset(sh.minus_half[:, :], -0.5).then_inc(s_const, 1)
                for m in range(2):
                    pool.memset(v[m][:, :, :, HD:32], 1.0).then_inc(s_const, 1)
                pool.wait_ge(s_const, 7)
                for m in (sh.ident, sh.ident_bf):
                    pool.affine_select(out=m[:, :], in_=m[:, :], compare_op=ALU.not_equal, fill=1.0, base=0,
                                       pattern=[[-1, P]], channel_multiplier=1).then_inc(s_const, 1)
                pool.affine_select(out=sh.causal_neg[:, :], in_=sh.causal_neg[:, :], compare_op=ALU.is_ge,
                                   fill=NEG, base=0, pattern=[[-1, P]], channel_multiplier=1).then_inc(s_const, 1)
                pool.affine_select(out=sh.causal_neg_t[:, :], in_=sh.causal_neg_t[:, :], compare_op=ALU.is_ge,
                                   fill=NEG, base=0, pattern=[[1, P]], channel_multiplier=-1).then_inc(s_const, 1)

                ln.deviation(pool, 0)
                pool.wait_ge(ln.s_rstd, 1)
                for k in heads.k:
                    pool.memset(k[ROWS:ROWS + 2, :, :], 1.0).then_inc(s_ones, 1)
                pool.wait_ge(s_ones, RING)
                ln.deviation(pool, 1)

                def step(b, p, half, first, last):
                    for u in range(2 * KT):
                        out.third(pool, b, u)
                        if u == 1 and not is_late(b):
                            ln.deviation(pool, b + 2)
                each_batch(pool, step, head=2)

            @block.scalar
            def _(act):
                for c in range(CHUNKS):
                    split_weights(act, None, raw[:, :, c * W:(c + 1) * W], wp[0][:, :, c * W:(c + 1) * W], None,
                                  s_w, 16, s_whi, None, 0)
                ln.take_hi(act, 0, 0)
                act.wait_ge(s_bias, 32)

                def step(b, p, half, first, last):
                    for u in range(2 * KT):
                        out.bias_and_first(act, b, u)
                        if u == 1 and not last:
                            if not first:
                                act.wait_ge(s_v, 2 * b)
                            ln.take_hi(act, b + 1, 1 - p)
                each_batch(act, step)

            @block.vector
            def _(dve):
                dve.wait_ge(s_x[0], 16)
                ln.moments(dve, 0)
                ln.normalise(dve, 0)
                for c in range(CHUNKS):
                    cut = slice(c * W, (c + 1) * W)
                    split_weights(None, dve, raw[:, :, cut], wp[0][:, :, cut], wp[1][:, :, cut],
                                  s_w, 16, s_whi, s_wlo, c + 1)
                ln.take_lo(dve, 0, 0)
                dve.wait_ge(s_x[1], 16)
                ln.moments(dve, 1)
                ln.normalise(dve, 1)
                dve.wait_ge(s_bias, 32)
                dve.wait_ge(s_const, 11)

                def step(b, p, half, first, last):
                    for u in range(2 * KT):
                        out.second(dve, b, u)
                        if u == 1:
                            if not last:
                                ln.take_lo(dve, b + 1, 1 - p)
                            if not is_late(b):
                                if first:
                                    dve.wait_ge(s_x[2], 16)
                                ln.moments(dve, b + 2)
                    if not is_late(b):
                        ln.normalise(dve, b + 2)
                    dve.wait_ge(s_vst[p], 16 * (half + 1))
                    for i in range(2):
                        dve.wait_ge(s_v, 2 * b + i + 1)
                        for j in range(2):
                            ins = dve.tensor_tensor(
                                v[p][:, 2 * i + j, :, 0:HD],
                                vbank[i][:, j * D:(j + 1) * D].rearrange("p (h d) -> p h d", d=HD),
                                bias_v[:, :].rearrange("p (h d) -> p h d", d=HD), ALU.add)
                        ins.then_inc(s_vout, 1)
                each_batch(dve, step, head=2)

            @block.tensor
            def _(pe):
                pe.wait_ge(s_const, 11)
                ln.turn(pe, 0)

                def step(b, p, half, first, last):
                    pe.wait_ge(ln.s_lo, KT * b + KT)
                    for u in range(2 * KT):
                        if first:
                            pe.wait_ge(s_wlo, 2 if u >= KT else 1)
                        else:
                            pe.wait_ge(out.s_t, 2 * KT * b + u - 3)
                        for i, (wi, xi) in enumerate(PASSES):
                            for k in range(KT):
                                mm = pe.matmul(out.banks[u][:, :], wp[wi][:, k, u * P:(u + 1) * P],
                                               xt[p][xi][k][:, :], start=(i == 0 and k == 0),
                                               stop=(i == 2 and k == KT - 1))
                        mm.then_inc(out.s_made, 1)
                        if u == 1 and not last:
                            ln.turn(pe, b + 1)
                    for j in range(TT):
                        if first:
                            pe.wait_ge(s_wlo, 3)
                        elif j % 2 == 0:
                            pe.wait_ge(s_vout, 2 * b - 1 + j // 2)
                        for i, (wi, xi) in enumerate(PASSES):
                            for k in range(KT):
                                mm = pe.matmul(vbank[j // 2][:, (j % 2) * D:(j % 2 + 1) * D],
                                               xt[p][xi][k][:, j * P:(j + 1) * P], wp[wi][:, k, 2 * D:3 * D],
                                               start=(i == 0 and k == 0), stop=(i == 2 and k == KT - 1))
                        if j % 2:
                            mm.then_inc(s_v, 1)
                each_batch(pe, step)


MAX_UNITS = [[(0, 3, 0, 512)], [(1, 3, 0, 512)],
             [(0, 2, 0, 384), (0, 0, 384, 128)], [(1, 2, 0, 384), (1, 0, 384, 128)],
             [(0, 1, 0, 256), (1, 1, 256, 256)]]
EXP_UNITS = [[(0, 0, 0, 512)], [(1, 0, 0, 512)],
             [(0, 1, 0, 384), (0, 3, 384, 128)], [(1, 1, 0, 384), (1, 3, 384, 128)],
             [(0, 2, 0, 256), (1, 2, 256, 256)]]
PAIRS = GH // 2
UNITS = PAIRS * len(MAX_UNITS)
RING = NG
MAX_DIAGONAL = [slice(3, 4), slice(3, 4), slice(2, 4), slice(2, 4), slice(1, 4, 2)]
EXP_DIAGONAL = [slice(0, 1), slice(0, 1), slice(0, 4, 3), slice(0, 4, 3), slice(0, 4, 2)]


def bank_of(u):
    return u % 3 if u < UNITS - 1 else 1


BANK_BEFORE = [max(u for u in range(UNITS) if bank_of(u) == bank) - UNITS for bank in range(3)]


def unit_before(u):
    return BANK_BEFORE[u] if u < 3 else max(n for n in range(u) if bank_of(n) == bank_of(u))


def probs_at(head, kt):
    for u, segments in enumerate(EXP_UNITS):
        for h, t, c, _ in segments:
            if (h, t) == (head % 2, kt):
                return head // 2 * len(EXP_UNITS) + u, c


class HeadBuffers:

    def __init__(self, nc, ctx):
        sb = lambda n: ctx.enter_context(nc.sbuf_tensor(n, [ROWS + 2, GH, S], BF16))
        self.q, self.k = [sb(f"q{i}") for i in range(RING)], [sb(f"k{i}") for i in range(RING)]


class HeadLoads:
    EARLY = (1, B - 2)
    COUNT = 2 * len(RUNS)

    def __init__(self, sh, name, buffers, q_parts, k_parts):
        self.q, self.k, self.q_parts, self.k_parts = buffers.q, buffers.k, q_parts, k_parts
        self.s_loaded = [sh.semaphore(f"{name}_loaded{i}") for i in range(RING)]
        self.stores = []

    def wait_stores(self, eng):
        for s, value in self.stores:
            eng.wait_ge(s, value)

    def load(self, sp, b, r):
        rows = slice(r % (P // GR) * GR, (r % (P // GR) + 1) * GR)
        for dst, parts, which in ((self.k, self.k_parts, 1), (self.q, self.q_parts, 0)):
            for row, *slots in RUNS:
                a, z = slots[which]
                sp.dma_start(dst[r][HD * row:HD * (row + z - a), :, :].rearrange("r h t -> r (h t)"),
                             parts[KT * b + r // (P // GR), a:z, rows].rearrange("s (r h) t -> s r (h t)", h=GH)
                             ).then_inc(self.s_loaded[r], 16)

    def load_early(self, sp, b, out):
        if isinstance(b, int) and b in self.EARLY:
            i = self.EARLY.index(b)
            for s in out.s_stored:
                sp.wait_ge(s, 16)
            self.load(sp, 0, i)


def attention(nc, sh, name, heads, v_ones, context):
    with ExitStack() as ctx:
        sb = lambda n, s, d=F32: ctx.enter_context(nc.sbuf_tensor(f"{name}_{n}", s, d))
        sem = lambda n: sh.semaphore(f"{name}_{n}")
        ring, two = range(RING), range(2)
        q, k, s_loaded = heads.q, heads.k, heads.s_loaded
        block_max = [sb(f"block_max{i}", [P, UNITS, TT]) for i in two]
        row_max = sb("row_max", [P, GH, TT])
        shift = sb("shift", [P, 2, GH * TT], BF16)
        shift_rows = [sb(f"shift_rows{i}", [2 * GH * TT, P], BF16) for i in two]
        raw = [sb(f"raw{i}", [P, S]) for i in two]
        recip = sb("recip", [P, TT * GH])
        v = [sb(f"v{i}", [P, TT, GH * 32]) for i in ring]
        probs = [sb(f"probs{i}", [P, UNITS, S]) for i in two]
        max_bank, exp_bank, pv_bank = sh.psum[0:3], sh.psum[3:6], sh.psum[6]
        turned_bank = sh.psum[7]

        s_v = [sem(f"v{i}") for i in ring]
        s_max_made, s_max_read = sem("max_made"), sem("max_read")
        s_row_max, s_shift_hi, s_shift = sem("row_max"), sem("hi"), sem("shift")
        s_shift_turned, s_shift_rows = sem("shift_turned"), sem("shift_rows")
        s_shifted = [sem(f"shifted{i}") for i in ring]
        s_exp_made, s_exp_read = sem("exp_made"), sem("exp_read")
        s_pv, s_raw, s_ctx = sem("pv"), sem("raw"), sem("ctx")
        s_ctx_turned, s_recip = sem("ctx_turned"), sem("recip")
        def each_group(eng, step):
            step(0, 0, 0)
            with eng.Fori(0, (GROUPS - RING) // RING) as t:
                for n in range(1, RING + 1):
                    step(RING * t + n, n % RING, t + n // RING)
            for i in range(GROUPS - RING + 1, GROUPS):
                step(i, i % RING, i // RING)

        def there(i, n):
            return not isinstance(i, int) or 0 <= i + n < GROUPS

        with nc.Block() as block:
            @block.sync
            def _(sp):
                def load_v(b, r):
                    sp.dma_start(v[r][:, :, :], v_ones[b, :, :, GH * 32 * r:GH * 32 * (r + 1)]).then_inc(s_v[r], 16)

                def store_shifts(i, r):
                    sp.wait_ge(s_shift_rows, i + 1)
                    sp.dma_start(q[r][ROWS:ROWS + 2, :, :].rearrange("s h (c t) -> s (h c) t", t=P),
                                 shift_rows[r % 2][:, :]).then_inc(s_shifted[r], 16)

                heads.load(sp, 0, 2)
                store_shifts(0, 0)
                heads.load(sp, 0, 3)
                heads.wait_stores(sp)
                load_v(0, 0)

                def step(i, r, turn):
                    if there(i, 3) and not is_first(i):
                        nr = (r + 3) % RING
                        sp.wait_ge(s_exp_made, UNITS * i)
                        heads.load(sp, turn + (r + 3) // RING, nr)
                    if there(i, 1):
                        store_shifts(i + 1, (r + 1) % RING)
                        if not is_first(i):
                            sp.wait_ge(s_pv, i - 2 + 2)
                        load_v(turn + (r + 1) // RING, (r + 1) % RING)
                each_group(sp, step)

            @block.scalar
            def _(act):
                act.sem_inc(s_raw, 1)
                heads.wait_stores(act)

                def take_pv(i, r):
                    act.wait_ge(s_pv, i + 2)
                    act.copy(raw[r % 2][:, :], pv_bank[:, :]).then_inc(s_raw, 1)

                def exponentials(i, r, units):
                    for u in units:
                        act.wait_ge(s_exp_made, UNITS * i + u + 1)
                        act.activation(probs[r % 2][:, u, :], exp_bank[bank_of(u)][:, :], ACT.Exp,
                                       scale=SCALE).then_inc(s_exp_read, 1)

                def step(i, r, turn):
                    if not is_first(i):
                        act.wait_ge(s_pv, i - 2 + 2)
                    exponentials(i, r, range(6))
                    if not is_first(i):
                        take_pv(i - 1, r + 1)
                    exponentials(i, r, range(6, UNITS))
                each_group(act, step)
                take_pv(GROUPS - 1, GROUPS - 1)

            @block.vector
            def _(dve):
                def maxima(i, r, units):
                    for u in units:
                        dve.wait_ge(s_max_made, UNITS * i + u + 1)
                        dve.tensor_reduce(block_max[r % 2][:, u, :],
                                          max_bank[bank_of(u)][:, :].rearrange("p (c t) -> p c t", t=P),
                                          AX.X, ALU.max).then_inc(s_max_read, 1)

                flat = row_max[:, :, :].rearrange("p h t -> p (h t)")

                def row_maxima(i, r):
                    bm = block_max[r % 2][:, :, :].rearrange("p (g u) c -> p g u c", g=PAIRS)
                    rm = row_max[:, :, :].rearrange("p (g h) t -> p g h t", g=PAIRS)
                    dve.wait_ge(s_max_read, UNITS * (i + 1))
                    dve.tensor_reduce(rm[:, :, :, 3], bm[:, :, 0:2, :], AX.X, ALU.max, negate=True).then_inc(s_row_max, 1)
                    dve.tensor_reduce(rm[:, :, :, 2], bm[:, :, 2:4, 0:3], AX.X, ALU.max, negate=True).then_inc(s_row_max, 1)
                    dve.tensor_scalar(rm[:, :, :, 0], bm[:, :, 2:4, 3], -1.0, None, ALU.mult).then_inc(s_row_max, 1)
                    for g in range(PAIRS):
                        dve.tensor_reduce(rm[:, g, :, 1], bm[:, g, 4, :].rearrange("p (h c) -> p h c", c=2),
                                          AX.X, ALU.max, negate=True).then_inc(s_row_max, 1)

                def shift_hi(i):
                    dve.wait_ge(s_row_max, (3 + PAIRS) * (i + 1))
                    if not is_first(i):
                        dve.wait_ge(s_shift_turned, i)
                    dve.tensor_copy(shift[:, 0, :], flat).then_inc(s_shift_hi, 1)

                def shift_lo(i):
                    dve.wait_ge(s_shift_hi, i + 1)
                    dve.tensor_tensor(shift[:, 1, :], flat, shift[:, 0, :], ALU.subtract).then_inc(s_shift, 1)

                def shift_to_rows(i, r):
                    dve.wait_ge(s_shift_turned, i + 1)
                    dve.tensor_copy(shift_rows[r % 2][:, :], turned_bank[0:2 * GH * TT, 0:P // 2].bitcast(BF16)).then_inc(s_shift_rows, 1)

                heads = turned_bank[:, :].rearrange("p (n c) -> p n c", c=32)

                def invert_sums(i):
                    dve.wait_ge(s_ctx_turned, i + 1)
                    dve.reciprocal(recip[:, :], heads[:, :, HD]).then_inc(s_recip, 1)

                def normalise(i):
                    dve.wait_ge(s_recip, i + 1)
                    dve.tensor_tensor(context[:, i, :, :].rearrange("p t (h d) -> p (t h) d", d=HD),
                                      heads[:, :, 0:HD], recip[:, :].unsqueeze(2).broadcast_to([P, TT * GH, HD]),
                                      ALU.mult).then_inc(s_ctx, 1)

                dve.sem_inc(s_ctx, 1)
                maxima(0, 0, range(UNITS))
                row_maxima(0, 0)
                shift_hi(0)
                shift_lo(0)
                maxima(1, 1, range(3))
                shift_to_rows(0, 0)
                maxima(1, 1, range(3, UNITS))

                def step(i, r, turn):
                    far, near = there(i, 2), there(i, 1)
                    if far:
                        maxima(i + 2, r + 2, [0])
                    if near:
                        row_maxima(i + 1, r + 1)
                    if far:
                        maxima(i + 2, r + 2, [1])
                    if near:
                        shift_hi(i + 1)
                    if far:
                        maxima(i + 2, r + 2, [2])
                    if near:
                        shift_lo(i + 1)
                    if far:
                        maxima(i + 2, r + 2, [3, 4])
                    if near:
                        shift_to_rows(i + 1, r + 1)
                    if far:
                        maxima(i + 2, r + 2, range(5, UNITS - 1))
                    if not is_first(i):
                        invert_sums(i - 1)
                    if far:
                        maxima(i + 2, r + 2, [UNITS - 1])
                    if not is_first(i):
                        normalise(i - 1)
                each_group(dve, step)
                invert_sums(GROUPS - 1)
                normalise(GROUPS - 1)

            @block.tensor
            def _(pe):
                pe.sem_inc(s_pv, 1)

                def mask(bank, blocks, causal):
                    out = bank[:, :].rearrange("p (c t) -> p c t", t=P)[:, blocks, :]
                    return pe.matmul(out, sh.ident_bf[:, :], causal[:, :].unsqueeze(1).broadcast_to([P, out.shape[1], P]),
                                     start=False, stop=True, skip_group_check=True)

                def wait_bank(s_read, i, u):
                    if not (is_first(i) and u < len(BANK_BEFORE)):
                        pe.wait_ge(s_read, UNITS * i + unit_before(u) + 1)

                def max_unit(i, r, u):
                    wait_bank(s_max_read, i, u)
                    bank = max_bank[bank_of(u)]
                    pair, segments = u // len(MAX_UNITS), MAX_UNITS[u % len(MAX_UNITS)]
                    for h, qt, c, w in segments:
                        h += 2 * pair
                        pe.matmul(bank[:, c:c + w], q[r][0:ROWS, h, qt * P:(qt + 1) * P], k[r][0:ROWS, h, 0:w],
                                  start=(c == 0), stop=False, skip_group_check=True)
                    mask(bank, MAX_DIAGONAL[u % len(MAX_UNITS)], sh.causal_neg).then_inc(s_max_made, 1)

                def exp_unit(i, r, u):
                    wait_bank(s_exp_read, i, u)
                    bank = exp_bank[bank_of(u)]
                    pair, segments = u // len(EXP_UNITS), EXP_UNITS[u % len(EXP_UNITS)]
                    for h, kt, c, w in segments:
                        h += 2 * pair
                        pe.matmul(bank[:, c:c + w], k[r][:, h, kt * P:(kt + 1) * P], q[r][:, h, kt * P:S],
                                  start=(c == 0), stop=False, skip_group_check=True)
                    mask(bank, EXP_DIAGONAL[u % len(EXP_UNITS)], sh.causal_neg_t).then_inc(s_exp_made, 1)

                def turn_shift(i):
                    pe.wait_ge(s_shift, i + 1)
                    if not (is_first(i) or is_first(i - 1)):
                        pe.wait_ge(s_ctx, i - 1)
                    pe.transpose(turned_bank[0:2 * GH * TT, 0:P // 2].bitcast(BF16), shift[:, :, :].rearrange("p s c -> p (s c)"),
                                 sh.ident_bf[:, :]).then_inc(s_shift_turned, 1)

                def weigh(i, r, turn, kt):
                    if kt == 0:
                        pe.wait_ge(s_v[r], 16 * (turn + 1))
                        pe.wait_ge(s_exp_read, UNITS * (i + 1))
                        pe.wait_ge(s_raw, i + 1)
                    for h in range(GH):
                        u, c = probs_at(h, kt)
                        mm = pe.matmul(pv_bank[32 * h:32 * (h + 1), kt * P:S], v[r][:, kt, 32 * h:32 * (h + 1)],
                                       probs[r % 2][:, u, c:c + S - kt * P], start=(kt == 0), stop=(kt == TT - 1))
                    if kt == TT - 1:
                        mm.then_inc(s_pv, 1)

                def turn_ctx(i, r):
                    pe.wait_ge(s_raw, i + 2)
                    for t in range(TT):
                        mm = pe.transpose(turned_bank[:, t * P:(t + 1) * P], raw[r % 2][:, t * P:(t + 1) * P],
                                          sh.ident[:, :])
                    mm.then_inc(s_ctx_turned, 1)

                for i in range(2):
                    pe.wait_ge(s_loaded[i], 16 * heads.COUNT)
                    for u in range(UNITS):
                        max_unit(i, i, u)
                        if i == 1 and u == 2:
                            turn_shift(0)

                def step(i, r, turn):
                    far, near, before = there(i, 2), there(i, 1), there(i, -1) and not is_first(i)
                    pr = (r - 1) % RING
                    pt = turn - 1 if r == 0 else turn
                    if far:
                        fr = (r + 2) % RING
                        pe.wait_ge(s_loaded[fr], 16 * heads.COUNT * ((turn + 1 if fr < r else turn) + 1))
                    pe.wait_ge(s_shifted[r], 16 * (turn + 1))
                    for u in range(UNITS):
                        exp_unit(i, r, u)
                        if far:
                            max_unit(i + 2, fr, u)
                        if u == 3 and near:
                            turn_shift(i + 1)
                        if 1 <= u <= TT and before:
                            weigh(i - 1, pr, pt, u - 1)
                        if u == 7 and before:
                            if near:
                                pe.wait_ge(s_shift_rows, i + 2)
                            else:
                                pe.wait_ge(s_ctx, i)
                            turn_ctx(i - 1, pr)
                each_group(pe, step)
                last = GROUPS - 1
                for kt in range(TT):
                    weigh(last, last % RING, last // RING, kt)
                pe.wait_ge(s_ctx, GROUPS)
                turn_ctx(last, last % RING)


def stage_context(act, turned, context, b):
    if not is_first(b):
        act.wait_ge(turned.s_turned, KT * b)
    act.copy(turned.tokens[:, :, :].rearrange("p t (g c) -> p g t c", c=GR),
             context[:, bass.ds(NG * b, NG), :, :]).then_inc(turned.s_tokens, 1)


def convolve(nc, sh, context, w, bias, heads):
    TAPS = 3
    with ExitStack() as ctx:
        sb = lambda n, s, d=F32: ctx.enter_context(nc.sbuf_tensor(f"conv_{n}", s, d))
        sem = lambda n: sh.semaphore(f"conv_{n}")
        raw = sb("raw", [P, KT, TAPS * D])
        wp = [sb(f"w{i}", [P, KT, TAPS * D], F32R) for i in range(2)]
        bias_sb = sb("bias", [P, KT])
        c = [[[sb(f"c{p}{i}{k}", [P, S + 2], F32R) for k in range(KT)] for i in range(2)] for p in range(2)]
        s_w, s_bias, s_zero, s_whi, s_wlo = sem("w"), sem("bias"), sem("zero"), sem("whi"), sem("wlo")
        turned = Turned(nc, ctx, sh, "conv_in", sh.psum[0:2], lambda b, p, k: c[p][0][k][:, 1:S + 1],
                        lambda b, p, k: c[p][1][k][:, 1:S + 1], 1)
        out = SplitOut(nc, ctx, sh, "conv_out", sh.psum[2:4], bias_sb,
                       [(sh.q2_parts, 0, False), (sh.q2_parts, 1, False)], KT)

        with nc.Block() as block:
            @block.sync
            def _(sp):
                sp.dma_start(raw[:, :, :], w.rearrange("(k p) n -> p k n", p=P)).then_inc(s_w, 16)
                sp.dma_start(bias_sb[:, :], bias).then_inc(s_bias, 16)

                def step(b, p, half, first, last):
                    for u in range(KT):
                        out.store(sp, b, u)
                    heads.load_early(sp, b, out)
                each_batch(sp, step, head=2)
                heads.stores = out.stores()

            @block.gpsimd
            def _(pool):
                for p in range(2):
                    for i in range(2):
                        for k in range(KT):
                            pool.memset(c[p][i][k][:, 0:S + 2:S + 1].bitcast(F32), 0.0).then_inc(s_zero, 1)

                def step(b, p, half, first, last):
                    for u in range(KT):
                        out.third(pool, b, u)
                each_batch(pool, step)

            @block.scalar
            def _(act):
                stage_context(act, turned, context, 0)
                for t in range(TAPS):
                    split_weights(act, None, raw[:, :, t * D:(t + 1) * D], wp[0][:, :, t * D:(t + 1) * D], None,
                                  s_w, 16, s_whi, None, 0)
                turned.take_hi(act, 0, 0)
                act.wait_ge(s_bias, 16)

                def step(b, p, half, first, last):
                    if not last:
                        stage_context(act, turned, context, b + 1)
                    out.bias_and_first(act, b, 0)
                    if not last:
                        turned.take_hi(act, b + 1, 1 - p)
                    out.bias_and_first(act, b, 1)
                each_batch(act, step)

            @block.vector
            def _(dve):
                for t in range(TAPS):
                    cut = slice(t * D, (t + 1) * D)
                    split_weights(None, dve, raw[:, :, cut], wp[0][:, :, cut], wp[1][:, :, cut],
                                  s_w, 16, s_whi, s_wlo, t + 1)
                turned.take_lo(dve, 0, 0)

                def step(b, p, half, first, last):
                    out.second(dve, b, 0)
                    if not last:
                        turned.take_lo(dve, b + 1, 1 - p)
                    out.second(dve, b, 1)
                each_batch(dve, step)

            @block.tensor
            def _(pe):
                turned.turn(pe, 0)
                pe.wait_ge(s_zero, 4 * KT)

                def step(b, p, half, first, last):
                    pe.wait_ge(turned.s_lo, KT * b + KT)
                    for u in range(KT):
                        if not first:
                            pe.wait_ge(out.s_t, KT * b + u - 1)
                        for t in range(TAPS):
                            if first and u == 0:
                                pe.wait_ge(s_wlo, t + 1)
                            for i, (wi, xi) in enumerate(PASSES):
                                for k in range(KT):
                                    at = t * D + u * P
                                    mm = pe.matmul(out.banks[u][:, :], wp[wi][:, k, at:at + P],
                                                   c[p][xi][k][:, t:t + S], start=(t == 0 and i == 0 and k == 0),
                                                   stop=(t == TAPS - 1 and i == 2 and k == KT - 1))
                        mm.then_inc(out.s_made, 1)
                        if u == 0 and not last:
                            turned.turn(pe, b + 1)
                each_batch(pe, step)


class Gate:

    def __init__(self, nc, ctx, sh, name, banks):
        sb = lambda n, s, d=F32: ctx.enter_context(nc.sbuf_tensor(f"{name}_{n}", s, d))
        sem = lambda n: sh.semaphore(f"{name}_{n}")
        self.sh, self.banks, self.rows = sh, banks, sb("rows", [NE, S])
        self.s_made, self.s_rows, self.s_turned, self.s_kept = sem("made"), sem("rows"), sem("turned"), sem("kept")

    def multiply(self, pe, b):
        if not is_first(b):
            pe.wait_ge(self.s_rows, b)
        for i, (wi, xi) in enumerate(PASSES):
            for k in range(KT):
                mm = pe.matmul(self.banks[0][:, :], self.sh.gate_w[wi][:, k, :],
                               self.sh.xt[:, xi, k, bass.ds(S * b, S)], start=(i == 0 and k == 0),
                               stop=(i == 2 and k == KT - 1))
        mm.then_inc(self.s_made, 1)

    def take_rows(self, act, b):
        act.wait_ge(self.s_made, b + 1)
        if not is_first(b):
            act.wait_ge(self.s_turned, b)
        act.activation(self.rows[:, :], self.banks[0][0:NE, :], ACT.Identity,
                       bias=self.sh.gate_b[:, :]).then_inc(self.s_rows, 1)

    def turn(self, pe, b):
        if not is_first(b):
            pe.wait_ge(self.s_kept, b)
        wait_apart(pe, self.s_rows, b + 1)
        for j in range(TT):
            mm = pe.transpose(self.banks[1][:, NE * j:NE * (j + 1)], self.rows[:, j * P:(j + 1) * P],
                              self.sh.ident[0:NE, 0:NE])
        mm.then_inc(self.s_turned, 1)

    def keep(self, dve, b):
        dve.wait_ge(self.s_turned, b + 1)
        dve.tensor_copy(self.sh.gates[:, bass.ds(TT * b, TT), :],
                        self.banks[1][:, 0:TT * NE].rearrange("p (t e) -> p t e", e=NE)).then_inc(self.s_kept, 1)


def project_out(nc, sh, context, w, bias, gate_w, gate_b):
    with ExitStack() as ctx:
        sb = lambda n, s, d=F32: ctx.enter_context(nc.sbuf_tensor(f"proj_{n}", s, d))
        sem = lambda n: sh.semaphore(f"proj_{n}")
        raw, gate_raw = sb("raw", [P, KT, D]), sb("gate_raw", [P, KT, P])
        wp = [sb(f"w{i}", [P, KT, D], F32R) for i in range(2)]
        bias_row = sb("bias", [P, D])
        c = [[[sb(f"c{p}{i}{k}", [P, S], F32R) for k in range(KT)] for i in range(2)] for p in range(2)]
        s_w, s_const, s_whi, s_wlo, s_pad = sem("w"), sem("const"), sem("whi"), sem("wlo"), sem("pad")
        s_gw = sem("gw")
        s_biased, s_made, s_added = sem("biased"), sem("made"), sem("added")
        turned = Turned(nc, ctx, sh, "proj_in", sh.psum[0:2], lambda b, p, k: c[p][0][k][:, :],
                        lambda b, p, k: c[p][1][k][:, :], 1)
        bank = sh.psum[2:4]
        ln = LayerNorm(nc, ctx, sh, "proj_ln", sh.psum[4:6], sh.xt_part(0), sh.xt_part(1))
        gate = Gate(nc, ctx, sh, "proj_gate", sh.psum[6:8])

        with nc.Block() as block:
            @block.sync
            def _(sp):
                sp.dma_start(raw[:, :, :], w.rearrange("(k p) n -> p k n", p=P)).then_inc(s_w, 16)
                sp.dma_start(bias_row[:, :], bias.unsqueeze(0).broadcast_to([P, D])).then_inc(s_const, 16)
                sp.dma_start(sh.gate_b[:, :], gate_b).then_inc(s_const, 16)
                sp.wait_ge(s_pad, 1)
                sp.dma_start(gate_raw[:, :, 0:NE], gate_w.rearrange("(k p) n -> p k n", p=P)).then_inc(s_gw, 16)
                sp.wait_ge(s_gw, 16)

            @block.gpsimd
            def _(pool):
                pool.memset(gate_raw[:, :, :], 0.0).then_inc(s_pad, 1)
                pool.wait_ge(s_const, 32)

                def add_bias(b):
                    row = bias_row[:, :].unsqueeze(1).broadcast_to([P, TT, D])
                    tokens = sh.x[:, bass.ds(TT * b, TT), :]
                    pool.tensor_tensor(tokens, tokens, row, ALU.add).then_inc(s_biased, 1)

                def step(b, p, half, first, last):
                    if not first:
                        ln.deviation(pool, b - 1)
                    if not last:
                        add_bias(b + 1)
                add_bias(0)
                each_batch(pool, step, head=2)
                ln.deviation(pool, B - 1)

            @block.scalar
            def _(act):
                stage_context(act, turned, context, 0)
                split_weights(act, None, raw[:, :, :], wp[0][:, :, :], None, s_w, 16, s_whi, None, 0)
                split_weights(act, None, gate_raw[:, :, :], sh.gate_w[0][:, :, :], None, s_gw, 16, s_whi, None, 0)
                turned.take_hi(act, 0, 0)
                act.wait_ge(s_const, 32)

                def step(b, p, half, first, last):
                    if not last:
                        stage_context(act, turned, context, b + 1)
                        if not first:
                            act.wait_ge(s_made, 2 * b)
                        turned.take_hi(act, b + 1, 1 - p)
                    if not is_early(b):
                        gate.take_rows(act, b - 2)
                    if not first:
                        ln.take_hi(act, b - 1, 0)
                each_batch(act, step, head=2)
                gate.take_rows(act, B - 2)
                ln.take_hi(act, B - 1, 0)
                gate.take_rows(act, B - 1)

            @block.vector
            def _(dve):
                split_weights(None, dve, raw[:, :, :], wp[0][:, :, :], wp[1][:, :, :], s_w, 16, s_whi, s_wlo, 1)
                split_weights(None, dve, gate_raw[:, :, :], sh.gate_w[0][:, :, :], sh.gate_w[1][:, :, :],
                              s_gw, 16, s_whi, s_wlo, 2)
                turned.take_lo(dve, 0, 0)

                def step(b, p, half, first, last):
                    dve.wait_ge(s_biased, b + 1)
                    for i in range(2):
                        if i == 1 and not first:
                            ln.normalise(dve, b - 1)
                        dve.wait_ge(s_made, 2 * b + i + 1)
                        tokens = sh.x[:, bass.ds(TT * b + 2 * i, 2), :]
                        dve.tensor_tensor(tokens, bank[i][:, :].rearrange("p (t d) -> p t d", d=D), tokens,
                                          ALU.add).then_inc(s_added, 1)
                    if not last:
                        turned.take_lo(dve, b + 1, 1 - p)
                    ln.moments(dve, b, (s_added, 2 * b + 2))
                    if not first:
                        ln.take_lo(dve, b - 1, 0)
                    if not is_early(b):
                        gate.keep(dve, b - 2)
                each_batch(dve, step, head=2)
                ln.normalise(dve, B - 1)
                gate.keep(dve, B - 2)
                ln.take_lo(dve, B - 1, 0)
                gate.keep(dve, B - 1)

            @block.tensor
            def _(pe):
                turned.turn(pe, 0)
                pe.wait_ge(s_wlo, 2)

                def step(b, p, half, first, last):
                    pe.wait_ge(turned.s_lo, KT * b + KT)
                    for j in range(TT):
                        if not first and j % 2 == 0:
                            pe.wait_ge(s_added, 2 * b - 1 + j // 2)
                        for i, (wi, xi) in enumerate(PASSES):
                            for k in range(KT):
                                mm = pe.matmul(bank[j // 2][:, (j % 2) * D:(j % 2 + 1) * D],
                                               c[p][xi][k][:, j * P:(j + 1) * P], wp[wi][:, k, :],
                                               start=(i == 0 and k == 0), stop=(i == 2 and k == KT - 1))
                        if j % 2:
                            mm.then_inc(s_made, 1)
                    if not last:
                        turned.turn(pe, b + 1)
                    if not is_early(b):
                        pe.wait_ge(ln.s_lo, KT * (b - 1))
                        gate.multiply(pe, b - 2)
                    if not first:
                        ln.turn(pe, b - 1)
                    if not is_early(b):
                        gate.turn(pe, b - 2)
                each_batch(pe, step, head=2)
                pe.wait_ge(ln.s_lo, KT * (B - 1))
                gate.multiply(pe, B - 2)
                gate.turn(pe, B - 2)
                ln.turn(pe, B - 1)
                pe.wait_ge(ln.s_lo, KT * B)
                gate.multiply(pe, B - 1)
                gate.turn(pe, B - 1)


def mix_experts(nc, sh, name, expert_b, out):
    TOTAL = B * S * TOP_K
    with ExitStack() as ctx:
        sb = lambda n, s, d=F32: ctx.enter_context(nc.sbuf_tensor(f"{name}_{n}", s, d))
        sem = lambda n: sh.semaphore(f"{name}_{n}")
        beats = sb("beats", [P, B * TT, NE, NE])
        rank, chosen = sb("rank", [P, B * TT, NE]), sb("chosen", [P, B * TT, NE])
        won, ones = sb("won", [P, NE]), sb("ones", [P, P])
        share = sb("share", [P, NE])
        bias_raw, floor, bias = sb("bias_raw", [P, KT, NE]), sb("floor", [P, KT, NE]), sb("bias_e", [P, KT, NE])
        bias_sum = sb("bias_sum", [P, KT])
        scaled = [sb(f"scaled{i}", [P, KT, D]) for i in range(2)]
        wp = [sb(f"w{i}", [P, KT, NE, D], F32R) for i in range(2)]
        acc = [[sb(f"acc{p}{m}", [P, S]) for m in range(KT)] for p in range(2)]
        s_bias, s_ones, s_beats, s_rank = sem("bias"), sem("ones"), sem("beats"), sem("rank")
        s_chosen, s_won, s_count = sem("chosen"), sem("won"), sem("count")
        s_share, s_floor, s_scaled, s_whi, s_wlo = sem("share"), sem("floor"), sem("scaled"), sem("whi"), sem("wlo")
        s_made, s_acc, s_back, s_added, s_stored = sem("made"), sem("acc"), sem("back"), sem("added"), sem("stored")
        unit_bank, back_bank = sh.psum[0:4], sh.psum[4:6]
        UN = NE * KT
        ln = None if out is not None else LayerNorm(nc, ctx, sh, f"{name}_ln", sh.psum[6:8], sh.xt_part(0), sh.xt_part(1))

        with nc.Block() as block:
            @block.sync
            def _(sp):
                sp.dma_start(bias_raw[:, :, :], expert_b).then_inc(s_bias, 16)
                sp.wait_ge(s_bias, 16)
                if out is not None:
                    def store(b):
                        sp.wait_ge(s_added, KT * (b + 1))
                        sp.dma_start(out[b].rearrange("(j p) d -> p j d", p=P),
                                     sh.x[:, bass.ds(TT * b, TT), :]).then_inc(s_stored, 16)

                    def step(b, p, half, first, last):
                        if not first:
                            store(b - 1)
                    each_batch(sp, step)
                    store(B - 1)
                    sp.wait_ge(s_stored, 16 * B)

            @block.gpsimd
            def _(pool):
                pool.memset(ones[:, :], 1.0).then_inc(s_ones, 1)
                pool.memset(beats[:, :, :, :], 0.0).then_inc(s_ones, 1)
                if ln is not None:
                    def step(b, p, half, first, last):
                        if not first:
                            ln.deviation(pool, b - 1)
                    each_batch(pool, step, head=2)
                    ln.deviation(pool, B - 1)

            @block.scalar
            def _(act):
                for e in range(NE):
                    act.wait_ge(s_scaled, e + 1)
                    act.copy(wp[0][:, :, e, :], scaled[e % 2][:, :, :]).then_inc(s_whi, 1)
                if ln is not None:
                    def step(b, p, half, first, last):
                        if not first:
                            ln.take_hi(act, b - 1, 0)
                    each_batch(act, step, head=2)
                    ln.take_hi(act, B - 1, 0)

            @block.vector
            def _(dve):
                dve.wait_ge(s_ones, 2)
                g = sh.gates
                for e in range(NE):
                    for lo, hi, op in ((0, e, ALU.is_ge), (e + 1, NE, ALU.is_gt)):
                        if lo < hi:
                            ins = dve.tensor_tensor(beats[:, :, e, lo:hi], g[:, :, lo:hi],
                                                    g[:, :, e:e + 1].broadcast_to([P, B * TT, hi - lo]), op)
                            ins.then_inc(s_beats, 1)
                dve.wait_ge(s_beats, 2 * NE - 2)
                dve.tensor_reduce(rank[:, :, :], beats[:, :, :, :], AX.X, ALU.add).then_inc(s_rank, 1)
                dve.wait_ge(s_rank, 1)
                dve.tensor_scalar(chosen[:, :, :], rank[:, :, :], TOP_K - 0.5, None, ALU.is_lt).then_inc(s_chosen, 1)
                dve.wait_ge(s_chosen, 1)
                dve.tensor_reduce(won[:, :], chosen[:, :, :].rearrange("p t e -> p e t"), AX.X, ALU.add).then_inc(s_won, 1)
                dve.wait_ge(s_count, 1)
                dve.tensor_scalar(share[:, :], unit_bank[0][:, 0:NE], 1.0 / TOTAL, None, ALU.mult).then_inc(s_share, 1)
                dve.wait_ge(s_share, 1)

                def scale_expert(e):
                    if e >= 2:
                        dve.wait_ge(s_wlo, e - 1)
                    dve.tensor_scalar(scaled[e % 2][:, :, :], sh.experts[:, :, e, :], share[:, e:e + 1], None,
                                      ALU.mult).then_inc(s_scaled, 1)

                def scaled_low(e):
                    dve.wait_ge(s_whi, e + 1)
                    dve.tensor_tensor(wp[1][:, :, e, :], scaled[e % 2][:, :, :], wp[0][:, :, e, :].bitcast(F32),
                                      ALU.subtract).then_inc(s_wlo, 1)

                dve.wait_ge(sh.s_experts, 16)
                scale_expert(0)
                dve.wait_ge(s_bias, 16)
                dve.tensor_tensor(bias[:, :, :], bias_raw[:, :, :],
                                  share[:, :].unsqueeze(1).broadcast_to([P, KT, NE]), ALU.mult).then_inc(s_floor, 1)
                dve.wait_ge(s_floor, 1)
                dve.tensor_scalar(floor[:, :, :], bias[:, :, :], -1.0, None, ALU.mult).then_inc(s_floor, 1)
                dve.tensor_reduce(bias_sum[:, :], bias[:, :, :], AX.X, ALU.add).then_inc(s_floor, 1)
                for e in range(1, NE):
                    scale_expert(e)
                    scaled_low(e - 1)
                scaled_low(NE - 1)
                dve.wait_ge(s_floor, 3)

                def add_expert(b, p, e):
                    for m in range(KT):
                        n = UN * b + KT * e + m
                        z = unit_bank[(KT * e + m) % 4]
                        dve.wait_ge(s_made, n + 1)
                        if e == 0:
                            dve.tensor_scalar(acc[p][m][:, :], z[:, :], floor[:, m, e:e + 1], bias_sum[:, m:m + 1],
                                              ALU.max, ALU.add).then_inc(s_acc, 1)
                        else:
                            dve.wait_ge(s_acc, n - 1)
                            dve.scalar_tensor_tensor(out=acc[p][m][:, :], in0=z[:, :], scalar=floor[:, m, e:e + 1],
                                                     in1=acc[p][m][:, :], op0=ALU.max, op1=ALU.add).then_inc(s_acc, 1)

                def add_residual(b):
                    for m in range(KT):
                        dve.wait_ge(s_back, KT * b + m + 1)
                        tokens = sh.x[:, bass.ds(TT * b, TT), m * P:(m + 1) * P]
                        dve.tensor_tensor(tokens, back_bank[m][:, :].rearrange("p (t d) -> p t d", d=P), tokens,
                                          ALU.add).then_inc(s_added, 1)

                def step(b, p, half, first, last):
                    for e in range(NE):
                        add_expert(b, p, e)
                        if not first:
                            if e == 1:
                                add_residual(b - 1)
                            if ln is not None and e == 2:
                                ln.moments(dve, b - 1, (s_added, KT * b))
                            if ln is not None and e == 4:
                                ln.normalise(dve, b - 1)
                            if ln is not None and e == 7:
                                ln.take_lo(dve, b - 1, 0)
                each_batch(dve, step, head=2)
                add_residual(B - 1)
                if ln is not None:
                    ln.moments(dve, B - 1, (s_added, KT * B))
                    ln.normalise(dve, B - 1)
                    ln.take_lo(dve, B - 1, 0)

            @block.tensor
            def _(pe):
                pe.wait_ge(s_ones, 1)
                pe.wait_ge(s_won, 1)
                pe.matmul(unit_bank[0][:, 0:NE], ones[:, :], won[:, :], start=True, stop=True).then_inc(s_count, 1)
                pe.wait_ge(s_share, 1)

                def turn_back(b, p):
                    for m in range(KT):
                        pe.wait_ge(s_acc, UN * b + UN - 1 + m)
                        if not is_first(b):
                            pe.wait_ge(s_added, KT * b - 1 + m)
                        for j in range(TT):
                            mm = pe.transpose(back_bank[m][:, j * P:(j + 1) * P], acc[p][m][:, j * P:(j + 1) * P],
                                              sh.ident[:, :])
                        mm.then_inc(s_back, 1)

                def step(b, p, half, first, last):
                    for e in range(NE):
                        if first:
                            pe.wait_ge(s_wlo, e + 1)
                        for m in range(KT):
                            u = KT * e + m
                            if not (first and u < 4):
                                pe.wait_ge(s_acc, UN * b + u - 3)
                            for i, (wi, xi) in enumerate(PASSES):
                                for k in range(KT):
                                    mm = pe.matmul(unit_bank[u % 4][:, :], wp[wi][:, k, e, m * P:(m + 1) * P],
                                                   sh.xt[:, xi, k, bass.ds(S * b, S)], start=(i == 0 and k == 0),
                                                   stop=(i == 2 and k == KT - 1))
                            mm.then_inc(s_made, 1)
                        if not first:
                            if e == 0:
                                turn_back(b - 1, 1 - p)
                            if ln is not None and e == 6:
                                ln.turn(pe, b - 1)
                each_batch(pe, step, head=2)
                turn_back(B - 1, (B - 1) % 2)
                if ln is not None:
                    ln.turn(pe, B - 1)


def distance_attention(nc, sh, w, bias, bias_o, spare):
    VC = D + 2
    UN = 10
    with ExitStack() as ctx:
        sb = lambda n, s, d=F32: ctx.enter_context(nc.sbuf_tensor(f"dist_{n}", s, d))
        sem = lambda n: sh.semaphore(f"dist_{n}")
        raw = spare[:, 0:KT * 4 * D].rearrange("p (k n) -> p k n", k=KT)
        free = [0]

        def take(columns):
            free[0] += columns
            return spare[:, free[0] - columns:free[0]]

        vw = [take(TT * VC).rearrange("p (t n) -> p t n", t=TT) for _ in range(2)]
        probs = take(TT * S).rearrange("p (t s) -> p t s", t=TT)
        squares = take(2 * KT * S)
        square = [squares[:, S * u:S * (u + 1)] for u in range(2 * KT)]
        q_norm = take(S)
        bias_row = take(D)
        wp = [sb(f"w{i}", [P, KT, 4 * D], F32R) for i in range(2)]
        bias_sb, ones = sb("bias", [P, 3 * KT]), sb("ones", [P, P])
        qk = [[[sb(f"qk{p}{i}{u}", [P, S], F32R) for u in range(2 * KT)] for i in range(2)] for p in range(2)]
        fv = [[sb(f"v{i}{u}", [P, S], F32R) for u in range(KT)] for i in range(2)]
        k_norm = [sb(f"k_norm{p}", [P, TT]) for p in range(2)]
        recip = sb("recip", [P, TT])
        unit_bank, score_bank = sh.psum[0:4], sh.psum[4:6]
        out_bank = unit_bank[2:4]
        s_w, s_const, s_ones, s_whi, s_wlo = sem("w"), sem("const"), sem("ones"), sem("whi"), sem("wlo")
        s_made, s_hi, s_square, s_lo = sem("made"), sem("hi"), sem("square"), sem("lo")
        s_q_norm, s_k_norm = sem("q_norm"), sem("k_norm")
        s_vw, s_score, s_exponent, s_kernel, s_probs = sem("vw"), sem("score"), sem("exponent"), sem("kernel"), sem("probs")
        s_out, s_recip, s_biased, s_added = sem("out"), sem("recip"), sem("biased"), sem("added")
        ln = LayerNorm(nc, ctx, sh, "dist_ln", sh.psum[6:8], sh.xt_part(0), sh.xt_part(1),
                       squares[:, 0:TT * D].rearrange("p (t d) -> p t d", t=TT))
        gate = Gate(nc, ctx, sh, "dist_gate", score_bank)

        with nc.Block() as block:
            @block.sync
            def _(sp):
                sp.dma_start(raw, w.rearrange("(k p) n -> p k n", p=P)).then_inc(s_w, 16)
                sp.dma_start(bias_sb[:, :], bias).then_inc(s_const, 16)
                sp.dma_start(bias_row[:, :], bias_o.unsqueeze(0).broadcast_to([P, D])).then_inc(s_const, 16)

            @block.gpsimd
            def _(pool):
                pool.memset(ones[:, :], 1.0).then_inc(s_ones, 1)
                pool.wait_ge(s_wlo, 4)
                for p in range(2):
                    pool.memset(vw[p][:, :, D:VC], 1.0).then_inc(s_ones, 1)
                pool.wait_ge(s_const, 32)

                def add_bias(b):
                    row = bias_row[:, :].unsqueeze(1).broadcast_to([P, TT, D])
                    tokens = sh.x[:, bass.ds(TT * b, TT), :]
                    pool.tensor_tensor(tokens, tokens, row, ALU.add).then_inc(s_biased, 1)

                def step(b, p, half, first, last):
                    if not first:
                        ln.deviation(pool, b - 1)
                    if not last:
                        add_bias(b + 1)
                add_bias(0)
                each_batch(pool, step, head=2)
                ln.deviation(pool, B - 1)

            @block.scalar
            def _(act):
                for c in range(4):
                    split_weights(act, None, raw[:, :, c * D:(c + 1) * D], wp[0][:, :, c * D:(c + 1) * D], None,
                                  s_w, 16, s_whi, None, 0)
                act.wait_ge(s_const, 32)

                def project(b, p):
                    for u in range(3 * KT):
                        act.wait_ge(s_made, UN * b + u + 1)
                        hi = (qk[p][0][u] if u < 2 * KT else fv[0][u - 2 * KT])[:, :]
                        act.activation(hi, unit_bank[u % 4][:, :], ACT.Identity,
                                       bias=bias_sb[:, u:u + 1]).then_inc(s_hi, 1)
                        if u < 2 * KT:
                            act.activation(square[u][:, :], unit_bank[u % 4][:, :], ACT.Square,
                                           bias=bias_sb[:, u:u + 1]).then_inc(s_square, 1)

                project(0, 0)

                def step(b, p, half, first, last):
                    act.wait_ge(s_k_norm, b + 1)
                    for t in range(TT):
                        act.wait_ge(s_exponent, TT * b + t + 1)
                        act.activation(probs[:, t, :], probs[:, t, :], ACT.Exp,
                                       bias=k_norm[p][:, t:t + 1]).then_inc(s_kernel, 1)
                        act.wait_ge(s_kernel, TT * b + t + 1)
                        act.activation(probs[:, t, :], probs[:, t, :], ACT.Exp).then_inc(s_probs, 1)
                    if not first:
                        ln.take_hi(act, b - 1, 0)
                    if not last:
                        project(b + 1, 1 - p)
                    if not first:
                        gate.take_rows(act, b - 1)
                each_batch(act, step, head=2)
                ln.take_hi(act, B - 1, 0)
                gate.take_rows(act, B - 1)

            @block.vector
            def _(dve):
                for c in range(4):
                    cut = slice(c * D, (c + 1) * D)
                    split_weights(None, dve, raw[:, :, cut], wp[0][:, :, cut], wp[1][:, :, cut],
                                  s_w, 16, s_whi, s_wlo, c + 1)
                dve.wait_ge(s_const, 32)

                def project(b, p):
                    for u in range(3 * KT):
                        dve.wait_ge(s_hi, 3 * KT * b + u + 1)
                        if u < 2 * KT:
                            dve.wait_ge(s_square, 2 * KT * b + u + 1)
                        hi, lo = ((qk[p][0][u], qk[p][1][u]) if u < 2 * KT else
                                  (fv[0][u - 2 * KT], fv[1][u - 2 * KT]))
                        dve.scalar_tensor_tensor(out=lo[:, :], in0=unit_bank[u % 4][:, :], scalar=bias_sb[:, u:u + 1],
                                                 in1=hi[:, :].bitcast(F32), op0=ALU.add,
                                                 op1=ALU.subtract).then_inc(s_lo, 1)
                    dve.wait_ge(s_made, UN * b + 7)
                    dve.tensor_scalar(k_norm[p][:, :], unit_bank[2][:, 0:2 * TT:2], -1.0, None,
                                      ALU.mult).then_inc(s_k_norm, 1)
                    dve.wait_ge(s_made, UN * b + 8)
                    dve.tensor_copy(q_norm[:, :], unit_bank[3][:, :]).then_inc(s_q_norm, 1)
                    for i in range(2):
                        dve.wait_ge(s_made, UN * b + 9 + i)
                        dve.tensor_copy(vw[p][:, 2 * i:2 * i + 2, 0:D],
                                        unit_bank[i][:, :].rearrange("p (t d) -> p t d", d=D)).then_inc(s_vw, 1)

                project(0, 0)

                def step(b, p, half, first, last):
                    dve.wait_ge(s_q_norm, b + 1)
                    for t in range(TT):
                        if t == 2 and not first:
                            ln.normalise(dve, b - 1)
                        dve.wait_ge(s_score, TT * b + t + 1)
                        dve.scalar_tensor_tensor(out=probs[:, t, :], in0=score_bank[t % 2][:, :], scalar=2.0,
                                                 in1=q_norm[:, :], op0=ALU.mult,
                                                 op1=ALU.subtract).then_inc(s_exponent, 1)
                    if not first:
                        ln.take_lo(dve, b - 1, 0)
                    if not last:
                        project(b + 1, 1 - p)
                    dve.wait_ge(s_biased, b + 1)
                    for j in range(TT):
                        dve.wait_ge(s_out, TT * b + j + 1)
                        dve.reciprocal(recip[:, j:j + 1], out_bank[j % 2][:, D:D + 1]).then_inc(s_recip, 1)
                        dve.wait_ge(s_recip, TT * b + j + 1)
                        dve.scalar_tensor_tensor(out=sh.x[:, TT * b + j, :], in0=out_bank[j % 2][:, 0:D],
                                                 scalar=recip[:, j:j + 1], in1=sh.x[:, TT * b + j, :],
                                                 op0=ALU.mult, op1=ALU.add).then_inc(s_added, 1)
                        if j == 2 and not first:
                            gate.keep(dve, b - 1)
                    ln.moments(dve, b, (s_added, TT * b + TT))
                each_batch(dve, step, head=2)
                ln.normalise(dve, B - 1)
                ln.take_lo(dve, B - 1, 0)
                gate.keep(dve, B - 1)

            @block.tensor
            def _(pe):
                def three_pass(out, weight, moving):
                    for i, (wi, xi) in enumerate(PASSES):
                        for k in range(KT):
                            mm = pe.matmul(out, weight(wi, k), moving(xi, k), start=(i == 0 and k == 0),
                                           stop=(i == 2 and k == KT - 1))
                    return mm

                def project(b, p):
                    for u in range(3 * KT):
                        if not is_first(b) and u < 2:
                            pe.wait_ge(s_vw, 2 * b - 1 + u)
                        if not is_early(b) and u in (2, 3):
                            pe.wait_ge(s_added, TT * (b - 1) - 3 + u)
                        if u >= 4:
                            pe.wait_ge(s_lo, 3 * KT * b + u - 3)
                        three_pass(unit_bank[u % 4][:, :], lambda i, k: wp[i][:, k, u * P:(u + 1) * P],
                                   lambda i, k: sh.xt[:, i, k, bass.ds(S * b, S)]).then_inc(s_made, 1)
                    pe.wait_ge(s_lo, 3 * KT * b + 2 * KT)
                    for t in range(TT):
                        for k in range(KT):
                            mm = pe.matmul(unit_bank[2][:, 2 * t:2 * t + 2], square[KT + k][:, t * P:(t + 1) * P],
                                           ones[:, 0:2], start=(k == 0), stop=(k == KT - 1))
                    mm.then_inc(s_made, 1)
                    for k in range(KT):
                        mm = pe.matmul(unit_bank[3][:, :], ones[:, :], square[k][:, :],
                                       start=(k == 0), stop=(k == KT - 1))
                    mm.then_inc(s_made, 1)
                    pe.wait_ge(s_lo, 3 * KT * (b + 1))
                    for j in range(TT):
                        mm = three_pass(unit_bank[j // 2][:, (j % 2) * D:(j % 2 + 1) * D],
                                        lambda i, k: fv[i][k][:, j * P:(j + 1) * P],
                                        lambda i, k: wp[i][:, k, 3 * D:4 * D])
                        if j % 2:
                            mm.then_inc(s_made, 1)

                pe.wait_ge(s_wlo, 4)
                pe.wait_ge(s_ones, 3)
                project(0, 0)

                def step(b, p, half, first, last):
                    pe.wait_ge(s_lo, 3 * KT * b + 2 * KT)
                    if not is_early(b):
                        pe.wait_ge(gate.s_rows, b - 1)
                        pe.wait_ge(gate.s_kept, b - 1)
                    for t in range(TT):
                        if not (first and t < 2):
                            pe.wait_ge(s_exponent, TT * b + t - 1)
                        three_pass(score_bank[t % 2][:, :], lambda i, k: qk[p][i][KT + k][:, t * P:(t + 1) * P],
                                   lambda i, k: qk[p][i][k][:, :]).then_inc(s_score, 1)
                    if not first:
                        ln.turn(pe, b - 1)
                    if not last:
                        project(b + 1, 1 - p)
                    if not first:
                        pe.wait_ge(ln.s_lo, KT * b)
                        pe.wait_ge(s_exponent, TT * b + TT)
                        gate.multiply(pe, b - 1)
                    pe.wait_ge(s_probs, TT * b + TT)
                    pe.wait_ge(s_vw, 2 * b + 2)
                    pe.wait_ge(s_q_norm, (b + 1 if last else b + 2))
                    for j in range(TT):
                        if j == 2 and not first:
                            gate.turn(pe, b - 1)
                        if not (first and j < 2):
                            pe.wait_ge(s_added, TT * b + j - 1)
                        for t in range(TT):
                            mm = pe.matmul(out_bank[j % 2][:, 0:VC], probs[:, t, j * P:(j + 1) * P], vw[p][:, t, :],
                                           start=(t == 0), stop=(t == TT - 1))
                        mm.then_inc(s_out, 1)
                each_batch(pe, step, head=2)
                ln.turn(pe, B - 1)
                pe.wait_ge(ln.s_lo, KT * B)
                gate.multiply(pe, B - 1)
                gate.turn(pe, B - 1)


def hybrid_layer(nc, x, w_qkv, b_qk, b_v, conv_w, conv_b, out_w, out_b, dist_w, dist_b, dist_bo, gate_w, gate_b,
                 expert_w, expert_b, out):
    with ExitStack() as ctx:
        sh = Shared(nc, ctx)
        context = ctx.enter_context(nc.sbuf_tensor("context", [P, GROUPS, TT, GR], F32))
        with ExitStack() as attention_ctx:
            buffers = HeadBuffers(nc, attention_ctx)
            heads = HeadLoads(sh, "attn1", buffers, sh.q_parts, sh.k_parts)
            project_qkv(nc, sh, x, w_qkv, b_qk, b_v, expert_w, heads)
            attention(nc, sh, "attn1", heads, sh.v_ones, context)
            heads = HeadLoads(sh, "attn2", buffers, sh.q2_parts, sh.k_parts)
            convolve(nc, sh, context, conv_w, conv_b, heads)
            attention(nc, sh, "attn2", heads, sh.v_ones, context)
        sh.after_attention(ctx)
        project_out(nc, sh, context, out_w, out_b, gate_w, gate_b)
        mix_experts(nc, sh, "ffn1", expert_b, None)
        sh.recycle_semaphores()
        distance_attention(nc, sh, dist_w, dist_b, dist_bo,
                           context[:, :, :, :].rearrange("p g t c -> p (g t c)"))
        mix_experts(nc, sh, "ffn2", expert_b, out)


def laid_out(i):
    import numpy as np

    def channels(a):
        return np.ascontiguousarray(a.reshape(NG, GH, HD, -1).transpose(0, 2, 1, 3)).reshape(a.shape)

    def by_partition(a):
        return np.ascontiguousarray(a.reshape(-1, P).T)

    w, b = i["L0_attn_a_Wqkv_w"], i["L0_attn_a_Wqkv_b"]
    return {
        "x": i["L0_attn_a_x"],
        "w_qkv": np.ascontiguousarray(np.concatenate([channels(w[:D]), channels(w[D:2 * D]), w[2 * D:]]).T),
        "b_qk": by_partition(np.concatenate([channels(b[:D]), channels(b[D:2 * D])])),
        "b_v": b[2 * D:],
        "conv_w": np.ascontiguousarray(channels(i["L0_attn_a_conv_w"]).transpose(1, 2, 0)).reshape(D, 3 * D),
        "conv_b": by_partition(channels(i["L0_attn_a_conv_b"])),
        "out_w": i["L0_attn_a_out_w"].T,
        "out_b": i["L0_attn_a_out_b"],
        "dist_w": np.concatenate([i["L0_attn_b_W" + n] for n in "qkvo"], axis=1),
        "dist_b": by_partition(np.concatenate([i["L0_attn_b_b" + n] for n in "qkv"])),
        "dist_bo": i["L0_attn_b_bo"],
        "gate_w": i["L0_ffn_gate_w"].T,
        "gate_b": i["L0_ffn_gate_b"].reshape(NE, 1),
        "expert_w": i["L0_ffn_expert_w"].transpose(2, 0, 1),
        "expert_b": np.ascontiguousarray(i["L0_ffn_expert_b"].reshape(NE, KT, P).transpose(2, 1, 0)),
    }


def kernel(**inputs):
    import numpy as np
    import concourse.bacc as bacc
    from concourse.bass_utils import run_bass_kernel_spmd

    nc = bacc.Bacc("TRN2", target_bir_lowering=False, num_devices=1)
    arrays, args = {}, []
    for name, a in laid_out({n: np.asarray(a) for n, a in inputs.items()}).items():
        arrays[name] = np.ascontiguousarray(a)
        args.append(nc.dram_tensor(name, a.shape, F32, kind="ExternalInput").ap())
    out = nc.dram_tensor("out", (B, S, D), F32, kind="ExternalOutput").ap()
    hybrid_layer(nc, *args, out)
    return run_bass_kernel_spmd(nc, [arrays], core_ids=[0]).results[0]["out"]
```

```python
from contextlib import ExitStack

import concourse.bass as bass
from concourse import mybir

ALU = mybir.AluOpType
ACT = mybir.ActivationFunctionType
AX = mybir.AxisListType
F32 = mybir.dt.float32
F32R = mybir.dt.float32r
BF16 = mybir.dt.bfloat16

P = 128
B, S, D = 8, 512, 256
KT = D // P
TT = S // P
H, HD = 16, 16
TAPS = 3
GH = 4
NG = H // GH
GROUPS = B * NG
GR = GH * HD
NE, TOP_K = 8, 2
EPS = 1e-5
SCALE = HD ** -0.5
NEG = -1e30
SPLITS = 3
ROWS = 6 * HD
RUNS = ((0, (0, 3), (0, 3)), (3, (0, 2), (1, 3)), (5, (0, 1), (2, 3)))
PASSES = ((0, 0), (0, 1), (1, 0))


def each_batch(eng, step, head=1):
    for b in range(head):
        step(b, b % 2, b // 2, b == 0, False)
    with eng.Fori(0, (B - 2 * head) // 2) as t:
        for j in range(head, head + 2):
            step(2 * t + j, j % 2, t + j // 2, False, False)
    for b in range(B - head, B):
        step(b, b % 2, b // 2, False, b == B - 1)


def is_first(b):
    return isinstance(b, int) and b == 0


def is_early(b):
    return isinstance(b, int) and b < 2


def is_late(b):
    return isinstance(b, int) and b >= B - 2


def wait_apart(eng, sem, value):
    eng.wait_ge(sem, value)
    eng.nop(nofuse=True)


class Shared:

    def __init__(self, nc, ctx):
        self.nc, self.used = nc, []
        self.x = ctx.enter_context(nc.sbuf_tensor("x_res", [P, B * TT, D], F32))
        self.ident = ctx.enter_context(nc.sbuf_tensor("ident", [P, P], F32))
        self.ident_bf = ctx.enter_context(nc.sbuf_tensor("ident_bf", [P, P], BF16))
        self.causal_neg_t = ctx.enter_context(nc.sbuf_tensor("causal_neg_t", [P, P], BF16))
        self.minus_half = ctx.enter_context(nc.sbuf_tensor("minus_half", [P, TT], F32))
        self.psum = [ctx.enter_context(nc.psum_tensor(f"bank{i}", [P, 512], F32)) for i in range(8)]
        self.experts = ctx.enter_context(nc.sbuf_tensor("experts", [P, KT, NE, D], F32))
        self.s_experts = ctx.enter_context(nc.semaphore("experts_in"))
        self.s_later_w = ctx.enter_context(nc.semaphore("later_weights_in"))
        self.s_dist_w = ctx.enter_context(nc.semaphore("dist_weights_in"))
        self.q_parts, self.k_parts, self.q2_parts = [
            nc.dram_tensor(n, [B * KT, SPLITS, P, S], BF16, kind="Internal").ap() for n in ("q_parts", "k_parts", "q2_parts")]
        self.v_ones = nc.dram_tensor("v_ones", [B, P, TT, H * 32], F32, kind="Internal").ap()

    def semaphore(self, name):
        self.used.append(self.nc.alloc_semaphore(name))
        return self.used[-1]

    def recycle_semaphores(self):
        self.nc.clear_and_free_semaphores(self.used)
        self.nc.all_engine_barrier()
        self.used = []

    def after_attention(self, ctx):
        sb = lambda n, s, d=F32: ctx.enter_context(self.nc.sbuf_tensor(f"{n}_sb", s, d))
        self.xt = sb("xt", [P, 2, KT, B * S], F32R)
        self.gate_w = [sb(f"gate_w{i}", [P, KT, P], F32R) for i in range(2)]
        self.gate_b = sb("gate_b", [NE, 1])
        self.gates = sb("gates", [P, B * TT, NE])

    def out_w(self):
        return self.experts[:, :, 0, :], self.experts[:, :, 1, 0:P]

    def xt_part(self, i):
        return lambda b, p, k: self.xt[:, i, k, bass.ds(S * b, S)]


class Turned:

    def __init__(self, nc, ctx, sh, name, banks, hi, lo, pieces, tokens=None):
        self.sb = lambda n, s, d=F32: ctx.enter_context(nc.sbuf_tensor(f"{name}_{n}", s, d))
        self.sem = lambda n: sh.semaphore(f"{name}_{n}")
        self.sh, self.banks, self.hi, self.lo, self.pieces = sh, banks, hi, lo, pieces
        self.tokens = self.sb("tokens", [P, TT, D]) if tokens is None else tokens
        self.s_tokens, self.s_turned = self.sem("tokens"), self.sem("turned")
        self.s_hi, self.s_lo = self.sem("hi"), self.sem("lo")

    def turn(self, pe, b):
        pe.wait_ge(self.s_tokens, self.pieces * (b + 1))
        if not is_first(b):
            pe.wait_ge(self.s_lo, KT * b)
        for k in range(KT):
            for j in range(TT):
                mm = pe.transpose(self.banks[k][:, j * P:(j + 1) * P], self.tokens[:, j, k * P:(k + 1) * P],
                                  self.sh.ident[:, :])
            mm.then_inc(self.s_turned, 1)

    def take_hi(self, act, b, p):
        for k in range(KT):
            act.wait_ge(self.s_turned, KT * b + k + 1)
            act.copy(self.hi(b, p, k), self.banks[k][:, :]).then_inc(self.s_hi, 1)

    def take_lo(self, dve, b, p):
        for k in range(KT):
            dve.wait_ge(self.s_hi, KT * b + k + 1)
            dve.tensor_tensor(self.lo(b, p, k), self.banks[k][:, :], self.hi(b, p, k).bitcast(F32),
                              ALU.subtract).then_inc(self.s_lo, 1)


class LayerNorm(Turned):

    def __init__(self, nc, ctx, sh, name, banks, hi, lo, tokens=None):
        super().__init__(nc, ctx, sh, name, banks, hi, lo, TT, tokens)
        self.stats, self.mv = self.sb("stats", [P, TT, 6]), self.sb("mv", [P, TT, 2])
        self.rstd, self.var_eps = self.sb("rstd", [P, TT]), self.sb("var_eps", [P, TT])
        self.s_stats, self.s_mean = self.sem("stats"), self.sem("mean")
        self.s_var, self.s_rstd = self.sem("var"), self.sem("rstd")

    def moments(self, dve, b, written=None):
        if written is not None:
            wait_apart(dve, *written)
        for j in range(TT):
            self.add_up(dve, b, j)
        self.take_moments(dve, b)

    def add_up(self, dve, b, j):
        dve.bn_stats(self.stats[:, j, :], self.sh.x[:, TT * b + j, :]).then_inc(self.s_stats, 1)

    def take_moments(self, dve, b):
        for j in range(TT):
            wait_apart(dve, self.s_stats, TT * b + j + 1)
            dve.bn_aggr(self.mv[:, j, :], self.stats[:, j, :]).then_inc(self.s_mean, 1)

    def deviation(self, pool, b):
        if not is_first(b):
            pool.wait_ge(self.s_tokens, TT * b)
        wait_apart(pool, self.s_mean, TT * b + TT)
        pool.tensor_scalar(self.var_eps[:, :], self.mv[:, :, 1], EPS, None, ALU.add).then_inc(self.s_var, 1)
        pool.wait_ge(self.s_var, b + 1)
        pool.tensor_tensor(self.rstd[:, :], self.var_eps[:, :], self.sh.minus_half[:, :], ALU.pow).then_inc(self.s_rstd, 1)

    def normalise(self, dve, b):
        dve.wait_ge(self.s_rstd, b + 1)
        if not is_first(b):
            dve.wait_ge(self.s_turned, KT * b)
        for j in range(TT):
            dve.tensor_scalar(self.tokens[:, j, :], self.sh.x[:, TT * b + j, :], self.mv[:, j, 0:1],
                              self.rstd[:, j:j + 1], ALU.subtract, ALU.mult).then_inc(self.s_tokens, 1)


class SplitOut:

    def __init__(self, nc, ctx, sh, name, banks, bias, dest, units):
        sb = lambda n, s, d=F32: ctx.enter_context(nc.sbuf_tensor(f"{name}_{n}", s, d))
        sem = lambda n: sh.semaphore(f"{name}_{n}")
        self.banks, self.bias, self.dest, self.units = banks, bias, dest, units
        self.t, self.rest = [sb(f"t{i}", [P, S]) for i in range(2)], [sb(f"rest{i}", [P, S]) for i in range(2)]
        self.parts = [sb(f"parts{i}", [P, SPLITS, S], BF16) for i in range(units)]
        self.s_made, self.s_t, self.s_p0, self.s_rest = sem("made"), sem("t"), sem("p0"), sem("rest")
        self.s_p1, self.s_p2 = sem("p1"), sem("p2")
        self.s_stored = [sem(f"stored{i}") for i in range(units)]

    def slot(self, u, part):
        return SPLITS - 1 - part if self.dest[u][2] else part

    def bias_and_first(self, act, b, u):
        n = self.units * b + u
        act.wait_ge(self.s_made, n + 1)
        if not (is_first(b) and u < 2):
            act.wait_ge(self.s_rest, n - 1)
        act.activation(self.t[u % 2][:, :], self.banks[u][:, :], ACT.Identity,
                       bias=self.bias[:, u:u + 1]).then_inc(self.s_t, 1)
        act.wait_ge(self.s_t, n + 1)
        if not is_first(b):
            act.wait_ge(self.s_stored[u], 16 * b)
        act.copy(self.parts[u][:, self.slot(u, 0), :], self.t[u % 2][:, :]).then_inc(self.s_p0, 1)

    def second(self, dve, b, u):
        n = self.units * b + u
        dve.wait_ge(self.s_p0, n + 1)
        if not (is_first(b) and u < 2):
            dve.wait_ge(self.s_p2, n - 1)
        dve.tensor_tensor(self.rest[u % 2][:, :], self.t[u % 2][:, :], self.parts[u][:, self.slot(u, 0), :],
                          ALU.subtract).then_inc(self.s_rest, 1)
        dve.wait_ge(self.s_rest, n + 1)
        dve.tensor_copy(self.parts[u][:, self.slot(u, 1), :], self.rest[u % 2][:, :]).then_inc(self.s_p1, 1)

    def third(self, pool, b, u):
        n = self.units * b + u
        pool.wait_ge(self.s_p1, n + 1)
        pool.tensor_tensor(self.parts[u][:, self.slot(u, 2), :], self.rest[u % 2][:, :], self.parts[u][:, self.slot(u, 1), :],
                           ALU.subtract).then_inc(self.s_p2, 1)

    def store(self, sp, b, u):
        dest, m, _ = self.dest[u]
        sp.wait_ge(self.s_p2, self.units * b + u + 1)
        sp.dma_start(dest[KT * b + m].rearrange("s p t -> p s t"), self.parts[u][:, :, :]).then_inc(self.s_stored[u], 16)

    def stores(self):
        return [(s, 16 * B) for s in self.s_stored]


def split_weights(act, dve, raw, hi, lo, s_raw, need, s_hi, s_lo, at):
    if act is not None:
        act.wait_ge(s_raw, need)
        act.copy(hi, raw).then_inc(s_hi, 1)
    if dve is not None:
        dve.wait_ge(s_hi, at)
        dve.tensor_tensor(lo, raw, hi.bitcast(F32), ALU.subtract).then_inc(s_lo, 1)


def project_qkv(nc, sh, x, w, b_qk, b_v, heads, conv_w, out_w, gate_w):
    with ExitStack() as ctx:
        sb = lambda n, s, d=F32: ctx.enter_context(nc.sbuf_tensor(f"qkv_{n}", s, d))
        sem = lambda n: sh.semaphore(f"qkv_{n}")
        raw = sb("raw", [P, KT, 3 * D])
        wp = [sb(f"w{i}", [P, KT, 3 * D], F32R) for i in range(2)]
        bias_qk, bias_v = sb("bias_qk", [P, 2 * KT]), sb("bias_v", [P, D])
        xt = [[[sb(f"xt{p}{i}{k}", [P, S], F32R) for k in range(KT)] for i in range(2)] for p in range(2)]
        v = [sb(f"v{p}", [P, TT, H, 32]) for p in range(2)]
        s_w, s_bias, s_const, s_whi, s_wlo = sem("w"), sem("bias"), sem("const"), sem("whi"), sem("wlo")
        s_x = [sem(f"x{i}") for i in range(3)]
        s_v, s_vout, s_ones, s_pad = sem("v"), sem("vout"), sem("ones"), sem("pad")
        s_vst = [sem(f"vst{p}") for p in range(2)]
        ln = LayerNorm(nc, ctx, sh, "qkv_ln", sh.psum[0:2], lambda b, p, k: xt[p][0][k][:, :],
                       lambda b, p, k: xt[p][1][k][:, :])
        out = SplitOut(nc, ctx, sh, "qkv_out", sh.psum[2:6], bias_qk,
                       [(sh.q_parts, 0, False), (sh.q_parts, 1, False), (sh.k_parts, 0, True), (sh.k_parts, 1, True)], 2 * KT)
        vbank = sh.psum[6:8]
        CHUNKS = 3
        W = 3 * D // CHUNKS

        with nc.Block() as block:
            @block.sync
            def _(sp):
                for p in range(2):
                    sp.sem_inc(s_vst[p], 16)
                xs = x.rearrange("b (j p) d -> p (b j) d", p=P)
                sp.dma_start(sh.x[:, 0:TT, :], xs[:, 0:TT, :]).then_inc(s_x[0], 16)
                sp.dma_start(raw[:, :, :], w.rearrange("(k p) n -> p k n", p=P)).then_inc(s_w, 16)
                sp.dma_start(bias_qk[:, :], b_qk).then_inc(s_bias, 16)
                sp.dma_start(bias_v[:, :], b_v.unsqueeze(0).broadcast_to([P, D])).then_inc(s_bias, 16)
                sp.dma_start(sh.x[:, TT:2 * TT, :], xs[:, TT:2 * TT, :]).then_inc(s_x[1], 16)
                sp.dma_start(sh.x[:, 2 * TT:B * TT, :], xs[:, 2 * TT:B * TT, :]).then_inc(s_x[2], 16)
                raw_out, raw_gate = sh.out_w()
                sp.wait_ge(s_pad, 1)
                for dst, src in ((heads.conv_w[:, :, :], conv_w), (raw_out, out_w), (raw_gate[:, :, 0:NE], gate_w)):
                    sp.dma_start(dst, src.rearrange("(k p) n -> p k n", p=P)).then_inc(sh.s_later_w, 16)

                def step(b, p, half, first, last):
                    for u in range(2 * KT):
                        out.store(sp, b, u)
                    sp.wait_ge(s_vout, 2 * b + 2)
                    sp.dma_start(sh.v_ones[b], v[p][:, :, :, :].rearrange("p k h c -> p k (h c)")).then_inc(s_vst[p], 16)
                    heads.load_early(sp, b, out)
                each_batch(sp, step, head=2)
                heads.stores = out.stores() + [(s, 16 * (B // 2 + 1)) for s in s_vst]

            @block.gpsimd
            def _(pool):
                pool.memset(sh.out_w()[1], 0.0).then_inc(s_pad, 1)
                pool.memset(sh.ident[:, :], 0.0).then_inc(s_const, 1)
                pool.memset(sh.ident_bf[:, :], 0.0).then_inc(s_const, 1)
                pool.memset(heads.causal[:, :], 0.0).then_inc(s_const, 1)
                pool.memset(sh.causal_neg_t[:, :], 0.0).then_inc(s_const, 1)
                pool.memset(sh.minus_half[:, :], -0.5).then_inc(s_const, 1)
                for m in range(2):
                    pool.memset(v[m][:, :, :, HD:32], 1.0).then_inc(s_const, 1)
                pool.wait_ge(s_const, 7)
                for m in (sh.ident, sh.ident_bf):
                    pool.affine_select(out=m[:, :], in_=m[:, :], compare_op=ALU.not_equal, fill=1.0, base=0,
                                       pattern=[[-1, P]], channel_multiplier=1).then_inc(s_const, 1)
                pool.affine_select(out=heads.causal[:, :], in_=heads.causal[:, :], compare_op=ALU.is_ge,
                                   fill=NEG, base=S - P, pattern=[[-1, S]], channel_multiplier=1).then_inc(s_const, 1)
                pool.affine_select(out=sh.causal_neg_t[:, :], in_=sh.causal_neg_t[:, :], compare_op=ALU.is_ge,
                                   fill=NEG, base=0, pattern=[[1, P]], channel_multiplier=-1).then_inc(s_const, 1)

                ln.deviation(pool, 0)
                pool.wait_ge(ln.s_rstd, 1)
                for k in heads.k:
                    pool.memset(k[ROWS:ROWS + 2, :, :], 1.0).then_inc(s_ones, 1)
                pool.wait_ge(s_ones, RING)
                ln.deviation(pool, 1)

                def step(b, p, half, first, last):
                    for u in range(2 * KT):
                        out.third(pool, b, u)
                        if u == 1 and not is_late(b):
                            ln.deviation(pool, b + 2)
                each_batch(pool, step, head=2)

            @block.scalar
            def _(act):
                for c in range(CHUNKS):
                    split_weights(act, None, raw[:, :, c * W:(c + 1) * W], wp[0][:, :, c * W:(c + 1) * W], None,
                                  s_w, 16, s_whi, None, 0)
                ln.take_hi(act, 0, 0)
                act.wait_ge(s_bias, 32)

                def step(b, p, half, first, last):
                    for u in range(2 * KT):
                        out.bias_and_first(act, b, u)
                        if u == 1 and not last:
                            if not first:
                                act.wait_ge(s_v, 2 * b)
                            ln.take_hi(act, b + 1, 1 - p)
                each_batch(act, step)

            @block.vector
            def _(dve):
                dve.wait_ge(s_x[0], 16)
                ln.moments(dve, 0)
                ln.normalise(dve, 0)
                for c in range(CHUNKS):
                    cut = slice(c * W, (c + 1) * W)
                    split_weights(None, dve, raw[:, :, cut], wp[0][:, :, cut], wp[1][:, :, cut],
                                  s_w, 16, s_whi, s_wlo, c + 1)
                ln.take_lo(dve, 0, 0)
                dve.wait_ge(s_x[1], 16)
                ln.moments(dve, 1)
                ln.normalise(dve, 1)
                dve.wait_ge(s_bias, 32)
                dve.wait_ge(s_const, 11)

                def step(b, p, half, first, last):
                    for u in range(2 * KT):
                        out.second(dve, b, u)
                        if u == 1:
                            if not last:
                                ln.take_lo(dve, b + 1, 1 - p)
                            if not is_late(b):
                                if first:
                                    dve.wait_ge(s_x[2], 16)
                                ln.moments(dve, b + 2)
                    if not is_late(b):
                        ln.normalise(dve, b + 2)
                    dve.wait_ge(s_vst[p], 16 * (half + 1))
                    for i in range(2):
                        dve.wait_ge(s_v, 2 * b + i + 1)
                        for j in range(2):
                            ins = dve.tensor_tensor(
                                v[p][:, 2 * i + j, :, 0:HD],
                                vbank[i][:, j * D:(j + 1) * D].rearrange("p (h d) -> p h d", d=HD),
                                bias_v[:, :].rearrange("p (h d) -> p h d", d=HD), ALU.add)
                        ins.then_inc(s_vout, 1)
                each_batch(dve, step, head=2)

            @block.tensor
            def _(pe):
                pe.wait_ge(s_const, 11)
                ln.turn(pe, 0)

                def step(b, p, half, first, last):
                    pe.wait_ge(ln.s_lo, KT * b + KT)
                    for u in range(2 * KT):
                        if first:
                            pe.wait_ge(s_wlo, 2 if u >= KT else 1)
                        else:
                            pe.wait_ge(out.s_t, 2 * KT * b + u - 3)
                        for i, (wi, xi) in enumerate(PASSES):
                            for k in range(KT):
                                mm = pe.matmul(out.banks[u][:, :], wp[wi][:, k, u * P:(u + 1) * P],
                                               xt[p][xi][k][:, :], start=(i == 0 and k == 0),
                                               stop=(i == 2 and k == KT - 1))
                        mm.then_inc(out.s_made, 1)
                        if u == 1 and not last:
                            ln.turn(pe, b + 1)
                    for j in range(TT):
                        if first:
                            pe.wait_ge(s_wlo, 3)
                        elif j % 2 == 0:
                            pe.wait_ge(s_vout, 2 * b - 1 + j // 2)
                        for i, (wi, xi) in enumerate(PASSES):
                            for k in range(KT):
                                mm = pe.matmul(vbank[j // 2][:, (j % 2) * D:(j % 2 + 1) * D],
                                               xt[p][xi][k][:, j * P:(j + 1) * P], wp[wi][:, k, 2 * D:3 * D],
                                               start=(i == 0 and k == 0), stop=(i == 2 and k == KT - 1))
                        if j % 2:
                            mm.then_inc(s_v, 1)
                each_batch(pe, step)


MAX_UNITS = [[(0, 3, 0, 512)], [(1, 3, 0, 512)],
             [(0, 2, 0, 384), (0, 0, 384, 128)], [(1, 2, 0, 384), (1, 0, 384, 128)],
             [(0, 1, 0, 256), (1, 1, 256, 256)]]
EXP_UNITS = [[(0, 0, 0, 512)], [(1, 0, 0, 512)],
             [(0, 1, 0, 384), (0, 3, 384, 128)], [(1, 1, 0, 384), (1, 3, 384, 128)],
             [(0, 2, 0, 256), (1, 2, 256, 256)]]
PAIRS = GH // 2
UNITS = PAIRS * len(MAX_UNITS)
WEIGH_AT = (1, 3, 5, 7)
RING = NG
EXP_DIAGONAL = [slice(0, 1), slice(0, 1), slice(0, 4, 3), slice(0, 4, 3), slice(0, 4, 2)]


def bank_of(u):
    return u % 3 if u < UNITS - 1 else 1


BANK_BEFORE = [max(u for u in range(UNITS) if bank_of(u) == bank) - UNITS for bank in range(3)]


def unit_before(u):
    return BANK_BEFORE[u] if u < 3 else max(n for n in range(u) if bank_of(n) == bank_of(u))


def probs_at(head, kt):
    for u, segments in enumerate(EXP_UNITS):
        for h, t, c, _ in segments:
            if (h, t) == (head % 2, kt):
                return head // 2 * len(EXP_UNITS) + u, c


class HeadBuffers:

    def __init__(self, nc, ctx):
        sb = lambda n: ctx.enter_context(nc.sbuf_tensor(n, [ROWS + 2, GH, S], BF16))
        self.q, self.k = [sb(f"q{i}") for i in range(RING)], [sb(f"k{i}") for i in range(RING)]
        self.causal = ctx.enter_context(nc.sbuf_tensor("causal", [P, S], F32))
        self.conv_w = ctx.enter_context(nc.sbuf_tensor("conv_w_raw", [P, KT, TAPS * D], F32))


class HeadLoads:
    EARLY = (1, B - 2)
    COUNT = 2 * len(RUNS)

    def __init__(self, sh, name, buffers, q_parts, k_parts):
        self.conv_w, self.causal = buffers.conv_w, buffers.causal
        self.q, self.k, self.q_parts, self.k_parts = buffers.q, buffers.k, q_parts, k_parts
        self.s_loaded = [sh.semaphore(f"{name}_loaded{i}") for i in range(RING)]
        self.stores = []

    def wait_stores(self, eng):
        for s, value in self.stores:
            eng.wait_ge(s, value)

    def load(self, sp, b, r):
        rows = slice(r % (P // GR) * GR, (r % (P // GR) + 1) * GR)
        for dst, parts, which in ((self.k, self.k_parts, 1), (self.q, self.q_parts, 0)):
            for row, *slots in RUNS:
                a, z = slots[which]
                sp.dma_start(dst[r][HD * row:HD * (row + z - a), :, :].rearrange("r h t -> r (h t)"),
                             parts[KT * b + r // (P // GR), a:z, rows].rearrange("s (r h) t -> s r (h t)", h=GH)
                             ).then_inc(self.s_loaded[r], 16)

    def load_early(self, sp, b, out):
        if isinstance(b, int) and b in self.EARLY:
            i = self.EARLY.index(b)
            for s in out.s_stored:
                sp.wait_ge(s, 16)
            self.load(sp, 0, i)


def attention(nc, sh, name, heads, v_ones, context):
    with ExitStack() as ctx:
        sb = lambda n, s, d=F32: ctx.enter_context(nc.sbuf_tensor(f"{name}_{n}", s, d))
        sem = lambda n: sh.semaphore(f"{name}_{n}")
        ring, two = range(RING), range(2)
        q, k, s_loaded, causal = heads.q, heads.k, heads.s_loaded, heads.causal
        row_max = [sb(f"row_max{i}", [P, GH, TT]) for i in two]
        shift = sb("shift", [P, 2, GH * TT], BF16)
        shift_rows = [sb(f"shift_rows{i}", [2 * GH * TT, P], BF16) for i in two]
        raw = [sb(f"raw{i}", [P, S]) for i in two]
        recip = sb("recip", [P, TT * GH])
        v = [sb(f"v{i}", [P, TT, GH * 32]) for i in ring]
        probs = [sb(f"probs{i}", [P, UNITS, S]) for i in two]
        max_bank, exp_bank, pv_bank = sh.psum[0:3], sh.psum[3:6], sh.psum[6]
        turned_bank = sh.psum[7]

        s_v = [sem(f"v{i}") for i in ring]
        s_max_made, s_max_read = sem("max_made"), sem("max_read")
        s_shift_hi, s_shift = sem("hi"), sem("shift")
        s_shift_turned, s_shift_rows = sem("shift_turned"), sem("shift_rows")
        s_shifted = [sem(f"shifted{i}") for i in ring]
        s_exp_made, s_exp_read = sem("exp_made"), sem("exp_read")
        s_pv, s_raw, s_ctx = sem("pv"), sem("raw"), sem("ctx")
        s_ctx_turned, s_recip = sem("ctx_turned"), sem("recip")
        def each_group(eng, step, head=2):
            for i in range(head):
                step(i, i % RING, i // RING)
            with eng.Fori(0, (GROUPS - RING) // RING) as t:
                for n in range(head, head + RING):
                    step(RING * t + n, n % RING, t + n // RING)
            for i in range(GROUPS - RING + head, GROUPS):
                step(i, i % RING, i // RING)

        def there(i, n):
            return not isinstance(i, int) or 0 <= i + n < GROUPS

        with nc.Block() as block:
            @block.sync
            def _(sp):
                def load_v(b, r):
                    sp.dma_start(v[r][:, :, :], v_ones[b, :, :, GH * 32 * r:GH * 32 * (r + 1)]).then_inc(s_v[r], 16)

                def store_shifts(i, r):
                    sp.wait_ge(s_shift_rows, i + 1)
                    sp.dma_start(q[r][ROWS:ROWS + 2, :, :].rearrange("s h (c t) -> s (h c) t", t=P),
                                 shift_rows[r % 2][:, :]).then_inc(s_shifted[r], 16)

                heads.load(sp, 0, 2)
                store_shifts(0, 0)
                heads.load(sp, 0, 3)
                heads.wait_stores(sp)
                load_v(0, 0)

                def step(i, r, turn):
                    if there(i, 3) and not is_first(i):
                        nr = (r + 3) % RING
                        sp.wait_ge(s_exp_made, UNITS * i)
                        heads.load(sp, turn + (r + 3) // RING, nr)
                    if there(i, 1):
                        store_shifts(i + 1, (r + 1) % RING)
                        if not is_first(i):
                            sp.wait_ge(s_pv, i - 2 + 2)
                        load_v(turn + (r + 1) // RING, (r + 1) % RING)
                each_group(sp, step, head=1)

            @block.scalar
            def _(act):
                act.sem_inc(s_raw, 1)
                heads.wait_stores(act)

                def take_pv(i, r):
                    act.wait_ge(s_pv, i + 2)
                    act.copy(raw[r % 2][:, :], pv_bank[:, :]).then_inc(s_raw, 1)

                def exponentials(i, r, units):
                    for u in units:
                        act.wait_ge(s_exp_made, UNITS * i + u + 1)
                        act.activation(probs[r % 2][:, u, :], exp_bank[bank_of(u)][:, :], ACT.Exp,
                                       scale=SCALE).then_inc(s_exp_read, 1)

                def step(i, r, turn):
                    if not is_first(i):
                        act.wait_ge(s_pv, i - 2 + 2)
                    exponentials(i, r, range(8))
                    if not is_first(i):
                        take_pv(i - 1, r + 1)
                    exponentials(i, r, range(8, UNITS))
                each_group(act, step)
                take_pv(GROUPS - 1, GROUPS - 1)

            @block.vector
            def _(dve):
                def maxima(i, r, units):
                    for u in units:
                        wait_apart(dve, s_max_made, UNITS * i + u + 1)
                        pair, segments = u // len(MAX_UNITS), MAX_UNITS[u % len(MAX_UNITS)]
                        for h, qt, c, w in segments:
                            h += 2 * pair
                            scores = max_bank[bank_of(u)][:, c:c + w]
                            ins = dve.tensor_tensor_reduce(scores, scores, causal[:, S - w:S], 1.0, NEG, ALU.add,
                                                           ALU.max, row_max[r % 2][:, h, qt:qt + 1])
                        ins.then_inc(s_max_read, 1)

                def shift_hi(i, r):
                    dve.wait_ge(s_max_read, UNITS * (i + 1))
                    if not is_first(i):
                        dve.wait_ge(s_shift_turned, i)
                    dve.tensor_scalar(shift[:, 0, :], row_max[r % 2][:, :, :].rearrange("p h t -> p (h t)"), -1.0, None,
                                      ALU.mult).then_inc(s_shift_hi, 1)

                def shift_lo(i, r):
                    dve.wait_ge(s_shift_hi, i + 1)
                    dve.scalar_tensor_tensor(out=shift[:, 1, :], in0=row_max[r % 2][:, :, :].rearrange("p h t -> p (h t)"),
                                             scalar=-1.0, in1=shift[:, 0, :], op0=ALU.mult,
                                             op1=ALU.subtract).then_inc(s_shift, 1)

                def shift_to_rows(i, r):
                    dve.wait_ge(s_shift_turned, i + 1)
                    dve.tensor_copy(shift_rows[r % 2][:, :], turned_bank[0:2 * GH * TT, 0:P // 2].bitcast(BF16)).then_inc(s_shift_rows, 1)

                heads = turned_bank[:, :].rearrange("p (n c) -> p n c", c=32)

                def invert_sums(i):
                    dve.wait_ge(s_ctx_turned, i + 1)
                    dve.reciprocal(recip[:, :], heads[:, :, HD]).then_inc(s_recip, 1)

                def normalise(i):
                    dve.wait_ge(s_recip, i + 1)
                    dve.tensor_tensor(context[:, i, :, :].rearrange("p t (h d) -> p (t h) d", d=HD),
                                      heads[:, :, 0:HD], recip[:, :].unsqueeze(2).broadcast_to([P, TT * GH, HD]),
                                      ALU.mult).then_inc(s_ctx, 1)

                dve.sem_inc(s_ctx, 1)
                maxima(0, 0, range(UNITS))
                shift_hi(0, 0)
                shift_lo(0, 0)
                maxima(1, 1, range(3))
                shift_to_rows(0, 0)
                maxima(1, 1, range(3, UNITS))

                def step(i, r, turn):
                    far, near = there(i, 2), there(i, 1)
                    if far:
                        maxima(i + 2, r + 2, [0])
                    if near:
                        shift_hi(i + 1, r + 1)
                    if not is_early(i):
                        invert_sums(i - 2)
                    if far:
                        maxima(i + 2, r + 2, [1])
                    if near:
                        shift_lo(i + 1, r + 1)
                    if not is_early(i):
                        normalise(i - 2)
                    if far:
                        maxima(i + 2, r + 2, range(2, 5))
                    if near:
                        shift_to_rows(i + 1, r + 1)
                    if far:
                        maxima(i + 2, r + 2, range(5, UNITS))
                each_group(dve, step)
                invert_sums(GROUPS - 2)
                normalise(GROUPS - 2)
                invert_sums(GROUPS - 1)
                normalise(GROUPS - 1)

            @block.tensor
            def _(pe):
                pe.sem_inc(s_pv, 1)

                def mask(bank, blocks):
                    out = bank[:, :].rearrange("p (c t) -> p c t", t=P)[:, blocks, :]
                    return pe.matmul(out, sh.ident_bf[:, :], sh.causal_neg_t[:, :].unsqueeze(1).broadcast_to([P, out.shape[1], P]),
                                     start=False, stop=True, skip_group_check=True)

                def wait_bank(s_read, i, u):
                    if not (is_first(i) and u < len(BANK_BEFORE)):
                        pe.wait_ge(s_read, UNITS * i + unit_before(u) + 1)

                def max_unit(i, r, u):
                    wait_bank(s_max_read, i, u)
                    bank = max_bank[bank_of(u)]
                    pair, segments = u // len(MAX_UNITS), MAX_UNITS[u % len(MAX_UNITS)]
                    for h, qt, c, w in segments:
                        h += 2 * pair
                        mm = pe.matmul(bank[:, c:c + w], q[r][0:ROWS, h, qt * P:(qt + 1) * P], k[r][0:ROWS, h, 0:w],
                                       start=(c == 0), stop=True, skip_group_check=True)
                    mm.then_inc(s_max_made, 1)

                def exp_unit(i, r, u):
                    wait_bank(s_exp_read, i, u)
                    bank = exp_bank[bank_of(u)]
                    pair, segments = u // len(EXP_UNITS), EXP_UNITS[u % len(EXP_UNITS)]
                    for h, kt, c, w in segments:
                        h += 2 * pair
                        pe.matmul(bank[:, c:c + w], k[r][:, h, kt * P:(kt + 1) * P], q[r][:, h, kt * P:S],
                                  start=(c == 0), stop=False, skip_group_check=True)
                    mask(bank, EXP_DIAGONAL[u % len(EXP_UNITS)]).then_inc(s_exp_made, 1)

                def turn_shift(i):
                    pe.wait_ge(s_shift, i + 1)
                    if not (is_first(i) or is_first(i - 1)):
                        pe.wait_ge(s_ctx, i - 1)
                    pe.transpose(turned_bank[0:2 * GH * TT, 0:P // 2].bitcast(BF16), shift[:, :, :].rearrange("p s c -> p (s c)"),
                                 sh.ident_bf[:, :]).then_inc(s_shift_turned, 1)

                def weigh(i, r, turn, kt):
                    if kt == 0:
                        pe.wait_ge(s_v[r], 16 * (turn + 1))
                        pe.wait_ge(s_exp_read, UNITS * (i + 1))
                        pe.wait_ge(s_raw, i + 1)
                    for h in range(GH):
                        u, c = probs_at(h, kt)
                        mm = pe.matmul(pv_bank[32 * h:32 * (h + 1), kt * P:S], v[r][:, kt, 32 * h:32 * (h + 1)],
                                       probs[r % 2][:, u, c:c + S - kt * P], start=(kt == 0), stop=(kt == TT - 1))
                    if kt == TT - 1:
                        mm.then_inc(s_pv, 1)

                def turn_ctx(i, r):
                    pe.wait_ge(s_raw, i + 2)
                    for t in range(TT):
                        mm = pe.transpose(turned_bank[:, t * P:(t + 1) * P], raw[r % 2][:, t * P:(t + 1) * P],
                                          sh.ident[:, :])
                    mm.then_inc(s_ctx_turned, 1)

                for i in range(2):
                    pe.wait_ge(s_loaded[i], 16 * heads.COUNT)
                    for u in range(UNITS):
                        max_unit(i, i, u)
                        if i == 1 and u == 2:
                            turn_shift(0)

                def step(i, r, turn):
                    far, near, before = there(i, 2), there(i, 1), there(i, -1) and not is_first(i)
                    pr = (r - 1) % RING
                    pt = turn - 1 if r == 0 else turn
                    if far:
                        fr = (r + 2) % RING
                        pe.wait_ge(s_loaded[fr], 16 * heads.COUNT * ((turn + 1 if fr < r else turn) + 1))
                    pe.wait_ge(s_shifted[r], 16 * (turn + 1))
                    for u in range(UNITS):
                        exp_unit(i, r, u)
                        if far:
                            max_unit(i + 2, fr, u)
                        if u == 3 and near:
                            turn_shift(i + 1)
                        if u in WEIGH_AT and before:
                            weigh(i - 1, pr, pt, WEIGH_AT.index(u))
                        if u == UNITS - 1 and before:
                            if near:
                                pe.wait_ge(s_shift_rows, i + 2)
                            else:
                                pe.wait_ge(s_ctx, i)
                            turn_ctx(i - 1, pr)
                each_group(pe, step)
                last = GROUPS - 1
                for kt in range(TT):
                    weigh(last, last % RING, last // RING, kt)
                pe.wait_ge(s_ctx, GROUPS)
                turn_ctx(last, last % RING)


def stage_context(act, turned, context, b):
    if not is_first(b):
        act.wait_ge(turned.s_turned, KT * b)
    act.copy(turned.tokens[:, :, :].rearrange("p t (g c) -> p g t c", c=GR),
             context[:, bass.ds(NG * b, NG), :, :]).then_inc(turned.s_tokens, 1)


def convolve(nc, sh, context, raw, bias, heads):
    with ExitStack() as ctx:
        sb = lambda n, s, d=F32: ctx.enter_context(nc.sbuf_tensor(f"conv_{n}", s, d))
        sem = lambda n: sh.semaphore(f"conv_{n}")
        wp = [sb(f"w{i}", [P, KT, TAPS * D], F32R) for i in range(2)]
        bias_sb = sb("bias", [P, KT])
        c = [[[sb(f"c{p}{i}{k}", [P, S + 2], F32R) for k in range(KT)] for i in range(2)] for p in range(2)]
        s_bias, s_zero, s_whi, s_wlo = sem("bias"), sem("zero"), sem("whi"), sem("wlo")
        turned = Turned(nc, ctx, sh, "conv_in", sh.psum[0:2], lambda b, p, k: c[p][0][k][:, 1:S + 1],
                        lambda b, p, k: c[p][1][k][:, 1:S + 1], 1)
        out = SplitOut(nc, ctx, sh, "conv_out", sh.psum[2:4], bias_sb,
                       [(sh.q2_parts, 0, False), (sh.q2_parts, 1, False)], KT)

        with nc.Block() as block:
            @block.sync
            def _(sp):
                sp.dma_start(bias_sb[:, :], bias).then_inc(s_bias, 16)

                def step(b, p, half, first, last):
                    for u in range(KT):
                        out.store(sp, b, u)
                    heads.load_early(sp, b, out)
                each_batch(sp, step, head=2)
                heads.stores = out.stores()

            @block.gpsimd
            def _(pool):
                for p in range(2):
                    for i in range(2):
                        for k in range(KT):
                            pool.memset(c[p][i][k][:, 0:S + 2:S + 1].bitcast(F32), 0.0).then_inc(s_zero, 1)

                def step(b, p, half, first, last):
                    for u in range(KT):
                        out.third(pool, b, u)
                each_batch(pool, step)

            @block.scalar
            def _(act):
                stage_context(act, turned, context, 0)
                for t in range(TAPS):
                    split_weights(act, None, raw[:, :, t * D:(t + 1) * D], wp[0][:, :, t * D:(t + 1) * D], None,
                                  sh.s_later_w, 48, s_whi, None, 0)
                    if t == 0:
                        turned.take_hi(act, 0, 0)
                act.wait_ge(s_bias, 16)

                def step(b, p, half, first, last):
                    if not last:
                        stage_context(act, turned, context, b + 1)
                    out.bias_and_first(act, b, 0)
                    if not last:
                        turned.take_hi(act, b + 1, 1 - p)
                    out.bias_and_first(act, b, 1)
                each_batch(act, step)

            @block.vector
            def _(dve):
                for t in range(TAPS):
                    cut = slice(t * D, (t + 1) * D)
                    split_weights(None, dve, raw[:, :, cut], wp[0][:, :, cut], wp[1][:, :, cut],
                                  sh.s_later_w, 48, s_whi, s_wlo, t + 1)
                    if t == 0:
                        turned.take_lo(dve, 0, 0)

                def step(b, p, half, first, last):
                    out.second(dve, b, 0)
                    if not last:
                        turned.take_lo(dve, b + 1, 1 - p)
                    out.second(dve, b, 1)
                each_batch(dve, step)

            @block.tensor
            def _(pe):
                turned.turn(pe, 0)
                pe.wait_ge(s_zero, 4 * KT)

                def step(b, p, half, first, last):
                    pe.wait_ge(turned.s_lo, KT * b + KT)
                    for u in range(KT):
                        if not first:
                            pe.wait_ge(out.s_t, KT * b + u - 1)
                        for t in range(TAPS):
                            if first and u == 0:
                                pe.wait_ge(s_wlo, t + 1)
                            for i, (wi, xi) in enumerate(PASSES):
                                for k in range(KT):
                                    at = t * D + u * P
                                    mm = pe.matmul(out.banks[u][:, :], wp[wi][:, k, at:at + P],
                                                   c[p][xi][k][:, t:t + S], start=(t == 0 and i == 0 and k == 0),
                                                   stop=(t == TAPS - 1 and i == 2 and k == KT - 1))
                        mm.then_inc(out.s_made, 1)
                        if u == 0 and not last:
                            turned.turn(pe, b + 1)
                each_batch(pe, step)


class Gate:

    def __init__(self, nc, ctx, sh, name, banks):
        sb = lambda n, s, d=F32: ctx.enter_context(nc.sbuf_tensor(f"{name}_{n}", s, d))
        sem = lambda n: sh.semaphore(f"{name}_{n}")
        self.sh, self.banks, self.rows = sh, banks, sb("rows", [NE, S])
        self.s_made, self.s_rows, self.s_turned, self.s_kept = sem("made"), sem("rows"), sem("turned"), sem("kept")

    def multiply(self, pe, b):
        if not is_first(b):
            pe.wait_ge(self.s_rows, b)
        for i, (wi, xi) in enumerate(PASSES):
            for k in range(KT):
                mm = pe.matmul(self.banks[0][:, :], self.sh.gate_w[wi][:, k, :],
                               self.sh.xt[:, xi, k, bass.ds(S * b, S)], start=(i == 0 and k == 0),
                               stop=(i == 2 and k == KT - 1))
        mm.then_inc(self.s_made, 1)

    def take_rows(self, act, b):
        act.wait_ge(self.s_made, b + 1)
        if not is_first(b):
            act.wait_ge(self.s_turned, b)
        act.activation(self.rows[:, :], self.banks[0][0:NE, :], ACT.Identity,
                       bias=self.sh.gate_b[:, :]).then_inc(self.s_rows, 1)

    def turn(self, pe, b):
        if not is_first(b):
            pe.wait_ge(self.s_kept, b)
        wait_apart(pe, self.s_rows, b + 1)
        for j in range(TT):
            mm = pe.transpose(self.banks[1][:, NE * j:NE * (j + 1)], self.rows[:, j * P:(j + 1) * P],
                              self.sh.ident[0:NE, 0:NE])
        mm.then_inc(self.s_turned, 1)

    def keep(self, dve, b):
        dve.wait_ge(self.s_turned, b + 1)
        dve.tensor_copy(self.sh.gates[:, bass.ds(TT * b, TT), :],
                        self.banks[1][:, 0:TT * NE].rearrange("p (t e) -> p t e", e=NE)).then_inc(self.s_kept, 1)


def project_out(nc, sh, context, bias, gate_b, experts):
    with ExitStack() as ctx:
        sb = lambda n, s, d=F32: ctx.enter_context(nc.sbuf_tensor(f"proj_{n}", s, d))
        sem = lambda n: sh.semaphore(f"proj_{n}")
        raw, gate_raw = sh.out_w()
        wp = [sb(f"w{i}", [P, KT, D], F32R) for i in range(2)]
        bias_row = sb("bias", [P, D])
        c = [[[sb(f"c{p}{i}{k}", [P, S], F32R) for k in range(KT)] for i in range(2)] for p in range(2)]
        s_const, s_whi, s_wlo = sem("const"), sem("whi"), sem("wlo")
        s_biased, s_made, s_added = sem("biased"), sem("made"), sem("added")
        turned = Turned(nc, ctx, sh, "proj_in", sh.psum[0:2], lambda b, p, k: c[p][0][k][:, :],
                        lambda b, p, k: c[p][1][k][:, :], 1)
        bank = sh.psum[2:4]
        ln = LayerNorm(nc, ctx, sh, "proj_ln", sh.psum[4:6], sh.xt_part(0), sh.xt_part(1))
        gate = Gate(nc, ctx, sh, "proj_gate", sh.psum[6:8])

        with nc.Block() as block:
            @block.sync
            def _(sp):
                sp.dma_start(bias_row[:, :], bias.unsqueeze(0).broadcast_to([P, D])).then_inc(s_const, 16)
                sp.dma_start(sh.gate_b[:, :], gate_b).then_inc(s_const, 16)
                sp.wait_ge(s_wlo, 2)
                sp.dma_start(sh.experts[:, :, :, :], experts.rearrange("(k p) e n -> p k e n", p=P)).then_inc(sh.s_experts, 16)

            @block.gpsimd
            def _(pool):
                pool.wait_ge(s_const, 32)

                def add_bias(b):
                    row = bias_row[:, :].unsqueeze(1).broadcast_to([P, TT, D])
                    tokens = sh.x[:, bass.ds(TT * b, TT), :]
                    pool.tensor_tensor(tokens, tokens, row, ALU.add).then_inc(s_biased, 1)

                def step(b, p, half, first, last):
                    if not first:
                        ln.deviation(pool, b - 1)
                    if not last:
                        add_bias(b + 1)
                add_bias(0)
                each_batch(pool, step, head=2)
                ln.deviation(pool, B - 1)

            @block.scalar
            def _(act):
                stage_context(act, turned, context, 0)
                split_weights(act, None, raw, wp[0][:, :, :], None, sh.s_later_w, 48, s_whi, None, 0)
                turned.take_hi(act, 0, 0)
                split_weights(act, None, gate_raw, sh.gate_w[0][:, :, :], None, sh.s_later_w, 48, s_whi, None, 0)
                act.wait_ge(s_const, 32)

                def step(b, p, half, first, last):
                    if not last:
                        stage_context(act, turned, context, b + 1)
                        if not first:
                            act.wait_ge(s_made, 2 * b)
                        turned.take_hi(act, b + 1, 1 - p)
                    if not is_early(b):
                        gate.take_rows(act, b - 2)
                    if not first:
                        ln.take_hi(act, b - 1, 0)
                each_batch(act, step, head=2)
                gate.take_rows(act, B - 2)
                ln.take_hi(act, B - 1, 0)
                gate.take_rows(act, B - 1)

            @block.vector
            def _(dve):
                split_weights(None, dve, raw, wp[0][:, :, :], wp[1][:, :, :], sh.s_later_w, 48, s_whi, s_wlo, 1)
                turned.take_lo(dve, 0, 0)
                split_weights(None, dve, gate_raw, sh.gate_w[0][:, :, :], sh.gate_w[1][:, :, :],
                              sh.s_later_w, 48, s_whi, s_wlo, 2)

                def step(b, p, half, first, last):
                    dve.wait_ge(s_biased, b + 1)
                    for i in range(2):
                        if i == 1 and not first:
                            ln.normalise(dve, b - 1)
                        dve.wait_ge(s_made, 2 * b + i + 1)
                        tokens = sh.x[:, bass.ds(TT * b + 2 * i, 2), :]
                        dve.tensor_tensor(tokens, bank[i][:, :].rearrange("p (t d) -> p t d", d=D), tokens,
                                          ALU.add).then_inc(s_added, 1)
                    if not last:
                        turned.take_lo(dve, b + 1, 1 - p)
                    ln.moments(dve, b, (s_added, 2 * b + 2))
                    if not first:
                        ln.take_lo(dve, b - 1, 0)
                    if not is_early(b):
                        gate.keep(dve, b - 2)
                each_batch(dve, step, head=2)
                ln.normalise(dve, B - 1)
                gate.keep(dve, B - 2)
                ln.take_lo(dve, B - 1, 0)
                gate.keep(dve, B - 1)

            @block.tensor
            def _(pe):
                turned.turn(pe, 0)
                pe.wait_ge(s_wlo, 1)

                def step(b, p, half, first, last):
                    if isinstance(b, int) and b == 1:
                        pe.wait_ge(s_wlo, 2)
                    pe.wait_ge(turned.s_lo, KT * b + KT)
                    for j in range(TT):
                        if not first and j % 2 == 0:
                            pe.wait_ge(s_added, 2 * b - 1 + j // 2)
                        for i, (wi, xi) in enumerate(PASSES):
                            for k in range(KT):
                                mm = pe.matmul(bank[j // 2][:, (j % 2) * D:(j % 2 + 1) * D],
                                               c[p][xi][k][:, j * P:(j + 1) * P], wp[wi][:, k, :],
                                               start=(i == 0 and k == 0), stop=(i == 2 and k == KT - 1))
                        if j % 2:
                            mm.then_inc(s_made, 1)
                    if not last:
                        turned.turn(pe, b + 1)
                    if not is_early(b):
                        pe.wait_ge(ln.s_lo, KT * (b - 1))
                        gate.multiply(pe, b - 2)
                    if not first:
                        ln.turn(pe, b - 1)
                    if not is_early(b):
                        gate.turn(pe, b - 2)
                each_batch(pe, step, head=2)
                pe.wait_ge(ln.s_lo, KT * (B - 1))
                gate.multiply(pe, B - 2)
                gate.turn(pe, B - 2)
                ln.turn(pe, B - 1)
                pe.wait_ge(ln.s_lo, KT * B)
                gate.multiply(pe, B - 1)
                gate.turn(pe, B - 1)


def mix_experts(nc, sh, name, expert_b, out, load_ahead=None):
    TOTAL = B * S * TOP_K
    with ExitStack() as ctx:
        sb = lambda n, s, d=F32: ctx.enter_context(nc.sbuf_tensor(f"{name}_{n}", s, d))
        sem = lambda n: sh.semaphore(f"{name}_{n}")
        beats = sb("beats", [P, B * TT, NE, NE])
        rank, chosen = sb("rank", [P, B * TT, NE]), sb("chosen", [P, B * TT, NE])
        won, ones = sb("won", [P, NE]), sb("ones", [P, P])
        share = sb("share", [P, NE])
        bias_raw, bias = sb("bias_raw", [P, KT, NE]), sb("bias_e", [P, KT, NE])
        relu = [sb(f"relu{m}", [P, S]) for m in range(KT)]
        wp = [sb(f"w{i}", [P, KT, NE, D], F32R) for i in range(2)]
        acc = [[sb(f"acc{p}{m}", [P, S]) for m in range(KT)] for p in range(2)]
        s_bias, s_ones, s_beats, s_rank = sem("bias"), sem("ones"), sem("beats"), sem("rank")
        s_chosen, s_won, s_count = sem("chosen"), sem("won"), sem("count")
        s_share, s_scaled, s_whi, s_wlo = sem("share"), sem("scaled"), sem("whi"), sem("wlo")
        s_relu = sem("relu")
        s_made, s_acc, s_back, s_added, s_stored = sem("made"), sem("acc"), sem("back"), sem("added"), sem("stored")
        unit_bank, back_bank = sh.psum[0:4], sh.psum[4:6]
        UN = NE * KT
        SUMS = UN - KT
        ln = None if out is not None else LayerNorm(nc, ctx, sh, f"{name}_ln", sh.psum[6:8], sh.xt_part(0), sh.xt_part(1))

        with nc.Block() as block:
            @block.sync
            def _(sp):
                sp.dma_start(bias_raw[:, :, :], expert_b).then_inc(s_bias, 16)
                if load_ahead is not None:
                    load_ahead(sp)
                sp.wait_ge(s_bias, 16)
                if out is not None:
                    def store(b):
                        sp.wait_ge(s_added, KT * (b + 1))
                        sp.dma_start(out[b].rearrange("(j p) d -> p j d", p=P),
                                     sh.x[:, bass.ds(TT * b, TT), :]).then_inc(s_stored, 16)

                    def step(b, p, half, first, last):
                        if not first:
                            store(b - 1)
                    each_batch(sp, step)
                    store(B - 1)
                    sp.wait_ge(s_stored, 16 * B)

            @block.gpsimd
            def _(pool):
                pool.memset(ones[:, :], 1.0).then_inc(s_ones, 1)
                pool.memset(beats[:, :, :, :].rearrange("p t e j -> p t (e j)")[:, :, ::NE + 1], 0.0).then_inc(s_ones, 1)
                for e in range(NE):
                    pool.wait_ge(s_whi, e + 1)
                    pool.tensor_tensor(wp[1][:, :, e, :], sh.experts[:, :, e, :], wp[0][:, :, e, :].bitcast(F32),
                                       ALU.subtract).then_inc(s_wlo, 1)
                if ln is not None:
                    def step(b, p, half, first, last):
                        if not first:
                            ln.deviation(pool, b - 1)
                    each_batch(pool, step, head=2)
                    ln.deviation(pool, B - 1)

            @block.scalar
            def _(act):
                act.wait_ge(sh.s_experts, 16)
                for e in range(NE):
                    act.copy(wp[0][:, :, e, :], sh.experts[:, :, e, :]).then_inc(s_whi, 1)
                act.wait_ge(s_scaled, 1)

                def step(b, p, half, first, last):
                    for e in range(NE):
                        for m in range(KT):
                            act.wait_ge(s_made, UN * b + KT * e + m + 1)
                            if e > 1 or (e == 1 and not first):
                                act.wait_ge(s_acc, SUMS * b + KT * (e - 2) + m + 1)
                            act.activation((acc[p][m] if e == 0 else relu[m])[:, :], unit_bank[(KT * e + m) % 4][:, :],
                                           ACT.Relu, scale=share[:, e:e + 1], bias=bias[:, m, e:e + 1]).then_inc(s_relu, 1)
                        if ln is not None and e == 6 and not first:
                            ln.take_hi(act, b - 1, 0)
                each_batch(act, step, head=2)
                if ln is not None:
                    ln.take_hi(act, B - 1, 0)

            @block.vector
            def _(dve):
                dve.wait_ge(s_ones, 2)
                g = sh.gates
                for e in range(NE):
                    for lo, hi, op in ((0, e, ALU.is_ge), (e + 1, NE, ALU.is_gt)):
                        if lo < hi:
                            ins = dve.tensor_tensor(beats[:, :, e, lo:hi], g[:, :, lo:hi],
                                                    g[:, :, e:e + 1].broadcast_to([P, B * TT, hi - lo]), op)
                            ins.then_inc(s_beats, 1)
                dve.wait_ge(s_beats, 2 * NE - 2)
                dve.tensor_reduce(rank[:, :, :], beats[:, :, :, :], AX.X, ALU.add).then_inc(s_rank, 1)
                dve.wait_ge(s_rank, 1)
                dve.tensor_scalar(chosen[:, :, :], rank[:, :, :], TOP_K - 0.5, None, ALU.is_lt).then_inc(s_chosen, 1)
                dve.wait_ge(s_chosen, 1)
                dve.tensor_reduce(won[:, :], chosen[:, :, :].rearrange("p t e -> p e t"), AX.X, ALU.add).then_inc(s_won, 1)
                dve.wait_ge(s_count, 1)
                dve.tensor_scalar(share[:, :], back_bank[0][:, 0:NE], 1.0 / TOTAL, None, ALU.mult).then_inc(s_share, 1)
                dve.wait_ge(s_share, 1)

                dve.wait_ge(s_bias, 16)
                dve.tensor_tensor(bias[:, :, :], bias_raw[:, :, :],
                                  share[:, :].unsqueeze(1).broadcast_to([P, KT, NE]), ALU.mult).then_inc(s_scaled, 1)

                def add_expert(b, p, e):
                    for m in range(KT):
                        dve.wait_ge(s_relu, UN * b + KT * e + m + 1)
                        if e > 1:
                            dve.wait_ge(s_acc, SUMS * b + KT * (e - 2) + m + 1)
                        dve.tensor_tensor(acc[p][m][:, :], acc[p][m][:, :], relu[m][:, :], ALU.add).then_inc(s_acc, 1)

                def add_residual(b):
                    for m in range(KT):
                        dve.wait_ge(s_back, KT * b + m + 1)
                        tokens = sh.x[:, bass.ds(TT * b, TT), m * P:(m + 1) * P]
                        dve.tensor_tensor(tokens, back_bank[m][:, :].rearrange("p (t d) -> p t d", d=P), tokens,
                                          ALU.add).then_inc(s_added, 1)

                def step(b, p, half, first, last):
                    for e in range(NE):
                        if e > 0:
                            add_expert(b, p, e)
                        if not first:
                            if e == 1:
                                add_residual(b - 1)
                            if ln is not None and e == 2:
                                ln.moments(dve, b - 1, (s_added, KT * b))
                            if ln is not None and e == 4:
                                ln.normalise(dve, b - 1)
                            if ln is not None and e == 7:
                                ln.take_lo(dve, b - 1, 0)
                each_batch(dve, step, head=2)
                add_residual(B - 1)
                if ln is not None:
                    ln.moments(dve, B - 1, (s_added, KT * B))
                    ln.normalise(dve, B - 1)
                    ln.take_lo(dve, B - 1, 0)

            @block.tensor
            def _(pe):
                def turn_back(b, p):
                    for m in range(KT):
                        pe.wait_ge(s_acc, SUMS * (b + 1) - 1 + m)
                        if not is_first(b):
                            pe.wait_ge(s_added, KT * b - 1 + m)
                        for j in range(TT):
                            mm = pe.transpose(back_bank[m][:, j * P:(j + 1) * P], acc[p][m][:, j * P:(j + 1) * P],
                                              sh.ident[:, :])
                        mm.then_inc(s_back, 1)

                def step(b, p, half, first, last):
                    for e in range(NE):
                        if first:
                            pe.wait_ge(s_wlo, e + 1)
                        for m in range(KT):
                            u = KT * e + m
                            if first and u == 3:
                                pe.wait_ge(s_ones, 1)
                                pe.wait_ge(s_won, 1)
                                pe.matmul(back_bank[0][:, 0:NE], ones[:, :], won[:, :], start=True, stop=True).then_inc(s_count, 1)
                            if not (first and u < 4):
                                pe.wait_ge(s_relu, UN * b + u - 3)
                            for i, (wi, xi) in enumerate(PASSES):
                                for k in range(KT):
                                    mm = pe.matmul(unit_bank[u % 4][:, :], wp[wi][:, k, e, m * P:(m + 1) * P],
                                                   sh.xt[:, xi, k, bass.ds(S * b, S)], start=(i == 0 and k == 0),
                                                   stop=(i == 2 and k == KT - 1))
                            mm.then_inc(s_made, 1)
                        if not first:
                            if e == 0:
                                turn_back(b - 1, 1 - p)
                            if ln is not None and e == 6:
                                ln.turn(pe, b - 1)
                each_batch(pe, step, head=2)
                turn_back(B - 1, (B - 1) % 2)
                if ln is not None:
                    ln.turn(pe, B - 1)


def distance_weights(spare):
    return spare[:, 0:KT * 4 * D].rearrange("p (k n) -> p k n", k=KT)


def distance_attention(nc, sh, bias, bias_o, spare):
    VC = D + 2
    UN = 8
    QK = 2 * KT
    with ExitStack() as ctx:
        sb = lambda n, s, d=F32: ctx.enter_context(nc.sbuf_tensor(f"dist_{n}", s, d))
        sem = lambda n: sh.semaphore(f"dist_{n}")
        raw = distance_weights(spare)
        free = [0]

        def take(columns):
            free[0] += columns
            return spare[:, free[0] - columns:free[0]]

        vw = [take(TT * VC).rearrange("p (t n) -> p t n", t=TT) for _ in range(2)]
        probs = take(TT * S).rearrange("p (t s) -> p t s", t=TT)
        squares = take(2 * KT * S)
        square = [squares[:, S * u:S * (u + 1)] for u in range(2 * KT)]
        q_norm = take(S)
        bias_row = take(D)
        bv_rows = probs[:, 0, 0:KT * P].rearrange("p (k m) -> p k m", k=KT)
        wp = [sb(f"w{i}", [P, KT, 4 * D], F32R) for i in range(2)]
        FOLDED = slice(2 * D, 3 * D)
        bias_sb, ones = sb("bias", [P, 3 * KT]), sb("ones", [P, P])
        qk = [[[sb(f"qk{p}{i}{u}", [P, S], F32R) for u in range(2 * KT)] for i in range(2)] for p in range(2)]
        xs = [[sb(f"x{i}{k}", [P, S], F32R) for k in range(KT)] for i in range(2)]
        k_norm = [sb(f"k_norm{p}", [P, TT]) for p in range(2)]
        recip = sb("recip", [P, TT])
        unit_bank, score_bank = sh.psum[0:4], sh.psum[4:6]
        fold_bank = sh.psum[6:8]
        out_bank = unit_bank[2:4]
        s_const, s_ones, s_whi, s_wlo = sem("const"), sem("ones"), sem("whi"), sem("wlo")
        s_made, s_hi, s_square, s_lo = sem("made"), sem("hi"), sem("square"), sem("lo")
        s_q_norm, s_k_norm, s_summed = sem("q_norm"), sem("k_norm"), sem("summed")
        s_bv, s_folded, s_fold_hi, s_fold_lo = sem("bv"), sem("folded"), sem("fold_hi"), sem("fold_lo")
        s_bias_made, s_bias_row, s_xs = sem("bias_made"), sem("bias_row"), sem("xs")
        s_vw, s_score, s_exponent, s_kernel, s_probs = sem("vw"), sem("score"), sem("exponent"), sem("kernel"), sem("probs")
        s_out, s_recip, s_biased, s_added = sem("out"), sem("recip"), sem("biased"), sem("added")
        ln = LayerNorm(nc, ctx, sh, "dist_ln", sh.psum[6:8], sh.xt_part(0), sh.xt_part(1),
                       take(TT * D).rearrange("p (t d) -> p t d", t=TT))
        gate = Gate(nc, ctx, sh, "dist_gate", score_bank)

        with nc.Block() as block:
            @block.sync
            def _(sp):
                sp.dma_start(bias_sb[:, :], bias).then_inc(s_const, 16)
                sp.dma_start(bias_row[:, :], bias_o.unsqueeze(0).broadcast_to([P, D])).then_inc(s_const, 16)

            @block.gpsimd
            def _(pool):
                pool.memset(ones[:, :], 1.0).then_inc(s_ones, 1)
                def sum_squares(b):
                    for n in range(2):
                        pool.wait_ge(s_square, KT * (2 * b + n + 1))
                        pool.tensor_tensor(square[KT * n], square[KT * n], square[KT * n + 1],
                                           ALU.add).then_inc(s_summed, 1)

                sum_squares(0)
                pool.wait_ge(s_wlo, 4)
                pool.wait_ge(s_bias_made, 1)
                for p in range(2):
                    pool.memset(vw[p][:, :, D:VC], 1.0).then_inc(s_ones, 1)
                pool.wait_ge(s_bias_row, 1)

                def add_bias(b):
                    row = bias_row[:, :].unsqueeze(1).broadcast_to([P, TT, D])
                    tokens = sh.x[:, bass.ds(TT * b, TT), :]
                    pool.tensor_tensor(tokens, tokens, row, ALU.add).then_inc(s_biased, 1)

                def step(b, p, half, first, last):
                    if not first:
                        ln.deviation(pool, b - 1)
                    if not last:
                        add_bias(b + 1)
                        sum_squares(b + 1)
                add_bias(0)
                each_batch(pool, step, head=2)
                ln.deviation(pool, B - 1)

            @block.scalar
            def _(act):
                for c in range(4):
                    split_weights(act, None, raw[:, :, c * D:(c + 1) * D], wp[0][:, :, c * D:(c + 1) * D], None,
                                  sh.s_dist_w, 16, s_whi, None, 0)
                act.wait_ge(s_const, 32)

                def project(b, p):
                    for u in range(QK):
                        act.wait_ge(s_made, UN * b + u + 1)
                        act.activation(qk[p][0][u][:, :], unit_bank[u][:, :], ACT.Identity,
                                       bias=bias_sb[:, u:u + 1]).then_inc(s_hi, 1)
                        act.activation(square[u][:, :], unit_bank[u][:, :], ACT.Square,
                                       bias=bias_sb[:, u:u + 1]).then_inc(s_square, 1)

                project(0, 0)
                act.wait_ge(s_folded, KT)
                for k in range(KT):
                    act.copy(wp[0][:, k, FOLDED], fold_bank[k][:, 0:D]).then_inc(s_fold_hi, 1)

                def step(b, p, half, first, last):
                    act.wait_ge(s_k_norm, b + 1)
                    for t in range(TT):
                        act.wait_ge(s_exponent, TT * b + t + 1)
                        act.activation(probs[:, t, :], probs[:, t, :], ACT.Exp,
                                       bias=k_norm[p][:, t:t + 1]).then_inc(s_kernel, 1)
                        act.wait_ge(s_kernel, TT * b + t + 1)
                        act.activation(probs[:, t, :], probs[:, t, :], ACT.Exp).then_inc(s_probs, 1)
                    if not last:
                        project(b + 1, 1 - p)
                    if not first:
                        ln.take_hi(act, b - 1, 0)
                    if not first:
                        gate.take_rows(act, b - 1)
                each_batch(act, step, head=2)
                ln.take_hi(act, B - 1, 0)
                gate.take_rows(act, B - 1)

            @block.vector
            def _(dve):
                for c in range(4):
                    cut = slice(c * D, (c + 1) * D)
                    split_weights(None, dve, raw[:, :, cut], wp[0][:, :, cut], wp[1][:, :, cut],
                                  sh.s_dist_w, 16, s_whi, s_wlo, c + 1)
                dve.wait_ge(s_const, 32)
                dve.wait_ge(s_ones, 1)
                for k in range(KT):
                    dve.tensor_scalar(bv_rows[:, k, :], ones[:, :], bias_sb[:, QK + k:QK + k + 1], None, ALU.mult).then_inc(s_bv, 1)

                def finish_fold():
                    for k in range(KT):
                        dve.wait_ge(s_fold_hi, k + 1)
                        dve.tensor_tensor(wp[1][:, k, FOLDED], fold_bank[k][:, 0:D], wp[0][:, k, FOLDED].bitcast(F32),
                                          ALU.subtract).then_inc(s_fold_lo, 1)
                    dve.wait_ge(s_bias_made, 1)
                    dve.tensor_tensor(bias_row[:, :], bias_row[:, :], score_bank[0][:, 0:D], ALU.add).then_inc(s_bias_row, 1)

                def copy_x(b):
                    if not is_first(b):
                        dve.wait_ge(s_made, UN * (b - 1) + 6)
                    for i in range(2):
                        for k in range(KT):
                            dve.tensor_copy(xs[i][k][:, :], sh.xt[:, i, k, bass.ds(S * b, S)]).then_inc(s_xs, 1)

                def project(b, p):
                    for u in range(QK):
                        dve.wait_ge(s_hi, QK * b + u + 1)
                        dve.wait_ge(s_square, QK * b + u + 1)
                        dve.scalar_tensor_tensor(out=qk[p][1][u][:, :], in0=unit_bank[u][:, :], scalar=bias_sb[:, u:u + 1],
                                                 in1=qk[p][0][u][:, :].bitcast(F32), op0=ALU.add,
                                                 op1=ALU.subtract).then_inc(s_lo, 1)
                    if is_first(b):
                        finish_fold()
                    elif not is_first(b - 1):
                        ln.take_lo(dve, b - 2, 0)
                    for i in range(2):
                        dve.wait_ge(s_made, UN * b + 5 + i)
                        dve.tensor_copy(vw[p][:, 2 * i:2 * i + 2, 0:D],
                                        unit_bank[i][:, :].rearrange("p (t d) -> p t d", d=D)).then_inc(s_vw, 1)
                    dve.wait_ge(s_made, UN * b + 7)
                    dve.tensor_scalar(k_norm[p][:, :], unit_bank[2][:, 0:2 * TT:2], -1.0, None,
                                      ALU.mult).then_inc(s_k_norm, 1)
                    dve.wait_ge(s_made, UN * b + 8)
                    dve.tensor_copy(q_norm[:, :], unit_bank[3][:, :]).then_inc(s_q_norm, 1)

                copy_x(0)
                project(0, 0)

                def step(b, p, half, first, last):
                    dve.wait_ge(s_q_norm, b + 1)
                    for t in range(TT):
                        if t == 2 and not first:
                            ln.normalise(dve, b - 1)
                        dve.wait_ge(s_score, TT * b + t + 1)
                        dve.scalar_tensor_tensor(out=probs[:, t, :], in0=score_bank[t % 2][:, :], scalar=2.0,
                                                 in1=q_norm[:, :], op0=ALU.mult,
                                                 op1=ALU.subtract).then_inc(s_exponent, 1)
                    if not last:
                        copy_x(b + 1)
                    if not last:
                        project(b + 1, 1 - p)
                    else:
                        ln.take_lo(dve, b - 1, 0)
                    dve.wait_ge(s_biased, b + 1)
                    for j in range(TT):
                        dve.wait_ge(s_out, TT * b + j + 1)
                        dve.reciprocal(recip[:, j:j + 1], out_bank[j % 2][:, D:D + 1]).then_inc(s_recip, 1)
                        dve.wait_ge(s_recip, TT * b + j + 1)
                        dve.scalar_tensor_tensor(out=sh.x[:, TT * b + j, :], in0=out_bank[j % 2][:, 0:D],
                                                 scalar=recip[:, j:j + 1], in1=sh.x[:, TT * b + j, :],
                                                 op0=ALU.mult, op1=ALU.add).then_inc(s_added, 1)
                        if j == 2 and not first:
                            gate.keep(dve, b - 1)
                        if j > 0:
                            wait_apart(dve, s_added, TT * b + j)
                            ln.add_up(dve, b, j - 1)
                    wait_apart(dve, s_added, TT * b + TT)
                    ln.add_up(dve, b, TT - 1)
                    ln.take_moments(dve, b)
                each_batch(dve, step, head=2)
                ln.normalise(dve, B - 1)
                ln.take_lo(dve, B - 1, 0)
                gate.keep(dve, B - 1)

            @block.tensor
            def _(pe):
                def three_pass(out, weight, moving):
                    for i, (wi, xi) in enumerate(PASSES):
                        for k in range(KT):
                            mm = pe.matmul(out, weight(wi, k), moving(xi, k), start=(i == 0 and k == 0),
                                           stop=(i == 2 and k == KT - 1))
                    return mm

                def fold():
                    pe.wait_ge(s_wlo, 4)
                    for n in range(KT):
                        three_pass(fold_bank[n][:, 0:D], lambda i, k: wp[i][:, k, 2 * D + n * P:2 * D + (n + 1) * P],
                                   lambda i, k: wp[i][:, k, 3 * D:4 * D]).then_inc(s_folded, 1)
                    pe.wait_ge(s_bv, KT)
                    for k in range(KT):
                        mm = pe.matmul(score_bank[0][:, 0:D], bv_rows[:, k, :], raw[:, k, 3 * D:4 * D],
                                       start=(k == 0), stop=(k == KT - 1))
                    mm.then_inc(s_bias_made, 1)
                    pe.wait_ge(s_fold_lo, KT)

                def project(b, p):
                    for u in range(QK):
                        if is_first(b) and u % KT == 0:
                            pe.wait_ge(s_wlo, u // KT + 1)
                        if not is_first(b) and u < 2:
                            pe.wait_ge(s_vw, 2 * b - 1 + u)
                        if not is_early(b) and u >= 2:
                            pe.wait_ge(s_added, TT * (b - 1) - 3 + u)
                        three_pass(unit_bank[u][:, :], lambda i, k: wp[i][:, k, u * P:(u + 1) * P],
                                   lambda i, k: sh.xt[:, i, k, bass.ds(S * b, S)]).then_inc(s_made, 1)
                    if is_first(b):
                        fold()
                    elif not is_first(b - 1):
                        ln.turn(pe, b - 2)
                    pe.wait_ge(s_xs, 2 * KT * (b + 1))
                    for j in range(TT):
                        if j % 2 == 0:
                            pe.wait_ge(s_lo, QK * b + 1 + j // 2)
                        mm = three_pass(unit_bank[j // 2][:, (j % 2) * D:(j % 2 + 1) * D],
                                        lambda i, k: xs[i][k][:, j * P:(j + 1) * P], lambda i, k: wp[i][:, k, FOLDED])
                        if j % 2:
                            mm.then_inc(s_made, 1)
                    pe.wait_ge(s_lo, QK * (b + 1))
                    if is_first(b):
                        pe.wait_ge(s_ones, 1)
                    pe.wait_ge(s_summed, 2 * b + 2)
                    for t in range(TT):
                        mm = pe.matmul(unit_bank[2][:, 2 * t:2 * t + 2], square[KT][:, t * P:(t + 1) * P],
                                       ones[:, 0:2], start=True, stop=True)
                    mm.then_inc(s_made, 1)
                    pe.matmul(unit_bank[3][:, :], ones[:, :], square[0][:, :], start=True, stop=True).then_inc(s_made, 1)

                project(0, 0)

                def step(b, p, half, first, last):
                    pe.wait_ge(s_lo, QK * (b + 1))
                    if first:
                        pe.wait_ge(s_bias_row, 1)
                    if not is_early(b):
                        pe.wait_ge(gate.s_rows, b - 1)
                        pe.wait_ge(gate.s_kept, b - 1)
                    for t in range(TT):
                        if not (first and t < 2):
                            pe.wait_ge(s_exponent, TT * b + t - 1)
                        three_pass(score_bank[t % 2][:, :], lambda i, k: qk[p][i][KT + k][:, t * P:(t + 1) * P],
                                   lambda i, k: qk[p][i][k][:, :]).then_inc(s_score, 1)
                    if not last:
                        project(b + 1, 1 - p)
                    else:
                        ln.turn(pe, b - 1)
                    if not first:
                        pe.wait_ge(ln.s_lo, KT * b)
                        pe.wait_ge(s_exponent, TT * b + TT)
                        gate.multiply(pe, b - 1)
                    pe.wait_ge(s_probs, TT * b + TT)
                    pe.wait_ge(s_ones, 3)
                    pe.wait_ge(s_vw, 2 * b + 2)
                    pe.wait_ge(s_q_norm, b + 1 if last else b + 2)
                    for j in range(TT):
                        if j == 2 and not first:
                            gate.turn(pe, b - 1)
                        if not (first and j < 2):
                            pe.wait_ge(s_added, TT * b + j - 1)
                        for t in range(TT):
                            mm = pe.matmul(out_bank[j % 2][:, 0:VC], probs[:, t, j * P:(j + 1) * P], vw[p][:, t, :],
                                           start=(t == 0), stop=(t == TT - 1))
                        mm.then_inc(s_out, 1)
                each_batch(pe, step, head=2)
                ln.turn(pe, B - 1)
                pe.wait_ge(ln.s_lo, KT * B)
                gate.multiply(pe, B - 1)
                gate.turn(pe, B - 1)


def hybrid_layer(nc, x, w_qkv, b_qk, b_v, conv_w, conv_b, out_w, out_b, dist_w, dist_b, dist_bo, gate_w, gate_b,
                 expert_w, expert_b, out):
    with ExitStack() as ctx:
        sh = Shared(nc, ctx)
        context = ctx.enter_context(nc.sbuf_tensor("context", [P, GROUPS, TT, GR], F32))
        with ExitStack() as attention_ctx:
            buffers = HeadBuffers(nc, attention_ctx)
            heads = HeadLoads(sh, "attn1", buffers, sh.q_parts, sh.k_parts)
            project_qkv(nc, sh, x, w_qkv, b_qk, b_v, heads, conv_w, out_w, gate_w)
            attention(nc, sh, "attn1", heads, sh.v_ones, context)
            heads = HeadLoads(sh, "attn2", buffers, sh.q2_parts, sh.k_parts)
            convolve(nc, sh, context, buffers.conv_w, conv_b, heads)
            attention(nc, sh, "attn2", heads, sh.v_ones, context)
        sh.after_attention(ctx)
        project_out(nc, sh, context, out_b, gate_b, expert_w)
        spare = context[:, :, :, :].rearrange("p g t c -> p (g t c)")
        mix_experts(nc, sh, "ffn1", expert_b, None, lambda sp: sp.dma_start(
            distance_weights(spare), dist_w.rearrange("(k p) n -> p k n", p=P)).then_inc(sh.s_dist_w, 16))
        sh.recycle_semaphores()
        distance_attention(nc, sh, dist_b, dist_bo, spare)
        mix_experts(nc, sh, "ffn2", expert_b, out)


def laid_out(i):
    import numpy as np

    def channels(a):
        return np.ascontiguousarray(a.reshape(NG, GH, HD, -1).transpose(0, 2, 1, 3)).reshape(a.shape)

    def by_partition(a):
        return np.ascontiguousarray(a.reshape(-1, P).T)

    w, b = i["L0_attn_a_Wqkv_w"], i["L0_attn_a_Wqkv_b"]
    return {
        "x": i["L0_attn_a_x"],
        "w_qkv": np.ascontiguousarray(np.concatenate([channels(w[:D]), channels(w[D:2 * D]), w[2 * D:]]).T),
        "b_qk": by_partition(np.concatenate([channels(b[:D]), channels(b[D:2 * D])])),
        "b_v": b[2 * D:],
        "conv_w": np.ascontiguousarray(channels(i["L0_attn_a_conv_w"]).transpose(1, 2, 0)).reshape(D, 3 * D),
        "conv_b": by_partition(channels(i["L0_attn_a_conv_b"])),
        "out_w": i["L0_attn_a_out_w"].T,
        "out_b": i["L0_attn_a_out_b"],
        "dist_w": np.concatenate([i["L0_attn_b_W" + n].T if n == "v" else i["L0_attn_b_W" + n] for n in "qkvo"], axis=1),
        "dist_b": by_partition(np.concatenate([i["L0_attn_b_b" + n] for n in "qkv"])),
        "dist_bo": i["L0_attn_b_bo"],
        "gate_w": i["L0_ffn_gate_w"].T,
        "gate_b": i["L0_ffn_gate_b"].reshape(NE, 1),
        "expert_w": i["L0_ffn_expert_w"].transpose(2, 0, 1),
        "expert_b": np.ascontiguousarray(i["L0_ffn_expert_b"].reshape(NE, KT, P).transpose(2, 1, 0)),
    }


def kernel(**inputs):
    import numpy as np
    import concourse.bacc as bacc
    from concourse.bass_utils import run_bass_kernel_spmd

    nc = bacc.Bacc("TRN2", target_bir_lowering=False, num_devices=1)
    arrays, args = {}, []
    for name, a in laid_out({n: np.asarray(a) for n, a in inputs.items()}).items():
        arrays[name] = np.ascontiguousarray(a)
        args.append(nc.dram_tensor(name, a.shape, F32, kind="ExternalInput").ap())
    out = nc.dram_tensor("out", (B, S, D), F32, kind="ExternalOutput").ap()
    hybrid_layer(nc, *args, out)
    return run_bass_kernel_spmd(nc, [arrays], core_ids=[0]).results[0]["out"]
```
